# Optimizing a Trainium2 kernel written in Bass

```python
import numpy as np
import jax
import jax.numpy as jnp

def _softmax(x, axis=-1):
    return jax.nn.softmax(x, axis=axis)

def _gelu(x):
    return jax.nn.gelu(x, approximate=True)

def _silu(x):
    return jax.nn.silu(x)

def _sigmoid(x):
    return jax.nn.sigmoid(x)

def _layernorm(x, axis=-1, eps=1e-05):
    m = jnp.mean(x, axis=axis, keepdims=True)
    v = jnp.var(x, axis=axis, keepdims=True)
    return (x - m) / jnp.sqrt(v + eps)

def _scatter_add(tgt, idx, src, axis=0):
    return tgt.at[idx].add(src)

def _segment_sum(src, seg, n):
    return jax.ops.segment_sum(src, seg, n)
kernel_name = 'mk_gnn_ffn_d1_gnn_r8_18bf41'

def setup_inputs(seed: int=0):
    np.random.seed(seed)
    _w = jnp.asarray

    def _rec_inputs():
        import jax
        import jax.numpy as jnp
        _gk = jax.random.key(seed)
        x = -0.0003713 + 1 * jax.random.normal(jax.random.fold_in(_gk, 1), (6250, 256), jnp.float32)
        src = jax.random.randint(jax.random.fold_in(_gk, 2), (200000,), 0, 6250, jnp.int32)
        dst = jax.random.randint(jax.random.fold_in(_gk, 3), (200000,), 0, 6250, jnp.int32)
        _o = jnp.argsort(dst, stable=True)
        src = src[_o]
        dst = dst[_o]
        edge_type_64 = jax.random.randint(jax.random.fold_in(_gk, 12), (200000,), 0, 64, jnp.int32)
        return (x, src, dst, edge_type_64)
    x, src, dst, edge_type_64 = _rec_inputs()

    def _L0_gnn_setup():
        import jax, jax.numpy as jnp
        import numpy as np
        N_NODES = 6250
        N_EDGES = 62500
        IN_DIM = 256
        HID = 64
        HEADS = 4
        N_REL = 64
        key = jax.random.key(seed)
        ks = jax.random.split(key, 16)
        s = 0.02
        return {'node_features': jax.random.normal(ks[0], (N_NODES, IN_DIM), jnp.float32), 'edge_index': jax.random.randint(ks[1], (2, N_EDGES), 0, N_NODES, jnp.int32), 'edge_relations': jax.random.randint(ks[2], (N_EDGES,), 0, N_REL, jnp.int32), 'query_emb': jax.random.normal(ks[3], (IN_DIM,), jnp.float32), 'Wq': jax.random.normal(ks[4], (IN_DIM, HID * HEADS), jnp.float32) * s, 'bq': jnp.zeros((HID * HEADS,), jnp.float32), 'Wk': jax.random.normal(ks[5], (IN_DIM, HID * HEADS), jnp.float32) * s, 'bk': jnp.zeros((HID * HEADS,), jnp.float32), 'Wv': jax.random.normal(ks[6], (IN_DIM, HID * HEADS), jnp.float32) * s, 'bv': jnp.zeros((HID * HEADS,), jnp.float32), 'rel_w': jax.random.normal(ks[7], (N_REL, HID), jnp.float32) * s, 'Wo': jax.random.normal(ks[8], (HID * HEADS, IN_DIM), jnp.float32) * s, 'bo': jnp.zeros((IN_DIM,), jnp.float32), 'gamma': jnp.ones((IN_DIM,), jnp.float32), 'beta': jnp.zeros((IN_DIM,), jnp.float32)}
    _L0_gnn_all = _L0_gnn_setup()
    _L0_gnn_in = {k: v for k, v in _L0_gnn_all.items() if k in ('query_emb', 'Wq', 'bq', 'Wk', 'bk', 'Wv', 'bv', 'rel_w', 'Wo', 'bo', 'gamma', 'beta')}
    del _L0_gnn_all

    def _L0_ffn_setup():
        import jax, jax.numpy as jnp
        import numpy as np
        TOP_K = 2
        LN_EPS = 1e-05
        key = jax.random.key(seed)
        ks = jax.random.split(key, 8)
        B, S, D, E, H = (16, 1024, 256, 8, 1024)
        x = jax.random.normal(ks[0], (B, S, D), dtype=jnp.float32)
        Wr = jax.random.normal(ks[1], (D, E), dtype=jnp.float32) * 0.1
        br = jnp.zeros((E,), dtype=jnp.float32)
        ln_g = jnp.ones((E, D), dtype=jnp.float32)
        ln_b = jnp.zeros((E, D), dtype=jnp.float32)
        W1 = jax.random.normal(ks[2], (E, D, H), dtype=jnp.float32) * (1.0 / np.sqrt(D))
        b1 = jnp.zeros((E, H), dtype=jnp.float32)
        W2 = jax.random.normal(ks[3], (E, H, D), dtype=jnp.float32) * (1.0 / np.sqrt(H))
        b2 = jnp.zeros((E, D), dtype=jnp.float32)
        return {'x': x, 'Wr': Wr, 'br': br, 'ln_g': ln_g, 'ln_b': ln_b, 'W1': W1, 'b1': b1, 'W2': W2, 'b2': b2}
    _L0_ffn_all = _L0_ffn_setup()
    _L0_ffn_in = {k: v for k, v in _L0_ffn_all.items() if k in ('Wr', 'br', 'ln_g', 'ln_b', 'W1', 'b1', 'W2', 'b2')}
    del _L0_ffn_all
    return {'x': x, 'src': src, 'dst': dst, 'edge_type_64': edge_type_64, 'L0_gnn_query_emb': _L0_gnn_in['query_emb'], 'L0_gnn_Wq': _L0_gnn_in['Wq'], 'L0_gnn_bq': _L0_gnn_in['bq'], 'L0_gnn_Wk': _L0_gnn_in['Wk'], 'L0_gnn_bk': _L0_gnn_in['bk'], 'L0_gnn_Wv': _L0_gnn_in['Wv'], 'L0_gnn_bv': _L0_gnn_in['bv'], 'L0_gnn_rel_w': _L0_gnn_in['rel_w'], 'L0_gnn_Wo': _L0_gnn_in['Wo'], 'L0_gnn_bo': _L0_gnn_in['bo'], 'L0_gnn_gamma': _L0_gnn_in['gamma'], 'L0_gnn_beta': _L0_gnn_in['beta'], 'L0_ffn_Wr': _L0_ffn_in['Wr'], 'L0_ffn_br': _L0_ffn_in['br'], 'L0_ffn_ln_g': _L0_ffn_in['ln_g'], 'L0_ffn_ln_b': _L0_ffn_in['ln_b'], 'L0_ffn_W1': _L0_ffn_in['W1'], 'L0_ffn_b1': _L0_ffn_in['b1'], 'L0_ffn_W2': _L0_ffn_in['W2'], 'L0_ffn_b2': _L0_ffn_in['b2']}

def reference(x, src, dst, edge_type_64, L0_gnn_query_emb, L0_gnn_Wq, L0_gnn_bq, L0_gnn_Wk, L0_gnn_bk, L0_gnn_Wv, L0_gnn_bv, L0_gnn_rel_w, L0_gnn_Wo, L0_gnn_bo, L0_gnn_gamma, L0_gnn_beta, L0_ffn_Wr, L0_ffn_br, L0_ffn_ln_g, L0_ffn_ln_b, L0_ffn_W1, L0_ffn_b1, L0_ffn_W2, L0_ffn_b2):
    import jax
    import jax.numpy as jnp

    def _L0_gnn_ref(node_features, edge_index, edge_relations, query_emb, Wq, bq, Wk, bk, Wv, bv, rel_w, Wo, bo, gamma, beta):
        import jax, jax.numpy as jnp
        import numpy as np
        N_NODES = 6250
        N_EDGES = 62500
        IN_DIM = 256
        HID = 64
        HEADS = 4
        N_REL = 64
        N = node_features.shape[0]
        D = rel_w.shape[1]
        H = Wq.shape[1] // D
        enh = node_features + 0.1 * query_emb[None, :]
        Q = (enh @ Wq + bq).reshape(N, H, D)
        K = (enh @ Wk + bk).reshape(N, H, D)
        V = (enh @ Wv + bv).reshape(N, H, D)
        src, dst = (edge_index[0], edge_index[1])
        rel = rel_w[edge_relations]
        mod_k = K[src] + 0.2 * rel[:, None, :]
        scores = jnp.einsum('ehd,ehd->eh', Q[dst], mod_k) / D ** 0.5
        seg_max = jax.ops.segment_max(scores, dst, num_segments=N)
        ex = jnp.exp(scores - seg_max[dst])
        denom = jax.ops.segment_sum(ex, dst, num_segments=N)
        w = ex / denom[dst]
        agg = jax.ops.segment_sum(w[:, :, None] * V[src], dst, num_segments=N)
        deg = jax.ops.segment_sum(jnp.ones((src.shape[0],), jnp.float32), dst, num_segments=N)
        msgs = jnp.where(deg[:, None, None] > 0, agg, V)
        out = msgs.reshape(N, H * D) @ Wo + bo
        x = out + node_features
        mu = jnp.mean(x, axis=-1, keepdims=True)
        var = jnp.var(x, axis=-1, keepdims=True)
        return (x - mu) / jnp.sqrt(var + 1e-05) * gamma + beta

    def _L0_ffn_ref(x, Wr, br, ln_g, ln_b, W1, b1, W2, b2):
        import jax, jax.numpy as jnp
        import numpy as np
        TOP_K = 2
        LN_EPS = 1e-05
        B, S, D = x.shape
        N = B * S
        xt = x.reshape(N, D)
        logits = xt @ Wr + br
        probs = jax.nn.softmax(logits, axis=-1)
        top_p, top_idx = jax.lax.top_k(probs, TOP_K)
        weights = top_p / top_p.sum(axis=-1, keepdims=True)
        mu = xt.mean(axis=-1, keepdims=True)
        var = ((xt - mu) ** 2).mean(axis=-1, keepdims=True)
        xn = (xt - mu) * jax.lax.rsqrt(var + LN_EPS)
        xe = xn[None, :, :] * ln_g[:, None, :] + ln_b[:, None, :]
        h = jax.nn.gelu(jnp.einsum('end,edh->enh', xe, W1) + b1[:, None, :], approximate=False)
        y = jnp.einsum('enh,ehd->end', h, W2) + b2[:, None, :]
        y_tok = jnp.transpose(y, (1, 0, 2))
        sel = jnp.take_along_axis(y_tok, top_idx[:, :, None], axis=1)
        out = (weights[:, :, None] * sel).sum(axis=1)
        return out.reshape(B, S, D)
    edge_index = jnp.stack([src, dst])
    x = x + _L0_gnn_ref(_layernorm(x, axis=-1), edge_index, edge_type_64, L0_gnn_query_emb, L0_gnn_Wq, L0_gnn_bq, L0_gnn_Wk, L0_gnn_bk, L0_gnn_Wv, L0_gnn_bv, L0_gnn_rel_w, L0_gnn_Wo, L0_gnn_bo, L0_gnn_gamma, L0_gnn_beta)
    x = x + _L0_ffn_ref(_layernorm(x, axis=-1)[None], L0_ffn_Wr, L0_ffn_br, L0_ffn_ln_g, L0_ffn_ln_b, L0_ffn_W1, L0_ffn_b1, L0_ffn_W2, L0_ffn_b2)[0]
    return x

_drawn_inputs = setup_inputs


def setup_inputs(seed=0):
    import zlib

    import numpy as np

    out = dict(_drawn_inputs(seed))
    spreads = {'L0_gnn_bq': (0.0, 0.8),
     'L0_gnn_bk': (0.0, 2.0),
     'L0_gnn_bv': (0.0, 0.298),
     'L0_gnn_bo': (0.0, 0.1),
     'L0_gnn_gamma': (1.0, 0.2),
     'L0_gnn_beta': (0.0, 0.1),
     'L0_ffn_br': (0.0, 0.1),
     'L0_ffn_ln_g': (1.0, 0.2),
     'L0_ffn_ln_b': (0.0, 0.307),
     'L0_ffn_b1': (0.0, 0.302),
     'L0_ffn_b2': (0.0, 0.1)}
    factors = {'L0_gnn_query_emb': 4.971,
     'L0_gnn_Wq': 8.0,
     'L0_gnn_Wk': 8.0,
     'L0_gnn_Wv': 3.039,
     'L0_gnn_rel_w': 51.329}
    for name, (base, spread) in spreads.items():
        noise = np.random.default_rng([zlib.crc32(name.encode()), seed]).standard_normal(out[name].shape)
        drawn = base * np.exp(spread * noise) if base else spread * noise
        out[name] = jnp.asarray(drawn.astype(out[name].dtype))
    for name, factor in factors.items():
        out[name] = (out[name] * factor).astype(out[name].dtype)
    return out
```

```python
from contextlib import ExitStack

import numpy as np

import concourse.bass as bass
from concourse import mybir
from concourse.alu_op_type import AluOpType as ALU

ACT = mybir.ActivationFunctionType
AX = mybir.AxisListType
F32 = mybir.dt.float32
BF16 = mybir.dt.bfloat16
I32 = mybir.dt.int32
U32 = mybir.dt.uint32

P = 128
N, D = 6250, 256
H, HD = 4, 64
DC = D // P
E = 200000
NREL = 64
W = P // H
TG = 6
G = TG * P
NG = -(-E // G)
GH = G // 2
CW = HD + 1
KVW = D + H * CW
NT = -(-N // P)
LAST = N - P
QW = N + W + 22
AR = 50 * P
NX, FF = 8, 1024
FC = FF // P
BT = 256
CAP = N + BT + 22
NB = (2 * N - NX) // BT + NX
BPE = -(-N // BT)
EPS = 1e-5
BIG = 1e30
FLOOR = -1e28
SCALE = HD ** -0.5


class Tile:

    def __init__(self, t, slot, rnd, live, first):
        self.t, self.slot, self.rnd, self.live, self.first = t, slot, rnd, live, first


def pipeline(eng, n, lo, hi, unroll, warm, step):
    def at(s_static, r, k, base):
        def T(off):
            if r is None:
                t = s_static - off
                return Tile(t, t % unroll, t // unroll, 0 <= t < n, t)
            c = base + k - off
            return Tile(r * unroll + c, c % unroll, r + c // unroll, True, c)
        return T
    loops = (n + lo - warm) // unroll if lo < 0 else (n - warm) // unroll
    for s in range(lo, warm):
        step(at(s, None, 0, 0))
    with eng.Fori(0, loops) as r:
        for k in range(unroll):
            step(at(None, r, k, warm))
    for s in range(warm + loops * unroll, n + hi):
        step(at(s, None, 0, 0))


def hold(eng, sem, value):
    eng.wait_ge(sem, value)
    eng.nop(nofuse=True)


def lay_constants():
    p = np.arange(P)
    q = np.arange(P)
    ident = np.eye(P, dtype=np.float32)
    first = (((q % W) == 0)[None, :] & ((p // W)[:, None] == (q // W)[None, :])).astype(np.float32)
    pen = np.zeros((P, P), np.float32)
    for r in range(W + 2):
        pen[NREL + r] = np.where((q % W) == r, 0.0, -BIG)
    match = np.zeros((P, 1), np.float32)
    match[:NREL, 0] = np.arange(NREL)
    match[NREL:NREL + W + 1, 0] = np.arange(W + 1)
    match[NREL + W + 1, 0] = -1
    inwin = (p % W).astype(np.float32)[:, None]
    isfirst = ((p % W) == 0).astype(np.float32)[:, None]
    before = (p[:, None] < q[None, :]).astype(np.float32)
    parts = dict(ident=ident, first=first, pen=pen, before=before, ones=np.ones((P, P), np.float32),
                 match=match, inwin=inwin, isfirst=isfirst,
                 eps=np.full((P, 1), EPS, np.float32),
                 iota8=np.tile(np.arange(NX, dtype=np.float32), (P, 1)),
                 cap8=np.tile(np.arange(NX, dtype=np.float32) * CAP, (P, 1)),
                 lastrows=(p >= P - (N - (NT - 1) * P)).astype(np.float32)[:, None],
                 fills=np.tile(np.arange(BPE, dtype=np.float32) * BT, (P, 1)),
                 nospare=np.zeros((P, 2), np.float32),
                 spare=np.where((p < P - (N - (NT - 1) * P))[:, None], NX * CAP + p[:, None] + [0, P],
                                0).astype(np.float32),
                 steps=np.tile(np.arange(NB, dtype=np.float32), (P, 1)))
    at, cols = {}, 0
    for name, a in parts.items():
        at[name] = (cols, cols + a.shape[1])
        cols += a.shape[1]
    return np.concatenate(list(parts.values()), 1), at


CONSTS, CAT = lay_constants()


def edge_pass(nc, ctx, cst, QT, kv_dram, src_dram, featx_dram, feat_t_dram, agg_dram, bases, flag, penc, relT):
    def sb(name, shape, dt=F32):
        return ctx.enter_context(nc.sbuf_tensor(name, shape, dt))

    def sem(name):
        return ctx.enter_context(nc.semaphore(name))

    R = 3
    NR = NREL + W + 2
    idx = [sb(f"e_idx{i}", [P, TG], I32) for i in range(R)]
    rows = [sb(f"e_rows{i}", [P, G], BF16) for i in range(R)]
    kv = [sb(f"e_kv{i}", [P, TG, KVW]) for i in range(R)]
    onehot = [sb(f"e_onehot{i}", [P, G]) for i in range(R)]
    qblock = [sb(f"e_qblock{i}", [P, DC, P]) for i in range(R)]
    qrel = [sb(f"e_qrel{i}", [P, P]) for i in range(R)]
    prob = [sb(f"e_prob{i}", [P, G]) for i in range(R)]
    probT = [sb(f"e_probT{i}", [P, TG, P]) for i in range(R)]
    carry = [sb(f"e_carry{i}", [P, P]) for i in range(R)]
    acc = [sb(f"e_acc{i}", [P, CW]) for i in range(R)]
    carried = [sb(f"e_carried{i}", [P, CW]) for i in range(R)]
    small = [sb(f"e_small{i}", [P, 8]) for i in range(R)]
    kT = sb("e_kT", [P, DC, G])
    psK = ctx.enter_context(nc.psum_tensor("psK", [P, 2, 512], F32))
    psD = ctx.enter_context(nc.psum_tensor("psD", [P, 2, 512], F32))
    psP = ctx.enter_context(nc.psum_tensor("psP", [P, 2, 512], F32))
    psA = ctx.enter_context(nc.psum_tensor("psA", [P, 512], F32))
    psX = ctx.enter_context(nc.psum_tensor("psX", [P, 512], F32))
    MX, MC, MM, NM, AL = (slice(i, i + 1) for i in range(5))

    ident = cst("ident")
    s_idx = [sem(f"es_idx{i}") for i in range(R)]
    s_rows = [sem(f"es_rows{i}") for i in range(R)]
    s_kv = [sem(f"es_kv{i}") for i in range(R)]
    s_out = [sem(f"es_out{i}") for i in range(R)]
    s_init = sem("es_init")
    s_qb = sem("es_qb")
    s_exp = sem("es_exp")
    s_pT = sem("es_pT")
    s_cas = sem("es_cas")
    s_m = sem("es_m")
    s_carry = sem("es_carry")
    s_oh = sem("es_oh")
    s_kTv = sem("es_kTv")
    s_kTa = sem("es_kTa")
    s_x = sem("es_x")
    s_acc = sem("es_acc")
    s_d = sem("es_d")
    s_pp = sem("es_pp")
    s_agg = sem("es_agg")
    s_pk = sem("es_pk")
    s_px = sem("es_px")

    LO, HI, WARM = -1, 2, 6

    with nc.Block() as blk:
        @blk.sync
        def _(sp):
            def step(T):
                g = T(0)
                if g.live:
                    if g.first >= R:
                        hold(sp, s_kv[g.slot], g.rnd * (16 * TG))
                    sp.dma_start(idx[g.slot][:, :], src_dram[bass.ds(g.t, 1)].rearrange("a (p t) -> (a p) t", t=TG)
                                 ).then_inc(s_idx[g.slot], 16)
                    if g.first >= R:
                        hold(sp, s_oh, g.t - (R - 1))
                    sp.dma_start(rows[g.slot][0:NREL, :],
                                 feat_t_dram[bass.ds(g.t, 1)].to_broadcast([NREL, G])).then_inc(s_rows[g.slot], 16)
                    sp.dma_start(rows[g.slot][NREL:NR, :],
                                 featx_dram[bass.ds(g.t, 1)].to_broadcast([W + 2, G])).then_inc(s_rows[g.slot], 16)
                o = T(5)
                if o.live:
                    base = sp.value_load(bases[0:1, bass.ds(o.t, 1)], min_val=0, max_val=N - 1)
                    if o.first >= 1:
                        b = T(6)
                        hold(sp, s_out[b.slot], (b.rnd + 1) * (16 * H))
                    hold(sp, s_acc, o.t + 1)
                    for h in range(H):
                        sp.dma_start(agg_dram[bass.ds(base, W), h, :], acc[o.slot][h * W:(h + 1) * W, :]
                                     ).then_inc(s_out[o.slot], 16)
            pipeline(sp, NG, 0, 6, R, WARM, step)
            for i in range(R):
                sp.wait_ge(s_out[i], (NG // R) * 16 * H)

        @blk.gpsimd
        def _(pool):
            def step(T):
                g = T(0)
                if g.live:
                    if g.first >= R:
                        pool.wait_ge(s_agg, g.t - (R - 1))
                    hold(pool, s_idx[g.slot], (g.rnd + 1) * 16)
                    for t in range(TG):
                        pool.indirect_dma_start(
                            out=kv[g.slot][:, t, :], out_offset=None, in_=kv_dram[:, :],
                            in_offset=bass.IndirectOffsetOnAxis(ap=idx[g.slot][:, t:t + 1], axis=0),
                        ).then_inc(s_kv[g.slot], 16)
            pipeline(pool, NG, 0, 0, R, WARM, step)

        @blk.scalar
        def _(act):
            act.preload_act_table(ACT.Exp)
            act.wait_ge(s_init, 3)

            def step(T):
                a = T(-1)
                if a.live:
                    base = act.value_load(bases[0:1, bass.ds(a.t, 1)], min_val=0, max_val=N - 1)
                    if a.first >= R:
                        hold(act, s_d, a.t - (R - 1))
                    for b in range(2):
                        act.copy(
                            qblock[a.slot][b * HD:(b + 1) * HD, :, :].rearrange(
                                "p a (h w) -> p a h w", w=W)[:, 0, b, :],
                            QT[b * HD:(b + 1) * HD, 0, bass.ds(base, W)])
                        act.copy(
                            qblock[a.slot][b * HD:(b + 1) * HD, :, :].rearrange(
                                "p a (h w) -> p a h w", w=W)[:, 1, 2 + b, :],
                            QT[b * HD:(b + 1) * HD, 1, bass.ds(base, W)]).then_inc(s_qb, 1)
                g, c = T(0), T(1)
                if g.live:
                    act.wait_ge(s_m, g.t * 3 + 3)
                    if g.first >= R:
                        act.wait_ge(s_pp, g.t * 2 - 2 * (R - 1))
                    act.activation(prob[g.slot][:, :].rearrange("p (c q) -> p c q", c=2), psD[:, :, 0:GH], ACT.Exp,
                                   bias=small[g.slot][:, NM], scale=SCALE).then_inc(s_exp, 1)
                    act.activation(small[g.slot][:, AL], small[g.slot][:, MC], ACT.Exp,
                                   bias=small[g.slot][:, NM], scale=SCALE).then_inc(s_exp, 1)
                if a.live:
                    if a.first >= 1:
                        act.wait_ge(s_d, a.t)
                    for j in range(2):
                        act.wait_ge(s_pk, a.t * 4 + 2 * j + 2)
                        act.copy(kT[:, 1, j * GH:(j + 1) * GH], psK[:, 1, 0:GH]).then_inc(s_kTa, 1)
                if c.live:
                    act.wait_ge(s_exp, c.t * 2 + 2)
                    act.wait_ge(s_agg, c.t + 1)
                    act.activation(carried[c.slot][:, :], psA[:, P:P + CW], ACT.Copy,
                                   scale=small[c.slot][:, AL]).then_inc(s_cas, 1)
                if g.live:
                    if g.first >= R:
                        act.wait_ge(s_agg, g.t - (R - 1))
                    for j, (lo, hi) in enumerate(((0, 4), (4, TG))):
                        act.wait_ge(s_pp, g.t * 2 + j + 1)
                        act.copy(probT[g.slot][:, lo:hi, :].rearrange("p t q -> p (t q)"),
                                 psP[:, j, 0:(hi - lo) * P]).then_inc(s_pT, 1)
            pipeline(act, NG, LO, HI, R, WARM, step)

        @blk.vector
        def _(dve):
            for i in range(R):
                dve.memset(qblock[i][:, :, :], 0.0)
                dve.tensor_copy(qrel[i][:, :], cst("pen"))
            dve.memset(acc[R - 1][:, :], 0.0).then_inc(s_init, 1)
            dve.memset(small[R - 1][:, :], 0.0).then_inc(s_init, 1)
            dve.memset(prob[0][:, 0:1], 0.0).then_inc(s_init, 1)
            dve.wait_ge(s_init, 3)

            def step(T):
                g = T(0)
                if g.live:
                    sm = small[g.slot]
                    dve.wait_ge(s_d, g.t + 1)
                    dve.tensor_reduce(sm[:, MX], psD[:, :, 0:GH], AX.XY, ALU.max).then_inc(s_m, 1)
                    dve.wait_ge(s_m, g.t * 3 + 1)
                    dve.wait_ge(s_x, g.t * 2 + 2)
                    dve.scalar_tensor_tensor(out=sm[:, MM], in0=sm[:, MX], scalar=FLOOR, in1=sm[:, MC],
                                             op0=ALU.max, op1=ALU.max).then_inc(s_m, 1)
                    dve.wait_ge(s_m, g.t * 3 + 2)
                    dve.tensor_scalar(sm[:, NM], sm[:, MM], -SCALE, None, ALU.mult).then_inc(s_m, 1)
                a = T(-1)
                if a.live:
                    if a.first >= R:
                        dve.wait_ge(s_agg, a.t - (R - 1))
                    dve.tensor_scalar(carry[a.slot][:, :], cst("first"), flag[:, bass.ds(a.t, 1)], None,
                                      ALU.mult).then_inc(s_carry, 1)
                    dve.wait_ge(s_rows[a.slot], (a.rnd + 1) * 32)
                    if a.first >= R:
                        dve.wait_ge(s_d, a.t - (R - 1))
                    dve.tensor_scalar(onehot[a.slot][0:NR, :], rows[a.slot][0:NR, :], cst("match")[0:NR, :], None,
                                      ALU.is_equal).then_inc(s_oh, 1)
                if a.live:
                    if a.first >= 1:
                        dve.wait_ge(s_d, a.t)
                    for j in range(2):
                        dve.wait_ge(s_pk, a.t * 4 + 2 * j + 1)
                        dve.tensor_copy(kT[:, 0, j * GH:(j + 1) * GH], psK[:, 0, 0:GH]).then_inc(s_kTv, 1)
                    dve.wait_ge(s_px, a.t + 1)
                    dve.tensor_copy(qrel[a.slot][0:NREL, :], psX[0:NREL, P:2 * P]).then_inc(s_x, 1)
                    dve.tensor_tensor(small[a.slot][:, MC], psX[:, 0:1], penc[:, bass.ds(a.t, 1)],
                                      ALU.add).then_inc(s_x, 1)
                c = T(1)
                if c.live:
                    dve.wait_ge(s_cas, c.t + 1)
                    if c.first >= R:
                        dve.wait_ge(s_out[c.slot], c.rnd * (16 * H))
                    dve.tensor_tensor(acc[c.slot][:, :], psA[:, 0:CW], carried[c.slot][:, :],
                                      ALU.add).then_inc(s_acc, 1)
            pipeline(dve, NG, LO, HI, R, WARM, step)

        @blk.tensor
        def _(pe):
            pe.wait_ge(s_init, 3)
            halves = [slice(a * P // DC, (a + 1) * P // DC) for a in range(DC)]

            def step(T):
                g = T(0)
                if g.live:
                    pe.wait_ge(s_x, g.t * 2 + 1)
                    pe.wait_ge(s_oh, g.t + 1)
                    if g.first >= 1:
                        pe.wait_ge(s_exp, g.t * 2 - 1)
                    for c in range(2):
                        cols = slice(c * GH, (c + 1) * GH)
                        for half in halves:
                            pe.matmul(psD[half, c, 0:GH], qrel[g.slot][0:NR, half], onehot[g.slot][0:NR, cols],
                                      start=True, stop=False, tile_position=(0, half.start))
                        pe.wait_ge(s_kTv, g.t * 2 + c + 1)
                        pe.wait_ge(s_kTa, g.t * 2 + c + 1)
                        for a, half in enumerate(halves):
                            mm = pe.matmul(psD[half, c, 0:GH], qblock[g.slot][:, a, half], kT[:, a, cols],
                                           start=False, stop=True, tile_position=(0, half.start))
                    mm.then_inc(s_d, 1)
                c = T(1)
                if c.live:
                    prev = (c.slot - 1) % R
                    if c.first >= 1:
                        pe.wait_ge(s_acc, c.t)
                    pe.wait_ge(s_carry, c.t + 1)
                    pe.matmul(psA[:, P:P + CW], carry[c.slot][:, :], acc[prev][:, :], start=True, stop=True)
                    for j, (lo, hi) in enumerate(((0, 4), (4, TG))):
                        pe.wait_ge(s_pT, c.t * 2 + j + 1)
                        for t in range(lo, hi):
                            for h in range(H):
                                mm = pe.matmul(psA[h * W:(h + 1) * W, 0:CW], probT[c.slot][:, t, h * W:(h + 1) * W],
                                               kv[c.slot][:, t, D + h * CW:D + (h + 1) * CW],
                                               start=t == 0, stop=t == TG - 1, tile_position=(0, h * W))
                    mm.then_inc(s_agg, 1)
                a = T(-1)
                if a.live:
                    pe.wait_ge(s_kv[a.slot], (a.rnd + 1) * (16 * TG))
                    for j in range(4):
                        half, third = j % 2, j // 2
                        if a.first >= 1 or j >= 2:
                            pe.wait_ge(s_kTa if half else s_kTv, a.t * 2 + third)
                        for t in range(3):
                            mm = pe.transpose(psK[:, half, t * P:(t + 1) * P],
                                              kv[a.slot][:, third * 3 + t, half * P:(half + 1) * P], ident)
                        mm.then_inc(s_pk, 1)
                    if a.first >= 1:
                        pe.wait_ge(s_m, a.t * 3 - 1)
                        pe.wait_ge(s_x, a.t * 2)
                    pe.wait_ge(s_carry, a.t + 1)
                    pe.matmul(psX[:, 0:1], carry[a.slot][:, :], small[(a.slot - 1) % R][:, MM], start=True, stop=True)
                    pe.wait_ge(s_qb, a.t * 2 + 2)
                    for b in range(DC):
                        mm = pe.matmul(psX[0:NREL, P:2 * P], relT, qblock[a.slot][:, b, :],
                                       start=b == 0, stop=b == DC - 1)
                    mm.then_inc(s_px, 1)
                if g.live:
                    pe.wait_ge(s_exp, g.t * 2 + 1)
                    for j, (lo, hi) in enumerate(((0, 4), (4, TG))):
                        if g.first >= 1:
                            pe.wait_ge(s_pT, g.t * 2 + j - 1)
                        for t in range(lo, hi):
                            mm = pe.transpose(psP[:, j, (t - lo) * P:(t - lo + 1) * P],
                                              prob[g.slot][:, t * P:(t + 1) * P], ident)
                        mm.then_inc(s_pp, 1)
            pipeline(pe, NG, LO, HI, R, WARM, step)


def node_rows(t):
    return min(t * P, LAST) if isinstance(t, int) else t * P


def own_rows(t):
    lo = NT * P - N if isinstance(t, int) and t == NT - 1 else 0
    return lo, bass.ds(node_rows(t) + lo, P - lo)


def prepare(nc, ctx, cst, io, dram, QT, bases, flag, penc, relT):
    def sb(name, shape, dt=F32):
        return ctx.enter_context(nc.sbuf_tensor(name, shape, dt))

    def sem(name):
        return ctx.enter_context(nc.semaphore(name))

    R = 2
    xin = [sb(f"p_x{i}", [P, D]) for i in range(R)]
    xn = [sb(f"p_xn{i}", [P, D]) for i in range(R)]
    enh = [sb(f"p_enh{i}", [P, D]) for i in range(R)]
    enhT = [sb(f"p_enhT{i}", [P, DC, P]) for i in range(R)]
    qrow = [sb(f"p_q{i}", [P, D]) for i in range(R)]
    kvrow = [sb(f"p_kv{i}", [P, KVW]) for i in range(R)]
    stat = [sb(f"p_stat{i}", [P, 12]) for i in range(R)]
    wkv = sb("p_wkv", [P, DC, 2 * D])
    wq = sb("p_wq", [P, DC, D])
    bias = sb("p_bias", [P, 3, D])
    qe = sb("p_qe", [P, D])
    qe01 = sb("p_qe01", [P, D])
    relraw = sb("p_relraw", [NREL, 2 * HD])
    edge = [sb(f"p_edge{i}", [P, G], I32) for i in range(2)]
    epos = sb("p_epos", [P, G])
    epos2 = sb("p_epos2", [P, G])
    feat = [sb(f"p_feat{i}", [P, G], BF16) for i in range(2)]
    zero = sb("p_zero", [P, 5 * H * CW])
    basef = sb("p_basef", [P, NG])
    baseall = sb("p_baseall", [P, NG])
    delta = sb("p_delta", [P, NG])
    psT = ctx.enter_context(nc.psum_tensor("p_psT", [P, 512], F32))
    psKV = [ctx.enter_context(nc.psum_tensor(f"p_psKV{i}", [P, 512], F32)) for i in range(R)]
    psQ = [ctx.enter_context(nc.psum_tensor(f"p_psQ{i}", [P, 512], F32)) for i in range(R)]
    psQT = ctx.enter_context(nc.psum_tensor("p_psQT", [P, 512], F32))
    ident = cst("ident")

    s_w = sem("ps_w")
    s_e = [sem(f"ps_e{i}") for i in range(2)]
    s_f = sem("ps_f")
    s_z = sem("ps_z")
    s_set = sem("ps_set")
    s_zero = sem("ps_zero")
    s_pb = sem("ps_pb")
    s_x = [sem(f"ps_x{i}") for i in range(R)]
    s_st = [sem(f"ps_st{i}") for i in range(R)]
    s_ln = sem("ps_ln")
    s_sd = sem("ps_sd")
    s_eT = sem("ps_eT")
    s_qT = sem("ps_qT")
    s_ev = sem("ps_ev")
    s_t = sem("ps_t")
    s_mm = sem("ps_mm")
    s_tq = sem("ps_tq")

    chunks = [(c * P, min(NG - c * P, P)) for c in range(-(-NG // P))]
    full, tail = divmod(E, G)
    NSRC = NG * G

    with nc.Block() as blk:
        @blk.sync
        def _(sp):
            for a in range(DC):
                rowsl = slice(a * P, (a + 1) * P)
                sp.dma_start(wkv[:, a, 0:D], io["Wk"][rowsl, :]).then_inc(s_w, 16)
                sp.dma_start(wkv[:, a, D:2 * D], io["Wv"][rowsl, :]).then_inc(s_w, 16)
                sp.dma_start(wq[:, a, :], io["Wq"][rowsl, :]).then_inc(s_w, 16)
            for j, name in enumerate(("bq", "bk", "bv")):
                sp.dma_start(bias[:, j, :], io[name].rearrange("(a d) -> a d", a=1).to_broadcast([P, D])
                             ).then_inc(s_w, 16)
            sp.dma_start(qe[:, :], io["query"].rearrange("(a d) -> a d", a=1).to_broadcast([P, D])
                         ).then_inc(s_w, 16)
            for b in range(2):
                sp.dma_start(relraw[:, b * HD:(b + 1) * HD], io["rel"]).then_inc(s_w, 16)
            with nc.allow_non_contiguous_dma("the first edge's node of each group"):
                sp.dma_start(bases[0:1, :], io["dst"].rearrange("(a e) -> a e", a=1)[:, 0:E:G]).then_inc(s_w, 16)

            def step(T):
                g = T(0)
                if g.live:
                    r0 = node_rows(g.t)
                    if g.first >= R:
                        hold(sp, s_ln, g.t * 5 - 5 * (R - 1) - 1)
                    sp.dma_start(xin[g.slot][:, :], io["x"][bass.ds(r0, P), :]).then_inc(s_x[g.slot], 16)
                o = T(2)
                if o.live:
                    lo, r = own_rows(o.t)
                    hold(sp, s_ln, o.t * 5 + 5)
                    sp.dma_start(dram["xn"][r, :], xn[o.slot][lo:P, :]).then_inc(s_st[o.slot], 16)
                    hold(sp, s_ev, o.t * 3 + 3)
                    sp.dma_start(dram["kv"][r, :], kvrow[o.slot][lo:P, :]).then_inc(s_st[o.slot], 16)
            pipeline(sp, NT, 0, 2, R, 4, step)
            for i in range(R):
                sp.wait_ge(s_st[i], 32 * len(range(i, NT, R)))
            sp.wait_ge(s_f, 32 * len(chunks))
            sp.wait_ge(s_z, 16 * (10 + 2 + 2))

        @blk.gpsimd
        def _(pool):
            pool.memset(zero[:, :], 0.0).then_inc(s_zero, 1)
            for c, (g0, n) in enumerate(chunks):
                whole = min(n, full - g0)
                for j, name in enumerate(("dst", "etype")):
                    if whole < n:
                        pool.memset(edge[j][:, :], 0 if j else 1000000).then_inc(s_zero, 1)
                        pool.wait_ge(s_zero, 2 + j)
                    pool.dma_start(edge[j][0:whole, :],
                                   io[name][g0 * G:(g0 + whole) * G].rearrange("(g e) -> g e", e=G)
                                   ).then_inc(s_e[j], 16)
                    if whole < n:
                        pool.dma_start(edge[j][whole:n, 0:tail],
                                       io[name][full * G:E].rearrange("(a e) -> a e", a=1)).then_inc(s_e[j], 16)
                pool.wait_ge(s_set, 2 + 4 * (c + 1))
                pool.dma_start(dram["featx"][g0:g0 + n, :], feat[0][0:n, :]).then_inc(s_f, 16)
                pool.dma_start(dram["featt"][g0:g0 + n, :], feat[1][0:n, :]).then_inc(s_f, 16)
            pool.wait_ge(s_zero, 1)
            pool.dma_start(dram["src"].rearrange("g e -> (g e)")[0:E].rearrange("(a b) -> a b", b=1250),
                           io["src"].rearrange("(a b) -> a b", b=1250)).then_inc(s_z, 16)
            pool.dma_start(dram["src"].rearrange("g e -> (g e)")[E:NSRC].rearrange("(a b) -> a b", a=1),
                           zero[0:1, 0:NSRC - E].bitcast(I32)).then_inc(s_z, 16)
            for j in range(10):
                pool.dma_start(dram["agg"][j * 5 * P:(j + 1) * 5 * P].rearrange("(p a) h c -> p (a h c)", a=5),
                               zero[:, :]).then_inc(s_z, 16)
            for j in range(2):
                pool.dma_start(dram["xs"][NX * CAP + 2 * P * j:NX * CAP + 2 * P * (j + 1)].rearrange(
                    "(p a) c -> p (a c)", a=2), zero[:, 0:2 * D]).then_inc(s_z, 16)

        @blk.scalar
        def _(act):
            act.preload_act_table(ACT.Sqrt)

            def step(T):
                g = T(0)
                if g.live:
                    act.wait_ge(s_ln, g.t * 5 + 2)
                    act.activation(stat[g.slot][:, 8:9], stat[g.slot][:, 7:8], ACT.Sqrt, bias=cst("eps")
                                   ).then_inc(s_sd, 1)
                    act.wait_ge(s_t, g.t + 1)
                    act.copy(enhT[g.slot][:, :, :].rearrange("p a q -> p (a q)"), psT[:, 0:D]).then_inc(s_eT, 1)
                c = T(1)
                if c.live:
                    act.wait_ge(s_tq, c.t + 1)
                    act.copy(QT[:, :, bass.ds(node_rows(c.t), P)],
                             psQT[:, 0:D].rearrange("p (a q) -> p a q", a=DC)).then_inc(s_qT, 1)
            pipeline(act, NT, 0, 1, R, 4, step)

        @blk.vector
        def _(dve):
            count = [0]

            def link(ins):
                count[0] += 1
                ins.then_inc(s_set, 1)
                dve.wait_ge(s_set, count[0])

            dve.memset(QT[:, :, N:QW], 0.0)
            for i in range(R):
                dve.memset(kvrow[i][:, :], 1.0)
            dve.wait_ge(s_w, 16 * 13)
            link(dve.tensor_scalar(qe01[:, :], qe[:, :], 0.1, None, ALU.mult))
            link(dve.tensor_copy(basef[0:1, :], bases[0:1, :]))
            for c, (g0, n) in enumerate(chunks):
                dmas = c + 1 + (g0 + n > full)
                for j in range(2):
                    dve.wait_ge(s_e[j], 16 * dmas)
                link(dve.tensor_copy(epos[0:n, :], edge[0][0:n, :]))
                link(dve.tensor_scalar(epos2[0:n, :], epos[0:n, :], epos[0:n, 0:1], float(W),
                                       ALU.subtract, ALU.min))
                if c:
                    dve.wait_ge(s_f, 32 * c)
                link(dve.tensor_scalar(feat[0][0:n, :].rearrange("g (t p) -> g t p", t=TG),
                                       epos2[0:n, :].rearrange("g (p t) -> g t p", t=TG), -1.0, None, ALU.max))
                link(dve.tensor_copy(feat[1][0:n, :].rearrange("g (t p) -> g t p", t=TG),
                                     edge[1][0:n, :].rearrange("g (p t) -> g t p", t=TG)))
            dve.wait_ge(s_pb, 2)
            link(dve.tensor_scalar(relT, psQT[:, 0:NREL], 0.2, None, ALU.mult))
            link(dve.tensor_copy(baseall[:, :], psT[:, 0:NG]))
            link(dve.memset(flag[:, 0:1], 0.0))
            link(dve.memset(penc[:, 0:1], -BIG))
            link(dve.tensor_tensor(delta[:, 1:NG], baseall[:, 1:NG], baseall[:, 0:NG - 1], ALU.subtract))
            link(dve.tensor_scalar(flag[:, 1:NG], delta[:, 1:NG], cst("inwin"), None, ALU.is_equal))
            link(dve.tensor_scalar(basef[:, 1:NG], delta[:, 1:NG], float(W), cst("isfirst"), ALU.is_lt, ALU.mult))
            link(dve.tensor_scalar(penc[:, 1:NG], basef[:, 1:NG], -1.0, BIG, ALU.add, ALU.mult))

            def step(T):
                g = T(0)
                if g.live:
                    st = stat[g.slot]
                    dve.wait_ge(s_x[g.slot], (g.rnd + 1) * 16)
                    dve.bn_stats(st[:, 0:6], xin[g.slot][:, :]).then_inc(s_ln, 1)
                    hold(dve, s_ln, g.t * 5 + 1)
                    dve.bn_aggr(st[:, 6:8], st[:, 0:6]).then_inc(s_ln, 1)
                c = T(1)
                if c.live:
                    dve.wait_ge(s_mm, c.t + 1)
                    if c.first >= R:
                        dve.wait_ge(s_st[c.slot], c.rnd * 32)
                    kvr = kvrow[c.slot]
                    dve.tensor_tensor(kvr[:, 0:D], psKV[c.slot][:, 0:D], bias[:, 1, :], ALU.add).then_inc(s_ev, 1)
                    dve.tensor_tensor(kvr[:, D:KVW].rearrange("p (h c) -> p h c", h=H)[:, :, 0:HD],
                                      psKV[c.slot][:, D:2 * D].rearrange("p (h c) -> p h c", h=H),
                                      bias[:, 2, :].rearrange("p (h c) -> p h c", h=H), ALU.add).then_inc(s_ev, 1)
                    if c.first >= R:
                        dve.wait_ge(s_tq, c.t - (R - 1))
                    dve.tensor_tensor(qrow[c.slot][:, :], psQ[c.slot][:, 0:D], bias[:, 0, :], ALU.add
                                      ).then_inc(s_ev, 1)
                if g.live:
                    dve.wait_ge(s_sd, g.t + 1)
                    dve.reciprocal(st[:, 9:10], st[:, 8:9]).then_inc(s_ln, 1)
                    dve.wait_ge(s_ln, g.t * 5 + 3)
                    if g.first >= R:
                        dve.wait_ge(s_st[g.slot], g.rnd * 32)
                    dve.tensor_scalar(xn[g.slot][:, :], xin[g.slot][:, :], st[:, 6:7], st[:, 9:10],
                                      ALU.subtract, ALU.mult).then_inc(s_ln, 1)
                    dve.wait_ge(s_ln, g.t * 5 + 4)
                    if g.first >= R:
                        dve.wait_ge(s_t, g.t - (R - 1))
                    dve.tensor_tensor(enh[g.slot][:, :], xn[g.slot][:, :], qe01[:, :], ALU.add).then_inc(s_ln, 1)
            pipeline(dve, NT, 0, 1, R, 4, step)

        @blk.tensor
        def _(pe):
            pe.wait_ge(s_w, 16 * 13)
            pe.transpose(psQT[:, 0:NREL], relraw[:, :], ident[0:NREL, 0:NREL]).then_inc(s_pb, 1)
            pe.wait_ge(s_set, 2)
            pe.matmul(psT[:, 0:NG], cst("ones")[0:1, :], basef[0:1, :], start=True, stop=True).then_inc(s_pb, 1)
            pe.wait_ge(s_set, 2 + 4 * len(chunks) + 2)

            def step(T):
                g = T(0)
                if g.live:
                    pe.wait_ge(s_ln, g.t * 5 + 5)
                    if g.first >= 1:
                        pe.wait_ge(s_eT, g.t)
                    for a in range(DC):
                        mm = pe.transpose(psT[:, a * P:(a + 1) * P], enh[g.slot][:, a * P:(a + 1) * P], ident)
                    mm.then_inc(s_t, 1)
                c = T(1)
                if c.live:
                    pe.wait_ge(s_ev, c.t * 3 + 3)
                    if c.first >= 1:
                        pe.wait_ge(s_qT, c.t)
                    for a in range(DC):
                        mm = pe.transpose(psQT[:, a * P:(a + 1) * P], qrow[c.slot][:, a * P:(a + 1) * P], ident)
                    mm.then_inc(s_tq, 1)
                if g.live:
                    pe.wait_ge(s_eT, g.t + 1)
                    if g.first >= R:
                        pe.wait_ge(s_ev, g.t * 3 - 3 * (R - 1))
                    for a in range(DC):
                        pe.matmul(psKV[g.slot][:, :], enhT[g.slot][:, a, :], wkv[:, a, :],
                                  start=a == 0, stop=a == DC - 1)
                    for a in range(DC):
                        mm = pe.matmul(psQ[g.slot][:, 0:D], enhT[g.slot][:, a, :], wq[:, a, :],
                                       start=a == 0, stop=a == DC - 1)
                    mm.then_inc(s_mm, 1)
            pipeline(pe, NT, 0, 1, R, 4, step)


def after_edges(nc, ctx, cst, io, dram, slots, gap, rows, ints):
    def sb(name, shape, dt=F32):
        return ctx.enter_context(nc.sbuf_tensor(name, shape, dt))

    def sem(name):
        return ctx.enter_context(nc.semaphore(name))

    R = 2
    ins = {n: [sb(f"n_{n}{i}", [P, w]) for i in range(R)]
           for n, w in (("x", D), ("xn", D), ("agg", H * CW), ("v", H * CW))}
    msg = [sb(f"n_msg{i}", [P, D]) for i in range(R)]
    tmp = [sb(f"n_tmp{i}", [P, D]) for i in range(R)]
    msgT = [sb(f"n_msgT{i}", [P, DC, P]) for i in range(R)]
    ya = [sb(f"n_ya{i}", [P, D]) for i in range(R)]
    yb = [sb(f"n_yb{i}", [P, D]) for i in range(R)]
    x1 = [sb(f"n_x1{i}", [P, D]) for i in range(R)]
    h2 = [sb(f"n_h2{i}", [P, D]) for i in range(R)]
    h2T = [sb(f"n_h2T{i}", [P, DC, P]) for i in range(R)]
    x2 = [sb(f"n_x2{i}", [P, D]) for i in range(R)]
    st = [sb(f"n_st{i}", [P, 3, 10]) for i in range(R)]
    den = [sb(f"n_den{i}", [P, 3, H]) for i in range(R)]
    rt = [sb(f"n_rt{i}", [P, 12, NX]) for i in range(R)]
    top = [sb(f"n_top{i}", [P, NX], U32) for i in range(R)]
    slot = [sb(f"n_slot{i}", [P, 2], I32) for i in range(R)]
    wo = sb("n_wo", [P, DC, D])
    wr = sb("n_wr", [P, DC, NX])
    vec = sb("n_vec", [P, 3, D])
    br = sb("n_br", [P, NX])
    run = sb("n_run", [P, NX])
    zero = sb("n_zero", [P, 2 * D])
    places = sb("n_places", [P, NT, 2])
    beyond = sb("n_beyond", [P, 2 * NT, NX])
    shift = sb("n_shift", [P, 2 * NT])
    bl = sb("n_bl", [P, 8, NX])
    blk_gt = sb("n_gt", [P, NX, BPE])
    blk_ge = sb("n_ge", [1, NB, NX])
    blk_gn = sb("n_gn", [1, NB, NX])
    blk_r = sb("n_r", [1, 6, NB])
    psM = ctx.enter_context(nc.psum_tensor("n_psM", [P, 512], F32))
    psO = ctx.enter_context(nc.psum_tensor("n_psO", [P, 512], F32))
    psH = ctx.enter_context(nc.psum_tensor("n_psH", [P, 512], F32))
    psL = ctx.enter_context(nc.psum_tensor("n_psL", [P, 512], F32))
    psR = ctx.enter_context(nc.psum_tensor("n_psR", [P, 512], F32))
    ident = cst("ident")

    s_w = sem("ns_w")
    s_in = [sem(f"ns_in{i}") for i in range(R)]
    s_x1 = [sem(f"ns_x1{i}") for i in range(R)]
    s_sc = [sem(f"ns_sc{i}") for i in range(R)]
    s_tail = sem("ns_tail")
    s_z = sem("ns_z")
    s_v = sem("ns_v")
    s_sd = sem("ns_sd")
    s_mT = sem("ns_mT")
    s_pe = sem("ns_pe")
    s_end = sem("ns_end")
    VK = 42

    with nc.Block() as blk:
        @blk.sync
        def _(sp):
            for a in range(DC):
                sp.dma_start(wo[:, a, :], io["Wo"][a * P:(a + 1) * P, :]).then_inc(s_w, 16)
                sp.dma_start(wr[:, a, :], io["Wr"][a * P:(a + 1) * P, :]).then_inc(s_w, 16)
            for j, name in enumerate(("bo", "gamma", "beta")):
                sp.dma_start(vec[:, j, :], io[name].rearrange("(a d) -> a d", a=1).to_broadcast([P, D])
                             ).then_inc(s_w, 16)
            sp.dma_start(br[:, :], io["br"].rearrange("(a d) -> a d", a=1).to_broadcast([P, NX])).then_inc(s_w, 16)

            def step(T):
                g = T(0)
                if g.live:
                    r0 = bass.ds(node_rows(g.t), P)
                    if g.first >= R:
                        hold(sp, s_v, (g.t - R) * VK + V_X1)
                    sp.dma_start(ins["agg"][g.slot][:, :], dram["agg"][r0].rearrange("n h c -> n (h c)")
                                 ).then_inc(s_in[g.slot], 16)
                    sp.dma_start(ins["v"][g.slot][:, :], dram["kv"][r0, D:KVW]).then_inc(s_in[g.slot], 16)
                    sp.dma_start(ins["xn"][g.slot][:, :], dram["xn"][r0, :]).then_inc(s_in[g.slot], 16)
                    sp.dma_start(ins["x"][g.slot][:, :], io["x"][r0, :]).then_inc(s_in[g.slot], 16)
                o = T(1)
                if o.live:
                    hold(sp, s_v, o.t * VK + V_X1)
                    lo, r = own_rows(o.t)
                    sp.dma_start(dram["x1"][r, :], x1[o.slot][lo:P, :]
                                 ).then_inc(s_x1[o.slot], 16)
            pipeline(sp, NT, 0, 1, R, 2, step)
            for i in range(R):
                sp.wait_ge(s_x1[i], 16 * len(range(i, NT, R)))
                sp.wait_ge(s_sc[i], 32 * len(range(i, NT, R)))
            sp.wait_ge(s_end, 1)
            for e in range(NX):
                n = sp.value_load(ints[0:1, e:e + 1], min_val=0, max_val=N)
                sp.dma_start(dram["xs"][bass.ds(n + e * CAP, BT), :].rearrange("(p a) c -> p (a c)", a=2),
                             zero[:, :]).then_inc(s_tail, 16)
            sp.wait_ge(s_tail, 16 * NX)

        @blk.gpsimd
        def _(pool):
            def step(T):
                g = T(0)
                if g.live:
                    hold(pool, s_v, g.t * VK + VK)
                    for k in range(2):
                        pool.indirect_dma_start(
                            out=dram["xs"][:, :], out_offset=bass.IndirectOffsetOnAxis(ap=slot[g.slot][:, k:k + 1],
                                                                                      axis=0),
                            in_=x2[g.slot][:, :], in_offset=None).then_inc(s_sc[g.slot], 16)
            pipeline(pool, NT, 0, 0, R, 2, step)

        @blk.scalar
        def _(act):
            act.preload_act_table(ACT.Sqrt)

            def step(T):
                g = T(0)
                if g.live:
                    act.wait_ge(s_pe, g.t * 5 + 1)
                    act.copy(msgT[g.slot][:, :, :].rearrange("p a q -> p (a q)"), psM[:, 0:D]).then_inc(s_mT, 1)
                    for j in range(3):
                        if j == 2:
                            act.wait_ge(s_pe, g.t * 5 + 3)
                            act.copy(h2T[g.slot][:, :, :].rearrange("p a q -> p (a q)"), psH[:, 0:D]
                                     ).then_inc(s_mT, 1)
                        act.wait_ge(s_v, g.t * VK + V_MV[j])
                        act.activation(st[g.slot][:, j, 8:9], st[g.slot][:, j, 7:8], ACT.Sqrt, bias=cst("eps")
                                       ).then_inc(s_sd, 1)
            pipeline(act, NT, 0, 0, R, 2, step)

        @blk.vector
        def _(dve):
            dve.memset(zero[:, :], 0.0).then_inc(s_z, 1)
            dve.memset(run[:, :], 0.0).then_inc(s_z, 1)
            dve.wait_ge(s_z, 2)
            dve.wait_ge(s_w, 16 * 8)

            def step(T):
                g = T(0)
                if not g.live:
                    return
                i, last = g.slot, isinstance(g.t, int) and g.t == NT - 1
                n = [0]

                def link(ins, alone=False):
                    n[0] += 1
                    ins.then_inc(s_v, 1)
                    if alone:
                        hold(dve, s_v, g.t * VK + n[0])
                    else:
                        dve.wait_ge(s_v, g.t * VK + n[0])

                agg = ins["agg"][i][:, :].rearrange("p (h c) -> p h c", h=H)
                v = ins["v"][i][:, :].rearrange("p (h c) -> p h c", h=H)
                heads = lambda a: a.rearrange("p (h c) -> p h c", h=H)
                wide = lambda a: a.unsqueeze(2).to_broadcast([P, H, HD])
                dve.wait_ge(s_in[i], (g.rnd + 1) * 64)
                link(dve.tensor_scalar(den[i][:, 0, :], agg[:, :, HD], 0.0, None, ALU.is_equal))
                link(dve.tensor_tensor(den[i][:, 1, :], den[i][:, 0, :], agg[:, :, HD], ALU.add))
                link(dve.reciprocal(den[i][:, 2, :], den[i][:, 1, :]))
                link(dve.tensor_tensor(heads(tmp[i][:, :]), v[:, :, 0:HD], wide(den[i][:, 0, :]), ALU.mult))
                link(dve.tensor_tensor(heads(ya[i][:, :]), agg[:, :, 0:HD], wide(den[i][:, 2, :]), ALU.mult))
                if g.first >= R:
                    dve.wait_ge(s_pe, g.t * 5 - 5 * R + 1)
                link(dve.tensor_tensor(msg[i][:, :], tmp[i][:, :], ya[i][:, :], ALU.add))
                assert n[0] == V_MSG
                dve.wait_ge(s_pe, g.t * 5 + 2)
                link(dve.tensor_tensor(ya[i][:, :], psO[:, 0:D], vec[:, 0, :], ALU.add))
                link(dve.tensor_tensor(yb[i][:, :], ya[i][:, :], ins["xn"][i][:, :], ALU.add))

                def norm(j, out, inp):
                    link(dve.bn_stats(st[i][:, j, 0:6], inp), alone=True)
                    link(dve.bn_aggr(st[i][:, j, 6:8], st[i][:, j, 0:6]))
                    assert n[0] == V_MV[j]
                    dve.wait_ge(s_sd, g.t * 3 + j + 1)
                    link(dve.reciprocal(st[i][:, j, 9:10], st[i][:, j, 8:9]))
                    link(dve.tensor_scalar(out, inp, st[i][:, j, 6:7], st[i][:, j, 9:10], ALU.subtract, ALU.mult))

                norm(0, ya[i][:, :], yb[i][:, :])
                link(dve.tensor_tensor(yb[i][:, :], ya[i][:, :], vec[:, 1, :], ALU.mult))
                link(dve.tensor_tensor(ya[i][:, :], yb[i][:, :], vec[:, 2, :], ALU.add))
                if g.first >= R:
                    dve.wait_ge(s_x1[i], g.rnd * 16)
                link(dve.tensor_tensor(x1[i][:, :], ya[i][:, :], ins["x"][i][:, :], ALU.add))
                assert n[0] == V_X1, n
                norm(1, h2[i][:, :], x1[i][:, :])
                assert n[0] == V_H2
                if g.first >= R:
                    dve.wait_ge(s_sc[i], g.rnd * 32)
                norm(2, x2[i][:, :], h2[i][:, :])
                r = rt[i]
                dve.wait_ge(s_pe, g.t * 5 + 4)
                link(dve.tensor_tensor(r[:, 0, :], psL[:, 0:NX], br[:, :], ALU.add), alone=True)
                link(dve.max(r[:, 1, :], r[:, 0, :]), alone=True)
                link(dve.max_index(top[i][:, :], r[:, 1, :], r[:, 0, :]))
                link(dve.tensor_tensor(gap[:, bass.ds(g.t, 1)], r[:, 1, 1:2], r[:, 1, 0:1], ALU.subtract))
                link(dve.tensor_copy(r[:, 2, 0:2], top[i][:, 0:2]))
                link(dve.tensor_scalar(r[:, 3, :], cst("iota8"), r[:, 2, 0:1], None, ALU.is_equal))
                link(dve.tensor_scalar(r[:, 4, :], cst("iota8"), r[:, 2, 1:2], None, ALU.is_equal))
                mask = cst("lastrows")[:, 0:1] if last else 1.0
                link(dve.tensor_scalar(r[:, 5, :], r[:, 3, :], mask, None, ALU.mult))
                link(dve.tensor_scalar(r[:, 6, :], r[:, 4, :], mask, None, ALU.mult))
                link(dve.tensor_tensor(r[:, 7, :], r[:, 5, :], r[:, 6, :], ALU.add))
                assert n[0] == V_C, n
                link(dve.tensor_tensor(r[:, 8, :], run[:, :], cst("cap8"), ALU.add))
                dve.wait_ge(s_pe, g.t * 5 + 5)
                link(dve.tensor_tensor(r[:, 9, :], psR[:, 0:NX], r[:, 8, :], ALU.add))
                link(dve.tensor_tensor(run[:, :], run[:, :], psR[:, NX:2 * NX], ALU.add))
                for k in range(2):
                    link(dve.tensor_tensor(r[:, 10 + k, :], r[:, 9, :], r[:, 5 + k, :], ALU.mult))
                link(dve.tensor_reduce(r[:, 2, 0:2], r[:, 10:12, :], AX.X, ALU.add))
                link(dve.tensor_tensor(r[:, 2, 2:4], r[:, 2, 0:2], cst("spare" if last else "nospare"), ALU.add))
                link(dve.tensor_copy(places[:, bass.ds(g.t, 1), :].rearrange("p a k -> p (a k)"), r[:, 2, 2:4]))
                link(dve.tensor_copy(slot[i][:, :], r[:, 2, 2:4]))
                assert n[0] == VK, n
            pipeline(dve, NT, 0, 0, R, 2, step)

            c = [1]

            def link(ins):
                c[0] += 1
                ins.then_inc(s_end, 1)
                dve.wait_ge(s_end, c[0])
            dve.tensor_copy(ints[0:1, 0:NX], run[0:1, :]).then_inc(s_end, 1)
            dve.wait_ge(s_end, 1)
            steps = cst("steps")[0:1, :]
            link(dve.tensor_tensor(blk_gt[:, :, :], run[:, :].unsqueeze(2).to_broadcast([P, NX, BPE]),
                                   cst("fills").unsqueeze(1).to_broadcast([P, NX, BPE]), ALU.is_gt))
            link(dve.tensor_reduce(bl[:, 0, :], blk_gt[:, :, :], AX.X, ALU.add))
            link(dve.tensor_scalar(bl[:, 2, :], bl[:, 0, :], float(BT), float(-CAP), ALU.mult, ALU.add))
            flat = places[:, :, :].rearrange("p t k -> p (t k)")
            link(dve.tensor_tensor(beyond[:, :, 0:NX - 1], flat.unsqueeze(2).to_broadcast([P, 2 * NT, NX - 1]),
                                   cst("cap8")[:, 1:NX].unsqueeze(1).to_broadcast([P, 2 * NT, NX - 1]), ALU.is_ge))
            link(dve.tensor_tensor(beyond[:, :, 0:NX - 1], beyond[:, :, 0:NX - 1],
                                   bl[:, 2:3, 0:NX - 1].to_broadcast([P, 2 * NT, NX - 1]), ALU.mult))
            link(dve.tensor_reduce(shift[:, :], beyond[:, :, 0:NX - 1], AX.X, ALU.add))
            link(dve.tensor_tensor(flat, flat, shift[:, :], ALU.add))
            link(dve.tensor_scalar(slots[:, :, :].rearrange("p t k -> p (t k)"), flat, float(NB * BT - 1), None,
                                   ALU.min))
            link(dve.tensor_tensor_scan(bl[0:1, 1, :], cst("ones")[0:1, 0:NX], bl[0:1, 0, :], 0.0, ALU.mult, ALU.add))
            link(dve.tensor_tensor(blk_ge[0:1], steps.unsqueeze(2).to_broadcast([1, NB, NX]),
                                   bl[0:1, 1:2, :].to_broadcast([1, NB, NX]), ALU.is_ge))
            link(dve.tensor_tensor(blk_gn[0:1], blk_ge[0:1], bl[0:1, 0:1, :].to_broadcast([1, NB, NX]), ALU.mult))
            link(dve.tensor_reduce(blk_r[0:1, 1, :], blk_ge[0:1], AX.X, ALU.add))
            link(dve.tensor_reduce(blk_r[0:1, 2, :], blk_gn[0:1], AX.X, ALU.add))
            link(dve.tensor_tensor(blk_r[0:1, 3, :], steps, blk_r[0:1, 2, :], ALU.subtract))
            link(dve.tensor_scalar(blk_r[0:1, 4, :], blk_r[0:1, 3, :], float(BT), None, ALU.mult))
            link(dve.tensor_scalar(blk_r[0:1, 5, :], blk_r[0:1, 1, :], float(CAP), None, ALU.mult))
            link(dve.tensor_tensor(blk_r[0:1, 2, :], blk_r[0:1, 4, :], blk_r[0:1, 5, :], ALU.add))
            link(dve.tensor_scalar(rows[0:1, NB:2 * NB], blk_r[0:1, 2, :], float(NX * CAP + BT), None, ALU.min))
            link(dve.tensor_scalar(rows[0:1, 0:NB], blk_r[0:1, 1, :], float(NX - 1), None, ALU.min))

        @blk.tensor
        def _(pe):
            pe.wait_ge(s_w, 16 * 8)

            def step(T):
                g = T(0)
                if not g.live:
                    return
                i = g.slot
                pe.wait_ge(s_v, g.t * VK + V_MSG)
                if g.first >= 1:
                    pe.wait_ge(s_mT, g.t * 2)
                for a in range(DC):
                    mm = pe.transpose(psM[:, a * P:(a + 1) * P], msg[i][:, a * P:(a + 1) * P], ident)
                mm.then_inc(s_pe, 1)
                pe.wait_ge(s_mT, g.t * 2 + 1)
                for a in range(DC):
                    mm = pe.matmul(psO[:, 0:D], msgT[i][:, a, :], wo[:, a, :], start=a == 0, stop=a == DC - 1)
                mm.then_inc(s_pe, 1)
                pe.wait_ge(s_v, g.t * VK + V_H2)
                for a in range(DC):
                    mm = pe.transpose(psH[:, a * P:(a + 1) * P], h2[i][:, a * P:(a + 1) * P], ident)
                mm.then_inc(s_pe, 1)
                pe.wait_ge(s_mT, g.t * 2 + 2)
                for a in range(DC):
                    mm = pe.matmul(psL[:, 0:NX], h2T[i][:, a, :], wr[:, a, :], start=a == 0, stop=a == DC - 1)
                mm.then_inc(s_pe, 1)
                pe.wait_ge(s_v, g.t * VK + V_C)
                pe.matmul(psR[:, 0:NX], cst("before"), rt[i][:, 7, :], start=True, stop=True)
                pe.matmul(psR[:, NX:2 * NX], cst("ones"), rt[i][:, 7, :], start=True, stop=True).then_inc(s_pe, 1)
            pipeline(pe, NT, 0, 0, R, 2, step)


V_MSG, V_X1, V_H2, V_C = 6, 15, 19, 33
V_MV = (10, 17, 21)


def experts(nc, ctx, cst, io, dram, rows):
    def sb(name, shape, dt=F32):
        return ctx.enter_context(nc.sbuf_tensor(name, shape, dt))

    def sem(name):
        return ctx.enter_context(nc.semaphore(name))

    R = 3
    A = BT // P
    xs = [sb(f"f_xs{i}", [P, A, D]) for i in range(R)]
    xT = [sb(f"f_xT{i}", [P, DC, BT]) for i in range(R)]
    w1 = [sb(f"f_w1{i}", [P, DC, FF]) for i in range(R)]
    w2 = [sb(f"f_w2{i}", [P, FC, D]) for i in range(R)]
    y = [sb(f"f_y{i}", [P, A, D]) for i in range(R)]
    hT = sb("f_hT", [P, FC, BT])
    lnraw = sb("f_lnraw", [2 * NX, D])
    ln = sb("f_ln", [P, DC, 2 * NX])
    b1raw = sb("f_b1raw", [NX * FC, P])
    b1 = sb("f_b1", [P, NX * FC])
    b2 = sb("f_b2", [P, NX * D])
    psT = ctx.enter_context(nc.psum_tensor("f_psT", [P, 512], F32))
    psH = ctx.enter_context(nc.psum_tensor("f_psH", [P, 4, 512], F32))
    psY = ctx.enter_context(nc.psum_tensor("f_psY", [P, A, 512], F32))
    ident = cst("ident")

    s_c = sem("fs_c")
    s_cp = sem("fs_cp")
    s_cv = sem("fs_cv")
    s_w = [sem(f"fs_w{i}") for i in range(R)]
    s_y = [sem(f"fs_y{i}") for i in range(R)]
    s_t = sem("fs_t")
    s_xT = sem("fs_xT")
    s_h = sem("fs_h")
    s_g = sem("fs_g")
    s_p = sem("fs_p")
    s_e = sem("fs_e")

    with nc.Block() as blk:
        @blk.sync
        def _(sp):
            sp.dma_start(lnraw[0:NX, :], io["ln_g"]).then_inc(s_c, 16)
            sp.dma_start(lnraw[NX:2 * NX, :], io["ln_b"]).then_inc(s_c, 16)
            sp.dma_start(b1raw[:, :], io["b1"].rearrange("e (c p) -> (e c) p", p=P)).then_inc(s_c, 16)
            sp.dma_start(b2[:, :], io["b2"].rearrange("(a e) d -> a (e d)", a=1).to_broadcast([P, NX * D])
                         ).then_inc(s_c, 16)

            def step(T):
                g = T(0)
                if g.live:
                    e = sp.value_load(rows[0:1, bass.ds(g.t, 1)], min_val=0, max_val=NX - 1)
                    r0 = sp.value_load(rows[0:1, bass.ds(g.t + NB, 1)], min_val=0, max_val=NX * CAP + BT)
                    if g.first >= R:
                        hold(sp, s_p, g.t * A - A * (R - 1))
                    sp.dma_start(xs[g.slot][:, :, :], dram["xs"][bass.ds(r0, BT), :].rearrange(
                        "(a p) c -> p a c", p=P)).then_inc(s_w[g.slot], 16)
                    sp.dma_start(w1[g.slot][:, :, :], io["W1"][bass.ds(e, 1)].rearrange(
                        "e (a p) f -> p (e a) f", p=P)).then_inc(s_w[g.slot], 16)
                    sp.dma_start(w2[g.slot][:, :, :], io["W2"][bass.ds(e, 1)].rearrange(
                        "e (c p) d -> p (e c) d", p=P)).then_inc(s_w[g.slot], 16)
                o = T(2)
                if o.live:
                    hold(sp, s_e, o.t * A + A)
                    sp.dma_start(dram["ys"][bass.ds(o.t * BT, BT), :].rearrange("(a p) c -> p a c", p=P), y[o.slot][:, :, :]
                                 ).then_inc(s_y[o.slot], 16)
            pipeline(sp, NB, 0, 2, R, 5, step)
            for i in range(R):
                sp.wait_ge(s_y[i], 16 * len(range(i, NB, R)))

        @blk.scalar
        def _(act):
            act.preload_act_table(ACT.Gelu)
            act.wait_ge(s_cv, 2)

            def step(T):
                g = T(0)
                e = act.value_load(rows[0:1, bass.ds(g.t, 1)], min_val=0, max_val=NX - 1)
                for c in range(FC):
                    act.wait_ge(s_h, g.t * FC + c + 1)
                    if c == 0 and g.first >= 1:
                        act.wait_ge(s_p, g.t * A)
                    act.activation(hT[:, c, :], psH[:, c % 4, 0:BT], ACT.Gelu,
                                   bias=b1[:, bass.ds(e * FC + c, 1)]).then_inc(s_g, 1)
            pipeline(act, NB, 0, 0, R, 5, step)

        @blk.vector
        def _(dve):
            dve.wait_ge(s_cp, 2)
            dve.tensor_copy(ln[:, :, :], psT[:, 0:DC * 2 * NX].rearrange("p (a e) -> p a e", a=DC)).then_inc(s_cv, 1)
            dve.tensor_copy(b1[:, :], psY[:, 0, 0:NX * FC]).then_inc(s_cv, 1)
            dve.wait_ge(s_cv, 2)
            dve.wait_ge(s_c, 64)

            def step(T):
                g = T(0)
                if g.live:
                    e = dve.value_load(rows[0:1, bass.ds(g.t, 1)], min_val=0, max_val=NX - 1)
                    dve.wait_ge(s_t, g.t + 1)
                    if g.first >= R:
                        dve.wait_ge(s_h, g.t * FC - FC * (R - 1))
                    for a in range(DC):
                        dve.tensor_scalar(xT[g.slot][:, a, :], psT[:, a * BT:(a + 1) * BT],
                                          ln[:, a, bass.ds(e, 1)], ln[:, a, bass.ds(e + NX, 1)],
                                          ALU.mult, ALU.add).then_inc(s_xT, 1)
                c = T(1)
                if c.live:
                    e1 = dve.value_load(rows[0:1, bass.ds(c.t, 1)], min_val=0, max_val=NX - 1)
                    if c.first >= R:
                        dve.wait_ge(s_y[c.slot], c.rnd * 16)
                    for a in range(A):
                        dve.wait_ge(s_p, c.t * A + a + 1)
                        dve.tensor_tensor(y[c.slot][:, a, :], psY[:, a, 0:D], b2[:, bass.ds(e1 * D, D)], ALU.add
                                          ).then_inc(s_e, 1)
            pipeline(dve, NB, 0, 1, R, 5, step)

        @blk.tensor
        def _(pe):
            pe.wait_ge(s_c, 64)
            for a in range(DC):
                mm = pe.transpose(psT[:, a * 2 * NX:(a + 1) * 2 * NX], lnraw[:, a * P:(a + 1) * P],
                                  ident[0:2 * NX, 0:2 * NX])
            mm.then_inc(s_cp, 1)
            pe.transpose(psY[:, 0, 0:NX * FC], b1raw[:, :], ident[0:NX * FC, 0:NX * FC]).then_inc(s_cp, 1)
            pe.wait_ge(s_cv, 2)

            def step(T):
                g = T(0)
                if g.live:
                    pe.wait_ge(s_w[g.slot], (g.rnd + 1) * 48)
                    if g.first >= 1:
                        pe.wait_ge(s_xT, g.t * DC)
                    for a in range(DC):
                        for t in range(A):
                            mm = pe.transpose(psT[:, a * BT + t * P:a * BT + (t + 1) * P],
                                              xs[g.slot][:, t, a * P:(a + 1) * P], ident)
                    mm.then_inc(s_t, 1)
                c = T(1)
                if c.live:
                    for t in range(A):
                        if c.first >= 1:
                            pe.wait_ge(s_e, c.t * A - A + t + 1)
                        for f in range(FC):
                            if t == 0:
                                pe.wait_ge(s_g, c.t * FC + f + 1)
                            mm = pe.matmul(psY[:, t, 0:D], hT[:, f, t * P:(t + 1) * P], w2[c.slot][:, f, :],
                                           start=f == 0, stop=f == FC - 1)
                        mm.then_inc(s_p, 1)
                if g.live:
                    pe.wait_ge(s_xT, g.t * DC + DC)
                    for f in range(FC):
                        if g.first >= 1 or f >= 4:
                            pe.wait_ge(s_g, g.t * FC + f - 3)
                        for a in range(DC):
                            mm = pe.matmul(psH[:, f % 4, 0:BT], w1[g.slot][:, a, f * P:(f + 1) * P],
                                           xT[g.slot][:, a, :], start=a == 0, stop=a == DC - 1)
                        mm.then_inc(s_h, 1)
            pipeline(pe, NB, 0, 1, R, 5, step)


def combine(nc, ctx, cst, dram, out, slots, gap):
    def sb(name, shape, dt=F32):
        return ctx.enter_context(nc.sbuf_tensor(name, shape, dt))

    def sem(name):
        return ctx.enter_context(nc.semaphore(name))

    R = 3
    idx = [sb(f"c_idx{i}", [P, 2], I32) for i in range(R)]
    yy = [sb(f"c_y{i}", [P, 2, D]) for i in range(R)]
    x1 = [sb(f"c_x1{i}", [P, D]) for i in range(R)]
    one = [sb(f"c_one{i}", [P, D]) for i in range(R)]
    two = [sb(f"c_two{i}", [P, D]) for i in range(R)]
    ex = sb("c_ex", [P, NT])
    sm = sb("c_sm", [P, NT])
    wa = sb("c_wa", [P, NT])
    wb = sb("c_wb", [P, NT])
    s_e = sem("cs_e")
    s_s = sem("cs_s")
    s_i = sem("cs_i")
    s_y = [sem(f"cs_y{i}") for i in range(R)]
    s_x = [sem(f"cs_x{i}") for i in range(R)]
    s_v = sem("cs_v")
    s_o = [sem(f"cs_o{i}") for i in range(R)]

    with nc.Block() as blk:
        @blk.scalar
        def _(act):
            act.activation(ex[:, :], gap[:, :], ACT.Exp).then_inc(s_e, 1)

        @blk.vector
        def _(dve):
            dve.wait_ge(s_e, 1)
            dve.tensor_scalar(sm[:, :], ex[:, :], 1.0, None, ALU.add).then_inc(s_s, 1)
            dve.wait_ge(s_s, 1)
            dve.reciprocal(wa[:, :], sm[:, :]).then_inc(s_s, 1)
            dve.wait_ge(s_s, 2)
            dve.tensor_tensor(wb[:, :], wa[:, :], ex[:, :], ALU.mult).then_inc(s_s, 1)
            dve.wait_ge(s_s, 3)

            def step(T):
                g = T(0)
                if g.live:
                    if g.first >= R:
                        dve.wait_ge(s_y[g.slot], g.rnd * 32)
                    dve.tensor_copy(idx[g.slot][:, :], slots[:, bass.ds(g.t, 1), :].rearrange("p a k -> p (a k)")
                                    ).then_inc(s_i, 1)
                c = T(2)
                if c.live:
                    i = c.slot
                    dve.wait_ge(s_y[i], (c.rnd + 1) * 32)
                    dve.wait_ge(s_x[i], (c.rnd + 1) * 16)
                    dve.scalar_tensor_tensor(out=one[i][:, :], in0=yy[i][:, 0, :], scalar=wa[:, bass.ds(c.t, 1)],
                                             in1=x1[i][:, :], op0=ALU.mult, op1=ALU.add).then_inc(s_v, 1)
                    dve.wait_ge(s_v, c.t * 2 + 1)
                    if c.first >= R:
                        dve.wait_ge(s_o[i], c.rnd * 16)
                    dve.scalar_tensor_tensor(out=two[i][:, :], in0=yy[i][:, 1, :], scalar=wb[:, bass.ds(c.t, 1)],
                                             in1=one[i][:, :], op0=ALU.mult, op1=ALU.add).then_inc(s_v, 1)
            pipeline(dve, NT, 0, 2, R, 6, step)

        @blk.gpsimd
        def _(pool):
            def step(T):
                g = T(0)
                if g.first >= R:
                    hold(pool, s_v, g.t * 2 - 2 * (R - 1))
                hold(pool, s_i, g.t + 1)
                for k in range(2):
                    pool.indirect_dma_start(out=yy[g.slot][:, k, :], out_offset=None, in_=dram["ys"][:, :],
                                            in_offset=bass.IndirectOffsetOnAxis(ap=idx[g.slot][:, k:k + 1], axis=0)
                                            ).then_inc(s_y[g.slot], 16)
            pipeline(pool, NT, 0, 0, R, 6, step)

        @blk.sync
        def _(sp):
            def step(T):
                g = T(0)
                if g.live:
                    if g.first >= R:
                        hold(sp, s_v, g.t * 2 - 2 * (R - 1))
                    sp.dma_start(x1[g.slot][:, :], dram["x1"][bass.ds(node_rows(g.t), P), :]).then_inc(s_x[g.slot], 16)
                o = T(2)
                if o.live:
                    hold(sp, s_v, o.t * 2 + 2)
                    lo, r = own_rows(o.t)
                    sp.dma_start(out[r, :], two[o.slot][lo:P, :]
                                 ).then_inc(s_o[o.slot], 16)
            pipeline(sp, NT, 0, 2, R, 6, step)
            for i in range(R):
                sp.wait_ge(s_o[i], 16 * len(range(i, NT, R)))


def build(nc, io, out):
    dram = {name: nc.dram_tensor(f"d_{name}", shape, dt, kind="Internal").ap() for name, shape, dt in (
        ("kv", (N, KVW), F32), ("xn", (N, D), F32), ("x1", (N, D), F32), ("src", (NG, G), I32),
        ("featx", (NG, G), BF16), ("featt", (NG, G), BF16), ("agg", (AR, H, CW), F32),
        ("xs", (NX * CAP + 2 * BT, D), F32), ("ys", (NB * BT, D), F32))}
    with ExitStack() as whole:
        def sb(name, shape, dt=F32):
            return whole.enter_context(nc.sbuf_tensor(name, shape, dt))
        consts = sb("consts", list(CONSTS.shape))
        slots = sb("slots", [P, NT, 2], I32)
        gap = sb("gap", [P, NT])
        rows = sb("rows", [1, 2 * NB], I32)
        ints = sb("ints", [1, NX], I32)
        loaded = whole.enter_context(nc.semaphore("loaded"))

        def cst(name):
            return consts[:, CAT[name][0]:CAT[name][1]]

        with nc.Block() as blk:
            @blk.sync
            def _(sp):
                sp.dma_start(consts[:, :], io["consts"]).then_inc(loaded, 16)
                sp.wait_ge(loaded, 16)
        with ExitStack() as ctx:
            def sb1(name, shape, dt=F32):
                return ctx.enter_context(nc.sbuf_tensor(name, shape, dt))
            QT = sb1("QT", [P, DC, QW])
            bases = sb1("bases", [1, NG], I32)
            flag = sb1("flag", [P, NG])
            penc = sb1("penc", [P, NG])
            relT = sb1("relT", [P, NREL])
            with ExitStack() as c1:
                prepare(nc, c1, cst, io, dram, QT, bases, flag, penc, relT[:, :])
            with ExitStack() as c2:
                edge_pass(nc, c2, cst, QT, dram["kv"], dram["src"], dram["featx"], dram["featt"], dram["agg"],
                          bases, flag, penc, relT[:, :])
        with ExitStack() as ctx:
            after_edges(nc, ctx, cst, io, dram, slots, gap, rows, ints)
        with ExitStack() as ctx:
            experts(nc, ctx, cst, io, dram, rows)
        with ExitStack() as ctx:
            combine(nc, ctx, cst, dram, out, slots, gap)


INPUTS = dict(x="x", src="src", dst="dst", etype="edge_type_64", query="L0_gnn_query_emb", Wq="L0_gnn_Wq",
              bq="L0_gnn_bq", Wk="L0_gnn_Wk", bk="L0_gnn_bk", Wv="L0_gnn_Wv", bv="L0_gnn_bv", rel="L0_gnn_rel_w",
              Wo="L0_gnn_Wo", bo="L0_gnn_bo", gamma="L0_gnn_gamma", beta="L0_gnn_beta", Wr="L0_ffn_Wr",
              br="L0_ffn_br", ln_g="L0_ffn_ln_g", ln_b="L0_ffn_ln_b", W1="L0_ffn_W1", b1="L0_ffn_b1",
              W2="L0_ffn_W2", b2="L0_ffn_b2")


def kernel(**inputs):
    import numpy as _np
    import concourse.bacc as _bacc
    from concourse import mybir as _mybir
    from concourse.bass_utils import run_bass_kernel_spmd as _run

    nc = _bacc.Bacc("TRN2", target_bir_lowering=False, num_devices=1)
    arrays = {"in_consts": CONSTS}
    for short, name in INPUTS.items():
        arrays[f"in_{short}"] = _np.ascontiguousarray(inputs[name])
    io = {name[3:]: nc.dram_tensor(name, a.shape, _mybir.dt.from_np(a.dtype), kind="ExternalInput").ap()
          for name, a in arrays.items()}
    out = nc.dram_tensor("out_0", (N, D), F32, kind="ExternalOutput").ap()
    build(nc, io, out)
    r = _run(nc, [arrays], core_ids=[0])
    return r.results[0]["out_0"]
```

```python
from contextlib import ExitStack

import numpy as np

import concourse.bass as bass
from concourse import mybir
from concourse.alu_op_type import AluOpType as ALU

ACT = mybir.ActivationFunctionType
AX = mybir.AxisListType
F32 = mybir.dt.float32
BF16 = mybir.dt.bfloat16
I32 = mybir.dt.int32
U32 = mybir.dt.uint32

P = 128
N, D = 6250, 256
H, HD = 4, 64
DC = D // P
E = 200000
NREL = 64
W = P // H
TG = 6
G = TG * P
NG = -(-E // G)
GH = G // 2
CW = HD + 1
KVW = D + H * CW
GE = 125
GS = E // GE
NT = -(-N // P)
LAST = N - P
QW = N + W + 22
AR = 50 * P
RN = 7
NX, FF = 8, 1024
FC = FF // P
BT = 256
CAP = N + BT + 22
NB = (2 * N - NX) // BT + NX
BPE = -(-N // BT)
EPS = 1e-5
BIG = 1e30
FLOOR = -1e28
SCALE = HD ** -0.5


class Tile:

    def __init__(self, t, slot, rnd, live, first):
        self.t, self.slot, self.rnd, self.live, self.first = t, slot, rnd, live, first


def pipeline(eng, n, lo, hi, unroll, warm, step):
    def at(s_static, r, k, base):
        def T(off):
            if r is None:
                t = s_static - off
                return Tile(t, t % unroll, t // unroll, 0 <= t < n, t)
            c = base + k - off
            return Tile(r * unroll + c, c % unroll, r + c // unroll, True, c)
        return T
    loops = (n + lo - warm) // unroll if lo < 0 else (n - warm) // unroll
    for s in range(lo, warm):
        step(at(s, None, 0, 0))
    with eng.Fori(0, loops) as r:
        for k in range(unroll):
            step(at(None, r, k, warm))
    for s in range(warm + loops * unroll, n + hi):
        step(at(s, None, 0, 0))


def hold(eng, sem, value):
    eng.wait_ge(sem, value)
    eng.nop(nofuse=True)


def lay_constants():
    p = np.arange(P)
    q = np.arange(P)
    ident = np.eye(P, dtype=np.float32)
    first = (((q % W) == 0)[None, :] & ((p // W)[:, None] == (q // W)[None, :])).astype(np.float32)
    pen = np.zeros((P, P), np.float32)
    for r in range(W + 2):
        pen[NREL + r] = np.where((q % W) == r, 0.0, -BIG)
    match = np.zeros((P, 1), np.float32)
    match[:NREL, 0] = np.arange(NREL)
    match[NREL:NREL + W + 1, 0] = np.arange(W + 1)
    match[NREL + W + 1, 0] = -1
    inwin = (p % W).astype(np.float32)[:, None]
    isfirst = ((p % W) == 0).astype(np.float32)[:, None]
    before = (p[:, None] < q[None, :]).astype(np.float32)
    parts = dict(ident=ident, first=first, pen=pen, before=before, ones=np.ones((P, P), np.float32),
                 match=match, inwin=inwin, isfirst=isfirst,
                 eps=np.full((P, 1), EPS, np.float32),
                 iota8=np.tile(np.arange(NX, dtype=np.float32), (P, 1)),
                 rank8=np.tile(NX - np.arange(NX, dtype=np.float32), (P, 1)),
                 restart=np.tile((np.arange(NX * RN) % RN > 0).astype(np.float32), (P, 1)),
                 cap8=np.tile(np.arange(NX, dtype=np.float32) * CAP, (P, 1)),
                 lastrows=(p >= P - (N - (NT - 1) * P)).astype(np.float32)[:, None],
                 fills=np.tile(np.arange(BPE, dtype=np.float32) * BT, (P, 1)),
                 nospare=np.zeros((P, 2), np.float32),
                 spare=np.where((p < P - (N - (NT - 1) * P))[:, None], NX * CAP + p[:, None] + [0, P],
                                0).astype(np.float32),
                 steps=np.tile(np.arange(NB, dtype=np.float32), (P, 1)))
    at, cols = {}, 0
    for name, a in parts.items():
        at[name] = (cols, cols + a.shape[1])
        cols += a.shape[1]
    return np.concatenate(list(parts.values()), 1), at


CONSTS, CAT = lay_constants()


def edge_pass(nc, ctx, cst, QT, kv_dram, src_dram, featx_dram, feat_t_dram, agg_dram, bases, flag, penc, relT):
    def sb(name, shape, dt=F32):
        return ctx.enter_context(nc.sbuf_tensor(name, shape, dt))

    def sem(name):
        return ctx.enter_context(nc.semaphore(name))

    R = 3
    NR = NREL + W + 2
    idx = [sb(f"e_idx{i}", [P, TG], I32) for i in range(R)]
    rows = [sb(f"e_rows{i}", [P, G], BF16) for i in range(R)]
    kv = [sb(f"e_kv{i}", [P, TG, KVW]) for i in range(R)]
    onehot = [sb(f"e_onehot{i}", [P, G]) for i in range(R)]
    qblock = [sb(f"e_qblock{i}", [P, DC, P]) for i in range(R)]
    qrel = [sb(f"e_qrel{i}", [P, P]) for i in range(R)]
    prob = [sb(f"e_prob{i}", [P, G]) for i in range(R)]
    probT = [sb(f"e_probT{i}", [P, TG, P]) for i in range(R)]
    carry = [sb(f"e_carry{i}", [P, P]) for i in range(R)]
    acc = [sb(f"e_acc{i}", [P, CW]) for i in range(R)]
    carried = [sb(f"e_carried{i}", [P, CW]) for i in range(R)]
    small = [sb(f"e_small{i}", [P, 8]) for i in range(R)]
    kT = sb("e_kT", [P, DC, G])
    psK = ctx.enter_context(nc.psum_tensor("psK", [P, 2, 512], F32))
    psD = ctx.enter_context(nc.psum_tensor("psD", [P, 2, 512], F32))
    psP = ctx.enter_context(nc.psum_tensor("psP", [P, 2, 512], F32))
    psA = ctx.enter_context(nc.psum_tensor("psA", [P, 512], F32))
    psX = ctx.enter_context(nc.psum_tensor("psX", [P, 512], F32))
    MX, MC, MM, NM, AL = (slice(i, i + 1) for i in range(5))

    ident = cst("ident")
    s_idx = [sem(f"es_idx{i}") for i in range(R)]
    s_rows = [sem(f"es_rows{i}") for i in range(R)]
    s_kv = [sem(f"es_kv{i}") for i in range(R)]
    s_out = [sem(f"es_out{i}") for i in range(R)]
    s_init = sem("es_init")
    s_qb = sem("es_qb")
    s_exp = sem("es_exp")
    s_pT = sem("es_pT")
    s_cas = sem("es_cas")
    s_m = sem("es_m")
    s_carry = sem("es_carry")
    s_oh = sem("es_oh")
    s_kTv = sem("es_kTv")
    s_kTa = sem("es_kTa")
    s_x = sem("es_x")
    s_acc = sem("es_acc")
    s_d = sem("es_d")
    s_pp = sem("es_pp")
    s_agg = sem("es_agg")
    s_pk = sem("es_pk")
    s_px = sem("es_px")

    LO, HI, WARM = -1, 2, 6

    with nc.Block() as blk:
        @blk.sync
        def _(sp):
            def step(T):
                g = T(0)
                if g.live:
                    if g.first >= R:
                        hold(sp, s_kv[g.slot], g.rnd * (16 * TG))
                    sp.dma_start(idx[g.slot][:, :], src_dram[bass.ds(g.t, 1)].rearrange("a (p t) -> (a p) t", t=TG)
                                 ).then_inc(s_idx[g.slot], 16)
                    if g.first >= R:
                        hold(sp, s_oh, g.t - (R - 1))
                    sp.dma_start(rows[g.slot][0:NREL, :],
                                 feat_t_dram[bass.ds(g.t, 1)].to_broadcast([NREL, G])).then_inc(s_rows[g.slot], 16)
                    sp.dma_start(rows[g.slot][NREL:NR, :],
                                 featx_dram[bass.ds(g.t, 1)].to_broadcast([W + 2, G])).then_inc(s_rows[g.slot], 16)
                o = T(5)
                if o.live:
                    base = sp.value_load(bases[0:1, bass.ds(o.t, 1)], min_val=0, max_val=N - 1)
                    if o.first >= 1:
                        b = T(6)
                        hold(sp, s_out[b.slot], (b.rnd + 1) * (16 * H))
                    hold(sp, s_acc, o.t + 1)
                    for h in range(H):
                        sp.dma_start(agg_dram[bass.ds(base, W), h, :], acc[o.slot][h * W:(h + 1) * W, :]
                                     ).then_inc(s_out[o.slot], 16)
            pipeline(sp, NG, 0, 6, R, WARM, step)
            for i in range(R):
                sp.wait_ge(s_out[i], (NG // R) * 16 * H)

        @blk.gpsimd
        def _(pool):
            def step(T):
                g = T(0)
                if g.live:
                    if g.first >= R:
                        pool.wait_ge(s_agg, g.t - (R - 1))
                    hold(pool, s_idx[g.slot], (g.rnd + 1) * 16)
                    for t in range(TG):
                        pool.indirect_dma_start(
                            out=kv[g.slot][:, t, :], out_offset=None, in_=kv_dram[:, :],
                            in_offset=bass.IndirectOffsetOnAxis(ap=idx[g.slot][:, t:t + 1], axis=0),
                        ).then_inc(s_kv[g.slot], 16)
            pipeline(pool, NG, 0, 0, R, WARM, step)

        @blk.scalar
        def _(act):
            act.preload_act_table(ACT.Exp)
            act.wait_ge(s_init, 3)

            def step(T):
                a = T(-1)
                if a.live:
                    base = act.value_load(bases[0:1, bass.ds(a.t, 1)], min_val=0, max_val=N - 1)
                    if a.first >= R:
                        hold(act, s_d, a.t - (R - 1))
                    for b in range(2):
                        act.copy(
                            qblock[a.slot][b * HD:(b + 1) * HD, :, :].rearrange(
                                "p a (h w) -> p a h w", w=W)[:, 0, b, :],
                            QT[b * HD:(b + 1) * HD, 0, bass.ds(base, W)])
                        act.copy(
                            qblock[a.slot][b * HD:(b + 1) * HD, :, :].rearrange(
                                "p a (h w) -> p a h w", w=W)[:, 1, 2 + b, :],
                            QT[b * HD:(b + 1) * HD, 1, bass.ds(base, W)]).then_inc(s_qb, 1)
                g, c = T(0), T(1)
                if g.live:
                    act.wait_ge(s_m, g.t * 3 + 3)
                    if g.first >= R:
                        act.wait_ge(s_pp, g.t * 2 - 2 * (R - 1))
                    act.activation(prob[g.slot][:, :].rearrange("p (c q) -> p c q", c=2), psD[:, :, 0:GH], ACT.Exp,
                                   bias=small[g.slot][:, NM], scale=SCALE).then_inc(s_exp, 1)
                    act.activation(small[g.slot][:, AL], small[g.slot][:, MC], ACT.Exp,
                                   bias=small[g.slot][:, NM], scale=SCALE).then_inc(s_exp, 1)
                if a.live:
                    if a.first >= 1:
                        act.wait_ge(s_d, a.t)
                    for j in range(2):
                        act.wait_ge(s_pk, a.t * 4 + 2 * j + 2)
                        act.copy(kT[:, 1, j * GH:(j + 1) * GH], psK[:, 1, 0:GH]).then_inc(s_kTa, 1)
                if c.live:
                    act.wait_ge(s_exp, c.t * 2 + 2)
                    act.wait_ge(s_agg, c.t + 1)
                    act.activation(carried[c.slot][:, :], psA[:, P:P + CW], ACT.Copy,
                                   scale=small[c.slot][:, AL]).then_inc(s_cas, 1)
                if g.live:
                    if g.first >= R:
                        act.wait_ge(s_agg, g.t - (R - 1))
                    for j, (lo, hi) in enumerate(((0, 4), (4, TG))):
                        act.wait_ge(s_pp, g.t * 2 + j + 1)
                        act.copy(probT[g.slot][:, lo:hi, :].rearrange("p t q -> p (t q)"),
                                 psP[:, j, 0:(hi - lo) * P]).then_inc(s_pT, 1)
            pipeline(act, NG, LO, HI, R, WARM, step)

        @blk.vector
        def _(dve):
            for i in range(R):
                dve.memset(qblock[i][:, :, :], 0.0)
                dve.tensor_copy(qrel[i][:, :], cst("pen"))
            dve.memset(acc[R - 1][:, :], 0.0).then_inc(s_init, 1)
            dve.memset(small[R - 1][:, :], 0.0).then_inc(s_init, 1)
            dve.memset(prob[0][:, 0:1], 0.0).then_inc(s_init, 1)
            dve.wait_ge(s_init, 3)

            def step(T):
                g = T(0)
                if g.live:
                    sm = small[g.slot]
                    dve.wait_ge(s_d, g.t + 1)
                    dve.tensor_reduce(sm[:, MX], psD[:, :, 0:GH], AX.XY, ALU.max).then_inc(s_m, 1)
                    dve.wait_ge(s_m, g.t * 3 + 1)
                    dve.wait_ge(s_x, g.t * 2 + 2)
                    dve.scalar_tensor_tensor(out=sm[:, MM], in0=sm[:, MX], scalar=FLOOR, in1=sm[:, MC],
                                             op0=ALU.max, op1=ALU.max).then_inc(s_m, 1)
                    dve.wait_ge(s_m, g.t * 3 + 2)
                    dve.tensor_scalar(sm[:, NM], sm[:, MM], -SCALE, None, ALU.mult).then_inc(s_m, 1)
                a = T(-1)
                if a.live:
                    if a.first >= R:
                        dve.wait_ge(s_agg, a.t - (R - 1))
                    dve.tensor_scalar(carry[a.slot][:, :], cst("first"), flag[:, bass.ds(a.t, 1)], None,
                                      ALU.mult).then_inc(s_carry, 1)
                    dve.wait_ge(s_rows[a.slot], (a.rnd + 1) * 32)
                    if a.first >= R:
                        dve.wait_ge(s_d, a.t - (R - 1))
                    dve.tensor_scalar(onehot[a.slot][0:NR, :], rows[a.slot][0:NR, :], cst("match")[0:NR, :], None,
                                      ALU.is_equal).then_inc(s_oh, 1)
                if a.live:
                    if a.first >= 1:
                        dve.wait_ge(s_d, a.t)
                    for j in range(2):
                        dve.wait_ge(s_pk, a.t * 4 + 2 * j + 1)
                        dve.tensor_copy(kT[:, 0, j * GH:(j + 1) * GH], psK[:, 0, 0:GH]).then_inc(s_kTv, 1)
                    dve.wait_ge(s_px, a.t + 1)
                    dve.tensor_copy(qrel[a.slot][0:NREL, :], psX[0:NREL, P:2 * P]).then_inc(s_x, 1)
                    dve.tensor_tensor(small[a.slot][:, MC], psX[:, 0:1], penc[:, bass.ds(a.t, 1)],
                                      ALU.add).then_inc(s_x, 1)
                c = T(1)
                if c.live:
                    dve.wait_ge(s_cas, c.t + 1)
                    if c.first >= R:
                        dve.wait_ge(s_out[c.slot], c.rnd * (16 * H))
                    dve.tensor_tensor(acc[c.slot][:, :], psA[:, 0:CW], carried[c.slot][:, :],
                                      ALU.add).then_inc(s_acc, 1)
            pipeline(dve, NG, LO, HI, R, WARM, step)

        @blk.tensor
        def _(pe):
            pe.wait_ge(s_init, 3)
            halves = [slice(a * P // DC, (a + 1) * P // DC) for a in range(DC)]

            def step(T):
                g = T(0)
                if g.live:
                    pe.wait_ge(s_x, g.t * 2 + 1)
                    pe.wait_ge(s_oh, g.t + 1)
                    if g.first >= 1:
                        pe.wait_ge(s_exp, g.t * 2 - 1)
                    for c in range(2):
                        cols = slice(c * GH, (c + 1) * GH)
                        for half in halves:
                            pe.matmul(psD[half, c, 0:GH], qrel[g.slot][0:NR, half], onehot[g.slot][0:NR, cols],
                                      start=True, stop=False, tile_position=(0, half.start))
                        pe.wait_ge(s_kTv, g.t * 2 + c + 1)
                        pe.wait_ge(s_kTa, g.t * 2 + c + 1)
                        for a, half in enumerate(halves):
                            mm = pe.matmul(psD[half, c, 0:GH], qblock[g.slot][:, a, half], kT[:, a, cols],
                                           start=False, stop=True, tile_position=(0, half.start))
                    mm.then_inc(s_d, 1)
                c = T(1)
                if c.live:
                    prev = (c.slot - 1) % R
                    if c.first >= 1:
                        pe.wait_ge(s_acc, c.t)
                    pe.wait_ge(s_carry, c.t + 1)
                    pe.matmul(psA[:, P:P + CW], carry[c.slot][:, :], acc[prev][:, :], start=True, stop=True)
                    for j, (lo, hi) in enumerate(((0, 4), (4, TG))):
                        pe.wait_ge(s_pT, c.t * 2 + j + 1)
                        for t in range(lo, hi):
                            for h in range(H):
                                mm = pe.matmul(psA[h * W:(h + 1) * W, 0:CW], probT[c.slot][:, t, h * W:(h + 1) * W],
                                               kv[c.slot][:, t, D + h * CW:D + (h + 1) * CW],
                                               start=t == 0, stop=t == TG - 1, tile_position=(0, h * W))
                    mm.then_inc(s_agg, 1)
                a = T(-1)
                if a.live:
                    pe.wait_ge(s_kv[a.slot], (a.rnd + 1) * (16 * TG))
                    for j in range(4):
                        half, third = j % 2, j // 2
                        if a.first >= 1 or j >= 2:
                            pe.wait_ge(s_kTa if half else s_kTv, a.t * 2 + third)
                        for t in range(3):
                            mm = pe.transpose(psK[:, half, t * P:(t + 1) * P],
                                              kv[a.slot][:, third * 3 + t, half * P:(half + 1) * P], ident)
                        mm.then_inc(s_pk, 1)
                    if a.first >= 1:
                        pe.wait_ge(s_m, a.t * 3 - 1)
                        pe.wait_ge(s_x, a.t * 2)
                    pe.wait_ge(s_carry, a.t + 1)
                    pe.matmul(psX[:, 0:1], carry[a.slot][:, :], small[(a.slot - 1) % R][:, MM], start=True, stop=True)
                    pe.wait_ge(s_qb, a.t * 2 + 2)
                    for b in range(DC):
                        mm = pe.matmul(psX[0:NREL, P:2 * P], relT, qblock[a.slot][:, b, :],
                                       start=b == 0, stop=b == DC - 1)
                    mm.then_inc(s_px, 1)
                if g.live:
                    pe.wait_ge(s_exp, g.t * 2 + 1)
                    for j, (lo, hi) in enumerate(((0, 4), (4, TG))):
                        if g.first >= 1:
                            pe.wait_ge(s_pT, g.t * 2 + j - 1)
                        for t in range(lo, hi):
                            mm = pe.transpose(psP[:, j, (t - lo) * P:(t - lo + 1) * P],
                                              prob[g.slot][:, t * P:(t + 1) * P], ident)
                        mm.then_inc(s_pp, 1)
            pipeline(pe, NG, LO, HI, R, WARM, step)


def node_rows(t):
    return min(t * P, LAST) if isinstance(t, int) else t * P


def own_rows(t):
    lo = NT * P - N if isinstance(t, int) and t == NT - 1 else 0
    return lo, bass.ds(node_rows(t) + lo, P - lo)


def prepare(nc, ctx, cst, io, dram, QT, bases, flag, penc, relT, unfit):
    def sb(name, shape, dt=F32):
        return ctx.enter_context(nc.sbuf_tensor(name, shape, dt))

    def sem(name):
        return ctx.enter_context(nc.semaphore(name))

    R = 2
    xin = [sb(f"p_x{i}", [P, D]) for i in range(R)]
    xn = [sb(f"p_xn{i}", [P, D]) for i in range(R)]
    xnb = [sb(f"p_xnb{i}", [P, D]) for i in range(R)]
    enh = [sb(f"p_enh{i}", [P, D]) for i in range(R)]
    enhT = [sb(f"p_enhT{i}", [P, DC, P]) for i in range(R)]
    qrow = [sb(f"p_q{i}", [P, D]) for i in range(R)]
    kvrow = [sb(f"p_kv{i}", [P, KVW]) for i in range(R)]
    stat = [sb(f"p_stat{i}", [P, 12]) for i in range(R)]
    wkv = sb("p_wkv", [P, DC, 2 * D])
    wq = sb("p_wq", [P, DC, D])
    bias = sb("p_bias", [P, 4, D])
    qe = sb("p_qe", [P, D])
    qe01 = sb("p_qe01", [P, D])
    relraw = sb("p_relraw", [NREL, 2 * HD])
    edge = [sb(f"p_edge{i}", [P, G], I32) for i in range(2)]
    epos = sb("p_epos", [P, G])
    epos2 = sb("p_epos2", [P, G])
    feat = [sb(f"p_feat{i}", [P, G], BF16) for i in range(2)]
    zero = sb("p_zero", [P, 5 * H * CW])
    basef = sb("p_basef", [P, NG])
    baseall = sb("p_baseall", [P, NG])
    delta = sb("p_delta", [P, NG])
    seq = sb("p_seq", [P, E // GE + 1], I32)
    drop = sb("p_drop", [P, E // GE])
    place = sb("p_place", [P, G])
    misfit = sb("p_misfit", [P, 4])
    misfits = sb("p_misfits", [P, 2])
    psT = ctx.enter_context(nc.psum_tensor("p_psT", [P, 512], F32))
    psKV = [ctx.enter_context(nc.psum_tensor(f"p_psKV{i}", [P, 512], F32)) for i in range(R)]
    psQ = [ctx.enter_context(nc.psum_tensor(f"p_psQ{i}", [P, 512], F32)) for i in range(R)]
    psQT = ctx.enter_context(nc.psum_tensor("p_psQT", [P, 512], F32))
    ident = cst("ident")

    s_w = sem("ps_w")
    s_e = [sem(f"ps_e{i}") for i in range(2)]
    s_f = sem("ps_f")
    s_z = sem("ps_z")
    s_set = sem("ps_set")
    s_zero = sem("ps_zero")
    s_seq = sem("ps_seq")
    s_pb = sem("ps_pb")
    s_x = [sem(f"ps_x{i}") for i in range(R)]
    s_st = [sem(f"ps_st{i}") for i in range(R)]
    s_ln = sem("ps_ln")
    s_xb = sem("ps_xb")
    s_sd = sem("ps_sd")
    s_eT = sem("ps_eT")
    s_qT = sem("ps_qT")
    s_ev = sem("ps_ev")
    s_t = sem("ps_t")
    s_mm = sem("ps_mm")
    s_tq = sem("ps_tq")

    chunks = [(c * P, min(NG - c * P, P)) for c in range(-(-NG // P))]
    full, tail = divmod(E, G)
    NSRC = NG * G

    with nc.Block() as blk:
        @blk.sync
        def _(sp):
            for a in range(DC):
                rowsl = slice(a * P, (a + 1) * P)
                sp.dma_start(wkv[:, a, 0:D], io["Wk"][rowsl, :]).then_inc(s_w, 16)
                sp.dma_start(wkv[:, a, D:2 * D], io["Wv"][rowsl, :]).then_inc(s_w, 16)
                sp.dma_start(wq[:, a, :], io["Wq"][rowsl, :]).then_inc(s_w, 16)
            for j, name in enumerate(("bq", "bk", "bv", "bo")):
                sp.dma_start(bias[:, j, :], io[name].rearrange("(a d) -> a d", a=1).to_broadcast([P, D])
                             ).then_inc(s_w, 16)
            sp.dma_start(qe[:, :], io["query"].rearrange("(a d) -> a d", a=1).to_broadcast([P, D])
                         ).then_inc(s_w, 16)
            for b in range(2):
                sp.dma_start(relraw[:, b * HD:(b + 1) * HD], io["rel"]).then_inc(s_w, 16)
            with nc.allow_non_contiguous_dma("the first edge's node of each group"):
                sp.dma_start(bases[0:1, :], io["dst"].rearrange("(a e) -> a e", a=1)[:, 0:E:G]).then_inc(s_w, 16)

            def step(T):
                g = T(0)
                if g.live:
                    r0 = node_rows(g.t)
                    if g.first >= R:
                        hold(sp, s_ln, g.t * 5 - 5 * (R - 1) - 1)
                    sp.dma_start(xin[g.slot][:, :], io["x"][bass.ds(r0, P), :]).then_inc(s_x[g.slot], 16)
                o = T(2)
                if o.live:
                    lo, r = own_rows(o.t)
                    hold(sp, s_xb, o.t + 1)
                    sp.dma_start(dram["xn"][r, :], xnb[o.slot][lo:P, :]).then_inc(s_st[o.slot], 16)
                    hold(sp, s_ev, o.t * 3 + 3)
                    sp.dma_start(dram["kv"][r, :], kvrow[o.slot][lo:P, :]).then_inc(s_st[o.slot], 16)
            pipeline(sp, NT, 0, 2, R, 4, step)
            for i in range(R):
                sp.wait_ge(s_st[i], 32 * len(range(i, NT, R)))
            sp.wait_ge(s_f, 32 * len(chunks))
            sp.wait_ge(s_z, 16 * (10 + 2 + 2))

        @blk.gpsimd
        def _(pool):
            pool.memset(zero[:, :], 0.0).then_inc(s_zero, 1)
            for c, (g0, n) in enumerate(chunks):
                whole = min(n, full - g0)
                for j, name in enumerate(("dst", "etype")):
                    if whole < n:
                        pool.memset(edge[j][:, :], 0 if j else 1000000).then_inc(s_zero, 1)
                        pool.wait_ge(s_zero, 2 + j)
                    pool.dma_start(edge[j][0:whole, :],
                                   io[name][g0 * G:(g0 + whole) * G].rearrange("(g e) -> g e", e=G)
                                   ).then_inc(s_e[j], 16)
                    if whole < n:
                        pool.dma_start(edge[j][whole:n, 0:tail],
                                       io[name][full * G:E].rearrange("(a e) -> a e", a=1)).then_inc(s_e[j], 16)
                pool.wait_ge(s_set, 3 + 6 * (c + 1))
                pool.dma_start(dram["featx"][g0:g0 + n, :], feat[0][0:n, :]).then_inc(s_f, 16)
                pool.dma_start(dram["featt"][g0:g0 + n, :], feat[1][0:n, :]).then_inc(s_f, 16)
            pool.dma_start(seq[0:GE, 0:E // GE], io["dst"].rearrange("(p e) -> p e", p=GE)).then_inc(s_seq, 16)
            with nc.allow_non_contiguous_dma("the first of the next partition"):
                pool.dma_start(seq[0:GE - 1, E // GE:], io["dst"].rearrange("(p e) -> p e", p=GE)[1:GE, 0:1]
                               ).then_inc(s_seq, 16)
                pool.dma_start(seq[GE - 1:GE, E // GE:], io["dst"].rearrange("(p e) -> p e", p=GE)[
                    GE - 1:GE, E // GE - 1:E // GE]).then_inc(s_seq, 16)
            pool.wait_ge(s_zero, 1)
            pool.dma_start(dram["src"].rearrange("g e -> (g e)")[0:E].rearrange("(a b) -> a b", b=1250),
                           io["src"].rearrange("(a b) -> a b", b=1250)).then_inc(s_z, 16)
            pool.dma_start(dram["src"].rearrange("g e -> (g e)")[E:NSRC].rearrange("(a b) -> a b", a=1),
                           zero[0:1, 0:NSRC - E].bitcast(I32)).then_inc(s_z, 16)
            for j in range(10):
                pool.dma_start(dram["agg"][j * 5 * P:(j + 1) * 5 * P].rearrange("(p a) h c -> p (a h c)", a=5),
                               zero[:, :]).then_inc(s_z, 16)
            for j in range(2):
                pool.dma_start(dram["xs"][NX * CAP + 2 * P * j:NX * CAP + 2 * P * (j + 1)].rearrange(
                    "(p a) c -> p (a c)", a=2), zero[:, 0:2 * D]).then_inc(s_z, 16)

            def step(T):
                g = T(0)
                pool.wait_ge(s_ln, g.t * 5 + 4)
                if g.first >= R:
                    pool.wait_ge(s_st[g.slot], g.rnd * 32)
                pool.tensor_tensor(xnb[g.slot][:, :], xn[g.slot][:, :], bias[:, 3, :], ALU.add).then_inc(s_xb, 1)
            pool.wait_ge(s_w, 16 * 14)
            pipeline(pool, NT, 0, 0, R, 4, step)

        @blk.scalar
        def _(act):
            act.preload_act_table(ACT.Sqrt)

            def step(T):
                g = T(0)
                if g.live:
                    act.wait_ge(s_ln, g.t * 5 + 2)
                    act.activation(stat[g.slot][:, 8:9], stat[g.slot][:, 7:8], ACT.Sqrt, bias=cst("eps")
                                   ).then_inc(s_sd, 1)
                    act.wait_ge(s_t, g.t + 1)
                    act.copy(enhT[g.slot][:, :, :].rearrange("p a q -> p (a q)"), psT[:, 0:D]).then_inc(s_eT, 1)
                c = T(1)
                if c.live:
                    act.wait_ge(s_tq, c.t + 1)
                    act.copy(QT[:, :, bass.ds(node_rows(c.t), P)],
                             psQT[:, 0:D].rearrange("p (a q) -> p a q", a=DC)).then_inc(s_qT, 1)
            pipeline(act, NT, 0, 1, R, 4, step)

        @blk.vector
        def _(dve):
            count = [0]

            def link(ins):
                count[0] += 1
                ins.then_inc(s_set, 1)
                dve.wait_ge(s_set, count[0])

            dve.memset(QT[:, :, N:QW], 0.0)
            for i in range(R):
                dve.memset(kvrow[i][:, :], 1.0)
            dve.wait_ge(s_w, 16 * 14)
            link(dve.tensor_scalar(qe01[:, :], qe[:, :], 0.1, None, ALU.mult))
            link(dve.tensor_copy(basef[0:1, :], bases[0:1, :]))
            link(dve.memset(misfit[:, :], 0.0))
            for c, (g0, n) in enumerate(chunks):
                dmas = c + 1 + (g0 + n > full)
                for j in range(2):
                    dve.wait_ge(s_e[j], 16 * dmas)
                link(dve.tensor_copy(epos[0:n, :], edge[0][0:n, :]))
                link(dve.tensor_scalar(epos2[0:n, :], epos[0:n, :], epos[0:n, 0:1], float(W),
                                       ALU.subtract, ALU.min))
                link(dve.scalar_tensor_tensor(out=place[0:n, :], in0=epos[0:n, :], scalar=float(N), in1=epos2[0:n, :],
                                              op0=ALU.is_lt, op1=ALU.mult))
                link(dve.tensor_reduce(misfit[0:n, c:c + 1], place[0:n, :], AX.X, ALU.max))
                if c:
                    dve.wait_ge(s_f, 32 * c)
                link(dve.tensor_scalar(feat[0][0:n, :].rearrange("g (t p) -> g t p", t=TG),
                                       epos2[0:n, :].rearrange("g (p t) -> g t p", t=TG), -1.0, None, ALU.max))
                link(dve.tensor_copy(feat[1][0:n, :].rearrange("g (t p) -> g t p", t=TG),
                                     edge[1][0:n, :].rearrange("g (p t) -> g t p", t=TG)))
            dve.wait_ge(s_pb, 2)
            link(dve.tensor_scalar(misfit[:, 0:3], misfit[:, 0:3], float(W), None, ALU.is_ge))
            dve.wait_ge(s_seq, 48)
            link(dve.tensor_tensor(drop[0:GE, :], seq[0:GE, 1:], seq[0:GE, 0:E // GE], ALU.is_lt))
            link(dve.tensor_reduce(misfit[0:GE, 3:4], drop[0:GE, :], AX.X, ALU.max))
            link(dve.tensor_reduce(misfits[:, 0:1], misfit[:, :], AX.X, ALU.add))
            link(dve.tensor_scalar(relT, psQT[:, 0:NREL], 0.2, None, ALU.mult))
            link(dve.tensor_copy(baseall[:, :], psT[:, 0:NG]))
            dve.wait_ge(s_pb, 3)
            link(dve.tensor_copy(misfits[0:1, 1:2], psKV[0][0:1, 0:1]))
            link(dve.tensor_scalar(unfit[0:1, :], misfits[0:1, 1:2], 1.0, None, ALU.min))
            link(dve.memset(flag[:, 0:1], 0.0))
            link(dve.memset(penc[:, 0:1], -BIG))
            link(dve.tensor_tensor(delta[:, 1:NG], baseall[:, 1:NG], baseall[:, 0:NG - 1], ALU.subtract))
            link(dve.tensor_scalar(flag[:, 1:NG], delta[:, 1:NG], cst("inwin"), None, ALU.is_equal))
            link(dve.tensor_scalar(basef[:, 1:NG], delta[:, 1:NG], float(W), cst("isfirst"), ALU.is_lt, ALU.mult))
            link(dve.tensor_scalar(penc[:, 1:NG], basef[:, 1:NG], -1.0, BIG, ALU.add, ALU.mult))

            def step(T):
                g = T(0)
                if g.live:
                    st = stat[g.slot]
                    dve.wait_ge(s_x[g.slot], (g.rnd + 1) * 16)
                    dve.bn_stats(st[:, 0:6], xin[g.slot][:, :]).then_inc(s_ln, 1)
                    hold(dve, s_ln, g.t * 5 + 1)
                    dve.bn_aggr(st[:, 6:8], st[:, 0:6]).then_inc(s_ln, 1)
                c = T(1)
                if c.live:
                    dve.wait_ge(s_mm, c.t + 1)
                    if c.first >= R:
                        dve.wait_ge(s_st[c.slot], c.rnd * 32)
                    kvr = kvrow[c.slot]
                    dve.tensor_tensor(kvr[:, 0:D], psKV[c.slot][:, 0:D], bias[:, 1, :], ALU.add).then_inc(s_ev, 1)
                    dve.tensor_tensor(kvr[:, D:KVW].rearrange("p (h c) -> p h c", h=H)[:, :, 0:HD],
                                      psKV[c.slot][:, D:2 * D].rearrange("p (h c) -> p h c", h=H),
                                      bias[:, 2, :].rearrange("p (h c) -> p h c", h=H), ALU.add).then_inc(s_ev, 1)
                    if c.first >= R:
                        dve.wait_ge(s_tq, c.t - (R - 1))
                    dve.tensor_tensor(qrow[c.slot][:, :], psQ[c.slot][:, 0:D], bias[:, 0, :], ALU.add
                                      ).then_inc(s_ev, 1)
                if g.live:
                    dve.wait_ge(s_sd, g.t + 1)
                    dve.reciprocal(st[:, 9:10], st[:, 8:9]).then_inc(s_ln, 1)
                    dve.wait_ge(s_ln, g.t * 5 + 3)
                    if g.first >= R:
                        dve.wait_ge(s_xb, g.t - (R - 1))
                    dve.tensor_scalar(xn[g.slot][:, :], xin[g.slot][:, :], st[:, 6:7], st[:, 9:10],
                                      ALU.subtract, ALU.mult).then_inc(s_ln, 1)
                    dve.wait_ge(s_ln, g.t * 5 + 4)
                    if g.first >= R:
                        dve.wait_ge(s_t, g.t - (R - 1))
                    dve.tensor_tensor(enh[g.slot][:, :], xn[g.slot][:, :], qe01[:, :], ALU.add).then_inc(s_ln, 1)
            pipeline(dve, NT, 0, 1, R, 4, step)

        @blk.tensor
        def _(pe):
            pe.wait_ge(s_w, 16 * 14)
            pe.transpose(psQT[:, 0:NREL], relraw[:, :], ident[0:NREL, 0:NREL]).then_inc(s_pb, 1)
            pe.wait_ge(s_set, 2)
            pe.matmul(psT[:, 0:NG], cst("ones")[0:1, :], basef[0:1, :], start=True, stop=True).then_inc(s_pb, 1)
            pe.wait_ge(s_set, 3 + 6 * len(chunks) + 4)
            pe.matmul(psKV[0][0:1, 0:1], misfits[:, 0:1], cst("ones")[:, 0:1], start=True, stop=True
                      ).then_inc(s_pb, 1)
            pe.wait_ge(s_set, 3 + 6 * len(chunks) + 8)

            def step(T):
                g = T(0)
                if g.live:
                    pe.wait_ge(s_ln, g.t * 5 + 5)
                    if g.first >= 1:
                        pe.wait_ge(s_eT, g.t)
                    for a in range(DC):
                        mm = pe.transpose(psT[:, a * P:(a + 1) * P], enh[g.slot][:, a * P:(a + 1) * P], ident)
                    mm.then_inc(s_t, 1)
                c = T(1)
                if c.live:
                    pe.wait_ge(s_ev, c.t * 3 + 3)
                    if c.first >= 1:
                        pe.wait_ge(s_qT, c.t)
                    for a in range(DC):
                        mm = pe.transpose(psQT[:, a * P:(a + 1) * P], qrow[c.slot][:, a * P:(a + 1) * P], ident)
                    mm.then_inc(s_tq, 1)
                if g.live:
                    pe.wait_ge(s_eT, g.t + 1)
                    if g.first >= R:
                        pe.wait_ge(s_ev, g.t * 3 - 3 * (R - 1))
                    for a in range(DC):
                        pe.matmul(psKV[g.slot][:, :], enhT[g.slot][:, a, :], wkv[:, a, :],
                                  start=a == 0, stop=a == DC - 1)
                    for a in range(DC):
                        mm = pe.matmul(psQ[g.slot][:, 0:D], enhT[g.slot][:, a, :], wq[:, a, :],
                                       start=a == 0, stop=a == DC - 1)
                    mm.then_inc(s_mm, 1)
            pipeline(pe, NT, 0, 1, R, 4, step)


def start_over(nc, counters):
    nums = [c.num for c in counters]
    assert nums == list(range(nums[0], nums[0] + len(nums)))
    own = range(nums[0], nums[-1] + 1)
    nc.gpsimd.dma_reset(own)
    nc.all_engine_barrier(sems_to_clear=own)


def any_order_pass(nc, ctx, cst, io, dram, QT):
    def sb(name, shape, dt=F32):
        return ctx.enter_context(nc.sbuf_tensor(name, shape, dt))

    qrows = sb("g_qrows", [P, D])
    floor = sb("g_floor", [P, N * H // GE])
    zero = sb("g_zero", [P, 5 * H * CW])
    ends = sb("g_ends", [P, 3], I32)
    others_i = sb("g_others_i", [P, GE], I32)
    others = sb("g_others", [P, GE])
    own = sb("g_own", [P, 1])
    same = sb("g_same", [P, GE])
    far = sb("g_far", [P, GE])
    q = sb("g_q", [P, D])
    kv = sb("g_kv", [P, KVW])
    rel = sb("g_rel", [P, HD])
    keys = sb("g_keys", [P, D])
    prod = sb("g_prod", [P, D])
    score = sb("g_score", [P, H])
    spread = sb("g_spread", [P, H, GE])
    masked = sb("g_masked", [P, H, GE])
    best = sb("g_best", [P, 3, H])
    diff = sb("g_diff", [P, 2, H])
    factor = sb("g_factor", [P, 2, H])
    weighted = sb("g_weighted", [P, H * CW])
    old = sb("g_old", [P, H * CW])
    kept = sb("g_kept", [P, H * CW])
    new = sb("g_new", [P, H * CW])
    psB = ctx.enter_context(nc.psum_tensor("g_psB", [P, 512], F32))
    psS = ctx.enter_context(nc.psum_tensor("g_psS", [P, 512], F32))
    ident = cst("ident")
    heads = lambda a: a.rearrange("p (h c) -> p h c", h=H)

    nc.all_engine_barrier()
    with ExitStack() as c:
        laid, stored = c.enter_context(nc.semaphore("g_laid")), c.enter_context(nc.semaphore("g_stored"))
        with nc.Block() as blk:
            @blk.vector
            def _(dve):
                dve.memset(zero[:, :], 0.0).then_inc(laid, 1)
                dve.memset(floor[:, :], FLOOR).then_inc(laid, 1)

            @blk.sync
            def _(sp):
                sp.wait_ge(laid, 2)
                for j in range(10):
                    sp.dma_start(dram["agg"][j * 5 * P:(j + 1) * 5 * P].rearrange("(p a) h c -> p (a h c)", a=5),
                                 zero[:, :]).then_inc(stored, 16)
                sp.dma_start(dram["best"].rearrange("(p a) h -> p (a h)", p=GE), floor[0:GE, :]).then_inc(stored, 16)
                sp.wait_ge(stored, 16 * 11)

    with ExitStack() as c:
        turned, copied, stored = counters = [c.enter_context(nc.semaphore(f"g_q{n}")) for n in
                                             ("turned", "copied", "stored")]
        with nc.Fori(0, N // GE) as t:
            with nc.Block() as blk:
                @blk.vector
                def _(dve):
                    for a in range(DC):
                        dve.tensor_copy(prod[:, a * GE:(a + 1) * GE], QT[:, a, bass.ds(t * GE, GE)]).then_inc(copied, 1)
                    dve.wait_ge(turned, 1)
                    dve.tensor_copy(qrows[0:GE, :], psB[0:GE, 0:D]).then_inc(copied, 1)

                @blk.tensor
                def _(pe):
                    pe.wait_ge(copied, DC)
                    for a in range(DC):
                        mm = pe.transpose(psB[0:GE, a * P:(a + 1) * P], prod[:, a * GE:(a + 1) * GE], ident)
                    mm.then_inc(turned, 1)

                @blk.sync
                def _(sp):
                    sp.wait_ge(copied, DC + 1)
                    sp.dma_start(dram["q"][bass.ds(t * GE, GE), :], qrows[0:GE, :]).then_inc(stored, 16)
                    sp.wait_ge(stored, 16)
            start_over(nc, counters)

    with ExitStack() as c:
        loaded, gathered, stepped, weighed, summed, written = counters = [
            c.enter_context(nc.semaphore(f"g_{n}")) for n in
            ("loaded", "gathered", "stepped", "weighed", "summed", "written")]
        with nc.Fori(0, GS) as s:
            with nc.Block() as blk:
                @blk.sync
                def _(sp):
                    with nc.allow_non_contiguous_dma("one word of an edge on each partition"):
                        for j, name in enumerate(("src", "dst", "etype")):
                            sp.dma_start(ends[0:GE, j:j + 1], io[name][bass.ds(s * GE, GE)].rearrange(
                                "(p a) -> p a", a=1)).then_inc(loaded, 16)
                    sp.dma_start(others_i[0:GE, :], io["dst"][bass.ds(s * GE, GE)].rearrange(
                        "(a e) -> a e", a=1).to_broadcast([GE, GE])).then_inc(loaded, 16)
                    sp.wait_ge(loaded, 64)

                @blk.gpsimd
                def _(pool):
                    hold(pool, loaded, 64)
                    for out, table, j in ((q[0:GE, :], dram["q"], 1), (kv[0:GE, :], dram["kv"], 0),
                                          (rel[0:GE, :], io["rel"], 2), (best[0:GE, 1, :], dram["best"], 1),
                                          (old[0:GE, :], dram["agg"].rearrange("n h c -> n (h c)"), 1)):
                        pool.indirect_dma_start(out=out, out_offset=None, in_=table,
                                                in_offset=bass.IndirectOffsetOnAxis(ap=ends[0:GE, j:j + 1], axis=0)
                                                ).then_inc(gathered, 16)
                    hold(pool, stepped, 16)
                    for table, rows_ in ((dram["best"], best[0:GE, 2, :]),
                                         (dram["agg"].rearrange("n h c -> n (h c)"), new[0:GE, :])):
                        pool.indirect_dma_start(out=table, out_offset=bass.IndirectOffsetOnAxis(
                            ap=ends[0:GE, 1:2], axis=0), in_=rows_, in_offset=None).then_inc(written, 16)
                    pool.wait_ge(written, 32)

                @blk.vector
                def _(dve):
                    n = [0]

                    def link(ins):
                        n[0] += 1
                        ins.then_inc(stepped, 1)
                        dve.wait_ge(stepped, n[0])

                    dve.wait_ge(loaded, 64)
                    link(dve.tensor_copy(others[0:GE, :], others_i[0:GE, :]))
                    link(dve.tensor_copy(own[0:GE, :], ends[0:GE, 1:2]))
                    link(dve.tensor_scalar(same[0:GE, :], others[0:GE, :], own[0:GE, :], None, ALU.is_equal))
                    link(dve.tensor_scalar(far[0:GE, :], same[0:GE, :], -1.0, BIG, ALU.add, ALU.mult))
                    dve.wait_ge(gathered, 16 * 5)
                    link(dve.scalar_tensor_tensor(out=heads(keys[0:GE, :]),
                                                  in0=rel[0:GE, :].unsqueeze(1).to_broadcast([GE, H, HD]), scalar=0.2,
                                                  in1=heads(kv[0:GE, 0:D]), op0=ALU.mult, op1=ALU.add))
                    link(dve.tensor_tensor(prod[0:GE, :], keys[0:GE, :], q[0:GE, :], ALU.mult))
                    link(dve.tensor_reduce(score[0:GE, :], heads(prod[0:GE, :]), AX.X, ALU.add))
                    link(dve.tensor_tensor(spread[0:GE], ident[0:GE, 0:GE].unsqueeze(1).to_broadcast([GE, H, GE]),
                                           score[0:GE, :].unsqueeze(2).to_broadcast([GE, H, GE]), ALU.mult))
                    assert n[0] == 8
                    dve.wait_ge(summed, 1)
                    link(dve.tensor_tensor(masked[0:GE], psB[0:GE, 0:H * GE].rearrange("p (h e) -> p h e", h=H),
                                           far[0:GE, :].unsqueeze(1).to_broadcast([GE, H, GE]), ALU.add))
                    link(dve.tensor_reduce(best[0:GE, 0, :], masked[0:GE], AX.X, ALU.max))
                    link(dve.tensor_tensor(best[0:GE, 2, :], best[0:GE, 0, :], best[0:GE, 1, :], ALU.max))
                    link(dve.tensor_tensor(diff[0:GE, 0, :], score[0:GE, :], best[0:GE, 2, :], ALU.subtract))
                    link(dve.tensor_tensor(diff[0:GE, 1, :], best[0:GE, 1, :], best[0:GE, 2, :], ALU.subtract))
                    assert n[0] == 13
                    dve.wait_ge(weighed, 1)
                    wide = lambda a: a.unsqueeze(2).to_broadcast([GE, H, CW])
                    link(dve.tensor_tensor(heads(weighted[0:GE, :]), heads(kv[0:GE, D:KVW]),
                                           wide(factor[0:GE, 0, :]), ALU.mult))
                    link(dve.tensor_tensor(heads(kept[0:GE, :]), heads(old[0:GE, :]),
                                           wide(factor[0:GE, 1, :]), ALU.mult))
                    assert n[0] == 15
                    dve.wait_ge(summed, 2)
                    link(dve.tensor_tensor(new[0:GE, :], psS[0:GE, 0:H * CW], kept[0:GE, :], ALU.add))

                @blk.scalar
                def _(act):
                    act.wait_ge(stepped, 13)
                    act.activation(factor[0:GE], diff[0:GE], ACT.Exp, scale=SCALE).then_inc(weighed, 1)

                @blk.tensor
                def _(pe):
                    pe.wait_ge(stepped, 8)
                    pe.matmul(psB[0:GE, 0:H * GE], cst("ones")[0:GE, 0:GE],
                              spread[0:GE].rearrange("p h e -> p (h e)"), start=True, stop=True).then_inc(summed, 1)
                    pe.wait_ge(stepped, 14)
                    pe.matmul(psS[0:GE, 0:H * CW], same[0:GE, :], weighted[0:GE, :], start=True, stop=True
                              ).then_inc(summed, 1)
            start_over(nc, counters)


assert NT % RN == 0
CHAINS = dict(A=4, B=3, C=6, D=4, E=3, R=26)
V_BOTH = 14


def after_edges(nc, ctx, cst, io, dram, x1, slots, gap, rows, ints):
    def sb(name, shape, dt=F32):
        return ctx.enter_context(nc.sbuf_tensor(name, shape, dt))

    def sem(name):
        return ctx.enter_context(nc.semaphore(name))

    R = B = RN
    x = [sb(f"n_x{i}", [P, D]) for i in range(R)]
    xn = [sb(f"n_xn{i}", [P, D]) for i in range(R)]
    agg = [sb(f"n_agg{i}", [P, H * CW]) for i in range(R)]
    v = [sb(f"n_v{i}", [P, H * CW]) for i in range(R)]
    own = [sb(f"n_own{i}", [P, D]) for i in range(R)]
    msg = [sb(f"n_msg{i}", [P, D]) for i in range(R)]
    msgT = [sb(f"n_msgT{i}", [P, DC, P]) for i in range(R)]
    y = [sb(f"n_y{i}", [P, D]) for i in range(R)]
    h2 = [sb(f"n_h2{i}", [P, D]) for i in range(R)]
    h2T = [sb(f"n_h2T{i}", [P, DC, P]) for i in range(R)]
    x2 = [sb(f"n_x2{i}", [P, D]) for i in range(R)]
    x2all = sb("n_x2all", [P, NT, D])
    st = [sb(f"n_st{i}", [P, 3, 10]) for i in range(R)]
    den = [sb(f"n_den{i}", [P, 2, H]) for i in range(R)]
    lone = [sb(f"n_lone{i}", [P, H]) for i in range(R)]
    logit = sb("n_logit", [P, NT, NX])
    key = sb("n_key", [P, 4, B, NX])
    eq = sb("n_eq", [P, 2, B, NX])
    hot = sb("n_hot", [P, 2, B, NX])
    top = sb("n_top", [P, 4, B])
    both = sb("n_both", [P, NX, B])
    tot = sb("n_tot", [P, 3, NX * B])
    base = sb("n_base", [P, NX, B])
    pos = sb("n_pos", [P, NX, B])
    cand = sb("n_cand", [P, 2, B, NX])
    at = sb("n_at", [P, 2, B])
    slot = sb("n_slot", [P, 2, B], I32)
    run = sb("n_run", [P, NX])
    places = sb("n_places", [P, 2, NT])
    wo = sb("n_wo", [P, DC, D])
    wr = sb("n_wr", [P, DC, NX])
    vec = sb("n_vec", [P, 2, D])
    br = sb("n_br", [P, NX])
    zero = sb("n_zero", [P, 2 * D])
    beyond = sb("n_beyond", [P, 2 * NT, NX])
    shift = sb("n_shift", [P, 2 * NT])
    bl = sb("n_bl", [P, 8, NX])
    blk_gt = sb("n_gt", [P, NX, BPE])
    blk_ge = sb("n_ge", [1, NB, NX])
    blk_gn = sb("n_gn", [1, NB, NX])
    blk_r = sb("n_r", [1, 6, NB])
    psM = ctx.enter_context(nc.psum_tensor("n_psM", [P, 512], F32))
    psO = ctx.enter_context(nc.psum_tensor("n_psO", [P, 512], F32))
    psH = ctx.enter_context(nc.psum_tensor("n_psH", [P, 512], F32))
    psL = ctx.enter_context(nc.psum_tensor("n_psL", [P, 512], F32))
    psR = ctx.enter_context(nc.psum_tensor("n_psR", [P, 512], F32))
    ident = cst("ident")
    heads = lambda a: a.rearrange("p (h c) -> p h c", h=H)
    wide = lambda a: a.unsqueeze(2).to_broadcast([P, H, HD])

    s_w = sem("ns_w")
    s_in = [sem(f"ns_in{i}") for i in range(R)]
    s_sc = [sem(f"ns_sc{i}") for i in range(R)]
    s_tail = sem("ns_tail")
    s_z = sem("ns_z")
    s_pool = sem("ns_pool")
    s_c = {k: sem(f"ns_{k}") for k in CHAINS}
    s_sd = [sem(f"ns_sd{j}") for j in range(3)]
    s_mT = sem("ns_mT")
    s_hT = sem("ns_hT")
    s_x2 = sem("ns_x2")
    s_pm = sem("ns_pm")
    s_po = sem("ns_po")
    s_ph = sem("ns_ph")
    s_pl = sem("ns_pl")
    s_pr = sem("ns_pr")
    s_end = sem("ns_end")
    LAG = dict(A=0, B=1, C=2, D=3, E=4, R=5)
    SCAT = 6 + LAG["R"] + 1

    def wait(eng, sem_, value):
        eng.wait_ge(sem_, value)

    def chain(dve, name, count, ops):
        assert len(ops) == CHAINS[name], (name, len(ops))
        for k, op in enumerate(ops):
            alone = isinstance(op, tuple)
            if k:
                (hold if alone else wait)(dve, s_c[name], count + k)
            (op[0] if alone else op)().then_inc(s_c[name], 1)
            yield

    with nc.Block() as blk:
        @blk.sync
        def _(sp):
            for a in range(DC):
                sp.dma_start(wo[:, a, :], io["Wo"][a * P:(a + 1) * P, :]).then_inc(s_w, 16)
                sp.dma_start(wr[:, a, :], io["Wr"][a * P:(a + 1) * P, :]).then_inc(s_w, 16)
            for j, name in enumerate(("gamma", "beta")):
                sp.dma_start(vec[:, j, :], io[name].rearrange("(a d) -> a d", a=1).to_broadcast([P, D])
                             ).then_inc(s_w, 16)
            sp.dma_start(br[:, :], io["br"].rearrange("(a d) -> a d", a=1).to_broadcast([P, NX])).then_inc(s_w, 16)

            def step(T):
                g = T(0)
                r0 = bass.ds(node_rows(g.t), P)
                if g.first >= R:
                    hold(sp, s_c["C"], (g.t - (R - 1)) * CHAINS["C"])
                sp.dma_start(agg[g.slot][:, :], dram["agg"][r0].rearrange("n h c -> n (h c)")
                             ).then_inc(s_in[g.slot], 16)
                sp.dma_start(v[g.slot][:, :], dram["kv"][r0, D:KVW]).then_inc(s_in[g.slot], 16)
                sp.dma_start(xn[g.slot][:, :], dram["xn"][r0, :]).then_inc(s_in[g.slot], 16)
                sp.dma_start(x[g.slot][:, :], io["x"][r0, :]).then_inc(s_in[g.slot], 16)
            pipeline(sp, NT - 1, 0, 0, R, R, step)
            step(lambda off: Tile(NT - 1, (NT - 1) % R, (NT - 1) // R, True, NT - 1))
            for i in range(R):
                sp.wait_ge(s_sc[i], 32 * len(range(i, NT, R)))
            sp.wait_ge(s_end, 2)
            for e in range(NX):
                n = sp.value_load(ints[0:1, e:e + 1], min_val=0, max_val=N)
                sp.dma_start(dram["xs"][bass.ds(n + e * CAP, BT), :].rearrange("(p a) c -> p (a c)", a=2),
                             zero[:, :]).then_inc(s_tail, 16)
            sp.wait_ge(s_tail, 16 * NX)

        @blk.gpsimd
        def _(pool):
            pool.wait_ge(s_w, 16 * 7)

            def step(T):
                g = T(0)
                if g.live:
                    i = g.slot
                    hold(pool, s_in[i], (g.rnd + 1) * 64)
                    pool.tensor_scalar(lone[i][:, :], heads(agg[i][:, :])[:, :, HD], 0.0, None, ALU.is_equal
                                       ).then_inc(s_pool, 1)
                    pool.wait_ge(s_pool, g.t * 3 + 1)
                    pool.tensor_tensor(heads(own[i][:, :]), heads(v[i][:, :])[:, :, 0:HD], wide(lone[i][:, :]),
                                       ALU.mult).then_inc(s_pool, 1)
                    pool.tensor_tensor(x[i][:, :], x[i][:, :], vec[:, 1, :], ALU.add).then_inc(s_pool, 1)
                o = T(SCAT)
                if o.live:
                    pool.wait_ge(s_c["R"], (o.rnd + 1) * CHAINS["R"])
                    hold(pool, s_x2, o.t + 1)
                    for k in range(2):
                        pool.indirect_dma_start(
                            out=dram["xs"][:, :], out_offset=bass.IndirectOffsetOnAxis(
                                ap=slot[:, k, o.slot:o.slot + 1], axis=0),
                            in_=x2[o.slot][:, :], in_offset=None).then_inc(s_sc[o.slot], 16)
            pipeline(pool, NT, 0, SCAT, R, 2 * R, step)

        @blk.scalar
        def _(act):
            act.preload_act_table(ACT.Sqrt)

            def step(T):
                def sqrt(j, g, name, steps):
                    act.wait_ge(s_c[name], g.t * CHAINS[name] + steps)
                    act.activation(st[g.slot][:, j, 8:9], st[g.slot][:, j, 7:8], ACT.Sqrt, bias=cst("eps")
                                   ).then_inc(s_sd[j], 1)
                d, c, b, a, o = T(LAG["D"]), T(LAG["C"]), T(LAG["B"]), T(0), T(SCAT - 1)
                if b.live:
                    sqrt(0, b, "B", 3)
                if c.live:
                    sqrt(1, c, "C", 6)
                if d.live:
                    sqrt(2, d, "D", 4)
                if a.live:
                    act.wait_ge(s_pm, a.t + 1)
                    act.copy(msgT[a.slot][:, :, :].rearrange("p a q -> p (a q)"), psM[:, 0:D]).then_inc(s_mT, 1)
                if d.live:
                    act.wait_ge(s_ph, d.t + 1)
                    act.copy(h2T[d.slot][:, :, :].rearrange("p a q -> p (a q)"), psH[:, 0:D]).then_inc(s_hT, 1)
                if o.live:
                    act.wait_ge(s_c["E"], (o.t + 1) * CHAINS["E"])
                    if o.first >= R:
                        act.wait_ge(s_sc[o.slot], o.rnd * 32)
                    act.copy(x2[o.slot][:, :], x2all[:, bass.ds(o.t, 1), :].rearrange("p a d -> p (a d)")
                             ).then_inc(s_x2, 1)
            pipeline(act, NT, 0, SCAT - 1, R, 3 * R, step)

        @blk.vector
        def _(dve):
            dve.memset(zero[:, :], 0.0).then_inc(s_z, 1)
            dve.tensor_copy(run[:, :], cst("cap8")).then_inc(s_z, 1)
            dve.wait_ge(s_z, 2)
            dve.wait_ge(s_w, 16 * 7)
            whole = lambda a, t: a[:, bass.ds(t, 1), :].rearrange("p a d -> p (a d)")


            def after(sem_, value, op):
                def lay():
                    dve.wait_ge(sem_, value)
                    return op()
                return lay

            def stats(j, i, inp):
                return [(lambda: dve.bn_stats(st[i][:, j, 0:6], inp),) if j == 1 else
                        lambda: dve.bn_stats(st[i][:, j, 0:6], inp),
                        (lambda: dve.bn_aggr(st[i][:, j, 6:8], st[i][:, j, 0:6]),)]

            def normed(j, g, out, inp):
                i = g.slot
                return [after(s_sd[j], g.t + 1, lambda: dve.reciprocal(st[i][:, j, 9:10], st[i][:, j, 8:9])),
                        lambda: dve.tensor_scalar(out, inp, st[i][:, j, 6:7], st[i][:, j, 9:10],
                                                  ALU.subtract, ALU.mult)]

            def messages(g):
                i = g.slot
                sums = heads(agg[i][:, :])
                return [
                    after(s_in[i], (g.rnd + 1) * 64, lambda: dve.scalar_tensor_tensor(
                        out=den[i][:, 0, :], in0=sums[:, :, HD], scalar=0.0, in1=sums[:, :, HD],
                        op0=ALU.is_equal, op1=ALU.add)),
                    lambda: dve.reciprocal(den[i][:, 1, :], den[i][:, 0, :]),
                    lambda: dve.tensor_tensor(heads(msg[i][:, :]), sums[:, :, 0:HD], wide(den[i][:, 1, :]), ALU.mult),
                    after(s_pool, g.t * 3 + 2,
                          lambda: dve.tensor_tensor(msg[i][:, :], msg[i][:, :], own[i][:, :], ALU.add))]

            def projected(g):
                i = g.slot
                return [after(s_po, g.t + 1,
                              lambda: dve.tensor_tensor(y[i][:, :], psO[:, 0:D], xn[i][:, :], ALU.add))
                        ] + stats(0, i, y[i][:, :])

            def attended(g):
                i, x1t = g.slot, whole(x1, g.t)
                return normed(0, g, y[i][:, :], y[i][:, :]) + [
                    lambda: dve.tensor_tensor(y[i][:, :], y[i][:, :], vec[:, 0, :], ALU.mult),
                    after(s_pool, g.t * 3 + 3, lambda: dve.tensor_tensor(x1t, y[i][:, :], x[i][:, :], ALU.add))
                ] + stats(1, i, x1t)

            def second(g):
                i = g.slot
                return normed(1, g, h2[i][:, :], whole(x1, g.t)) + stats(2, i, h2[i][:, :])

            def third(g):
                return normed(2, g, whole(x2all, g.t), h2[g.slot][:, :]) + [
                    after(s_pl, g.t + 1,
                          lambda: dve.tensor_tensor(whole(logit, g.t), psL[:, 0:NX], br[:, :], ALU.add))]

            def routed(g):
                end = isinstance(g.t, int) and g.t == NT - 1
                lg = logit[:, bass.ds(g.t - (B - 1), B), :]
                now = bass.ds(g.t - (B - 1), B)
                bc = lambda a: a.unsqueeze(2).to_broadcast([P, B, NX])
                rank = cst("rank8").unsqueeze(1).to_broadcast([P, B, NX])
                flat = lambda a: a.rearrange("p e t -> p (e t)")
                by_tile = lambda a: a.rearrange("p e t -> p t e")

                def best(k, src):
                    return [after(s_c["E"], (g.t + 1) * CHAINS["E"],
                                  lambda: dve.tensor_reduce(top[:, 2 * k, :], src, AX.X, ALU.max)),
                            lambda: dve.tensor_tensor(eq[:, k, :, :], src, bc(top[:, 2 * k, :]), ALU.is_equal),
                            lambda: dve.tensor_tensor(key[:, k, :, :], eq[:, k, :, :], rank, ALU.mult),
                            lambda: dve.tensor_reduce(top[:, 2 * k + 1, :], key[:, k, :, :], AX.X, ALU.max),
                            lambda: dve.tensor_tensor(hot[:, k, :, :], key[:, k, :, :], bc(top[:, 2 * k + 1, :]),
                                                      ALU.is_equal)]
                kept = cst("lastrows") if end else 1.0
                tiles = hot[:, :, B - 1:B, :] if end else hot[:, :, 0:1, :]

                def free_slots():
                    for sc in s_sc:
                        if g.first >= B:
                            dve.wait_ge(sc, g.rnd * 32)
                    return dve.tensor_copy(slot[:, :, :], at[:, :, :])

                return best(0, lg) + [
                    lambda: dve.scalar_tensor_tensor(out=key[:, 2, :, :], in0=hot[:, 0, :, :], scalar=-BIG, in1=lg,
                                                     op0=ALU.mult, op1=ALU.add)
                ] + best(1, key[:, 2, :, :]) + [
                    lambda: dve.tensor_tensor(gap[:, now], top[:, 2, :], top[:, 0, :], ALU.subtract),
                    lambda: dve.tensor_scalar(tiles, tiles, kept, None, ALU.mult),
                    lambda: dve.tensor_tensor(by_tile(both[:, :, :]), hot[:, 0, :, :], hot[:, 1, :, :], ALU.add),
                    after(s_pr, g.rnd + 1, lambda: dve.tensor_copy(tot[:, 0, :], psR[:, NX * B:2 * NX * B])),
                    lambda: dve.tensor_tensor_scan(tot[:, 1, :], cst("restart"), tot[:, 0, :], 0.0, ALU.mult, ALU.add),
                    lambda: dve.tensor_tensor(tot[:, 2, :], tot[:, 1, :], tot[:, 0, :], ALU.subtract),
                    lambda: dve.tensor_tensor(base[:, :, :], tot[:, 2, :].rearrange("p (e t) -> p e t", t=B),
                                              run[:, :].unsqueeze(2).to_broadcast([P, NX, B]), ALU.add),
                    lambda: dve.tensor_tensor(flat(pos[:, :, :]), psR[:, 0:NX * B], flat(base[:, :, :]), ALU.add),
                    lambda: dve.tensor_tensor(run[:, :], run[:, :],
                                              tot[:, 1, :].rearrange("p (e t) -> p e t", t=B)[:, :, B - 1], ALU.add),
                    lambda: dve.tensor_tensor(cand[:, 0, :, :], by_tile(pos[:, :, :]), hot[:, 0, :, :], ALU.mult),
                    lambda: dve.tensor_tensor(cand[:, 1, :, :], by_tile(pos[:, :, :]), hot[:, 1, :, :], ALU.mult),
                    lambda: dve.tensor_reduce(at[:, :, :], cand[:, :, :, :], AX.X, ALU.add),
                    lambda: dve.tensor_tensor(at[:, :, B - 1], at[:, :, B - 1], cst("spare" if end else "nospare"),
                                              ALU.add),
                    lambda: dve.tensor_copy(places[:, :, now], at[:, :, :]),
                    free_slots]

            def step(T):
                parts = [chain(dve, name, g.t * CHAINS[name], ops(g)) for name, ops in (
                    ("E", third), ("D", second), ("C", attended), ("B", projected), ("A", messages))
                    for g in (T(LAG[name]),) if g.live]
                g = T(LAG["R"])
                if g.live and g.slot == B - 1:
                    parts.append(chain(dve, "R", g.rnd * CHAINS["R"], routed(g)))
                while parts:
                    parts = [p for p in parts if next(p, "end") != "end"]
            pipeline(dve, NT, 0, LAG["R"], R, 2 * R, step)

            c = [0]

            def link(ins):
                c[0] += 1
                ins.then_inc(s_end, 1)
                dve.wait_ge(s_end, c[0])
            dve.wait_ge(s_c["R"], NT // B * CHAINS["R"])
            link(dve.tensor_tensor(bl[:, 3, :], run[:, :], cst("cap8"), ALU.subtract))
            link(dve.tensor_copy(ints[0:1, 0:NX], bl[0:1, 3, :]))
            steps = cst("steps")[0:1, :]
            link(dve.tensor_tensor(blk_gt[:, :, :], bl[:, 3, :].unsqueeze(2).to_broadcast([P, NX, BPE]),
                                   cst("fills").unsqueeze(1).to_broadcast([P, NX, BPE]), ALU.is_gt))
            link(dve.tensor_reduce(bl[:, 0, :], blk_gt[:, :, :], AX.X, ALU.add))
            link(dve.tensor_scalar(bl[:, 2, :], bl[:, 0, :], float(BT), float(-CAP), ALU.mult, ALU.add))
            flat = places[:, :, :].rearrange("p k t -> p (k t)")
            link(dve.tensor_tensor(beyond[:, :, 0:NX - 1], flat.unsqueeze(2).to_broadcast([P, 2 * NT, NX - 1]),
                                   cst("cap8")[:, 1:NX].unsqueeze(1).to_broadcast([P, 2 * NT, NX - 1]), ALU.is_ge))
            link(dve.tensor_tensor(beyond[:, :, 0:NX - 1], beyond[:, :, 0:NX - 1],
                                   bl[:, 2:3, 0:NX - 1].to_broadcast([P, 2 * NT, NX - 1]), ALU.mult))
            link(dve.tensor_reduce(shift[:, :], beyond[:, :, 0:NX - 1], AX.X, ALU.add))
            link(dve.tensor_tensor(flat, flat, shift[:, :], ALU.add))
            link(dve.tensor_scalar(slots[:, :, :].rearrange("p k t -> p (k t)"), flat, float(NB * BT - 1), None,
                                   ALU.min))
            link(dve.tensor_tensor_scan(bl[0:1, 1, :], cst("ones")[0:1, 0:NX], bl[0:1, 0, :], 0.0, ALU.mult, ALU.add))
            link(dve.tensor_tensor(blk_ge[0:1], steps.unsqueeze(2).to_broadcast([1, NB, NX]),
                                   bl[0:1, 1:2, :].to_broadcast([1, NB, NX]), ALU.is_ge))
            link(dve.tensor_tensor(blk_gn[0:1], blk_ge[0:1], bl[0:1, 0:1, :].to_broadcast([1, NB, NX]), ALU.mult))
            link(dve.tensor_reduce(blk_r[0:1, 1, :], blk_ge[0:1], AX.X, ALU.add))
            link(dve.tensor_reduce(blk_r[0:1, 2, :], blk_gn[0:1], AX.X, ALU.add))
            link(dve.tensor_tensor(blk_r[0:1, 3, :], steps, blk_r[0:1, 2, :], ALU.subtract))
            link(dve.tensor_scalar(blk_r[0:1, 4, :], blk_r[0:1, 3, :], float(BT), None, ALU.mult))
            link(dve.tensor_scalar(blk_r[0:1, 5, :], blk_r[0:1, 1, :], float(CAP), None, ALU.mult))
            link(dve.tensor_tensor(blk_r[0:1, 2, :], blk_r[0:1, 4, :], blk_r[0:1, 5, :], ALU.add))
            link(dve.tensor_scalar(rows[0:1, NB:2 * NB], blk_r[0:1, 2, :], float(NX * CAP + BT), None, ALU.min))
            link(dve.tensor_scalar(rows[0:1, 0:NB], blk_r[0:1, 1, :], float(NX - 1), None, ALU.min))

        @blk.tensor
        def _(pe):
            pe.wait_ge(s_w, 16 * 7)

            def step(T):
                a, d, g = T(0), T(LAG["D"]), T(LAG["R"])
                if a.live:
                    pe.wait_ge(s_c["A"], (a.t + 1) * CHAINS["A"])
                    if a.first >= 1:
                        pe.wait_ge(s_mT, a.t)
                    for b in range(DC):
                        mm = pe.transpose(psM[:, b * P:(b + 1) * P], msg[a.slot][:, b * P:(b + 1) * P], ident)
                    mm.then_inc(s_pm, 1)
                if d.live:
                    pe.wait_ge(s_c["D"], d.t * CHAINS["D"] + 2)
                    if d.first >= 1:
                        pe.wait_ge(s_hT, d.t)
                    for b in range(DC):
                        mm = pe.transpose(psH[:, b * P:(b + 1) * P], h2[d.slot][:, b * P:(b + 1) * P], ident)
                    mm.then_inc(s_ph, 1)
                if a.live:
                    pe.wait_ge(s_mT, a.t + 1)
                    if a.first >= 1:
                        pe.wait_ge(s_c["B"], (a.t - 1) * CHAINS["B"] + 1)
                    for b in range(DC):
                        mm = pe.matmul(psO[:, 0:D], msgT[a.slot][:, b, :], wo[:, b, :], start=b == 0, stop=b == DC - 1)
                    mm.then_inc(s_po, 1)
                if d.live:
                    pe.wait_ge(s_hT, d.t + 1)
                    if d.first >= 1:
                        pe.wait_ge(s_c["E"], d.t * CHAINS["E"])
                    for b in range(DC):
                        mm = pe.matmul(psL[:, 0:NX], h2T[d.slot][:, b, :], wr[:, b, :], start=b == 0, stop=b == DC - 1)
                    mm.then_inc(s_pl, 1)
                if g.live and g.slot == B - 1:
                    pe.wait_ge(s_c["R"], g.rnd * CHAINS["R"] + V_BOTH)
                    chosen = both[:, :, :].rearrange("p e t -> p (e t)")
                    pe.matmul(psR[:, 0:NX * B], cst("before"), chosen, start=True, stop=True)
                    pe.matmul(psR[:, NX * B:2 * NX * B], cst("ones"), chosen, start=True, stop=True).then_inc(s_pr, 1)
            pipeline(pe, NT, 0, LAG["R"], R, 2 * R, step)


def experts(nc, ctx, cst, io, dram, rows):
    def sb(name, shape, dt=F32):
        return ctx.enter_context(nc.sbuf_tensor(name, shape, dt))

    def sem(name):
        return ctx.enter_context(nc.semaphore(name))

    R = 3
    A = BT // P
    xs = [sb(f"f_xs{i}", [P, A, D]) for i in range(R)]
    xT = [sb(f"f_xT{i}", [P, DC, BT]) for i in range(R)]
    w1 = [sb(f"f_w1{i}", [P, DC, FF]) for i in range(R)]
    w2 = [sb(f"f_w2{i}", [P, FC, D]) for i in range(R)]
    y = [sb(f"f_y{i}", [P, A, D]) for i in range(R)]
    hT = sb("f_hT", [P, FC, BT])
    lnraw = sb("f_lnraw", [2 * NX, D])
    ln = sb("f_ln", [P, DC, 2 * NX])
    b1raw = sb("f_b1raw", [NX * FC, P])
    b1 = sb("f_b1", [P, NX * FC])
    b2 = sb("f_b2", [P, NX * D])
    psT = ctx.enter_context(nc.psum_tensor("f_psT", [P, 512], F32))
    psH = ctx.enter_context(nc.psum_tensor("f_psH", [P, 4, 512], F32))
    psY = ctx.enter_context(nc.psum_tensor("f_psY", [P, A, 512], F32))
    ident = cst("ident")

    s_c = sem("fs_c")
    s_cp = sem("fs_cp")
    s_cv = sem("fs_cv")
    s_w = [sem(f"fs_w{i}") for i in range(R)]
    s_y = [sem(f"fs_y{i}") for i in range(R)]
    s_t = sem("fs_t")
    s_xT = sem("fs_xT")
    s_h = sem("fs_h")
    s_g = sem("fs_g")
    s_p = sem("fs_p")
    s_e = sem("fs_e")

    with nc.Block() as blk:
        @blk.sync
        def _(sp):
            sp.dma_start(lnraw[0:NX, :], io["ln_g"]).then_inc(s_c, 16)
            sp.dma_start(lnraw[NX:2 * NX, :], io["ln_b"]).then_inc(s_c, 16)
            sp.dma_start(b1raw[:, :], io["b1"].rearrange("e (c p) -> (e c) p", p=P)).then_inc(s_c, 16)
            sp.dma_start(b2[:, :], io["b2"].rearrange("(a e) d -> a (e d)", a=1).to_broadcast([P, NX * D])
                         ).then_inc(s_c, 16)

            def step(T):
                g = T(0)
                if g.live:
                    e = sp.value_load(rows[0:1, bass.ds(g.t, 1)], min_val=0, max_val=NX - 1)
                    r0 = sp.value_load(rows[0:1, bass.ds(g.t + NB, 1)], min_val=0, max_val=NX * CAP + BT)
                    if g.first >= R:
                        hold(sp, s_p, g.t * A - A * (R - 1))
                    sp.dma_start(xs[g.slot][:, :, :], dram["xs"][bass.ds(r0, BT), :].rearrange(
                        "(a p) c -> p a c", p=P)).then_inc(s_w[g.slot], 16)
                    sp.dma_start(w1[g.slot][:, :, :], io["W1"][bass.ds(e, 1)].rearrange(
                        "e (a p) f -> p (e a) f", p=P)).then_inc(s_w[g.slot], 16)
                    sp.dma_start(w2[g.slot][:, :, :], io["W2"][bass.ds(e, 1)].rearrange(
                        "e (c p) d -> p (e c) d", p=P)).then_inc(s_w[g.slot], 16)
                o = T(2)
                if o.live:
                    hold(sp, s_e, o.t * A + A)
                    sp.dma_start(dram["ys"][bass.ds(o.t * BT, BT), :].rearrange("(a p) c -> p a c", p=P), y[o.slot][:, :, :]
                                 ).then_inc(s_y[o.slot], 16)
            pipeline(sp, NB, 0, 2, R, 5, step)
            for i in range(R):
                sp.wait_ge(s_y[i], 16 * len(range(i, NB, R)))

        @blk.scalar
        def _(act):
            act.preload_act_table(ACT.Gelu)
            act.wait_ge(s_cv, 2)

            def step(T):
                g = T(0)
                e = act.value_load(rows[0:1, bass.ds(g.t, 1)], min_val=0, max_val=NX - 1)
                for c in range(FC):
                    act.wait_ge(s_h, g.t * FC + c + 1)
                    if c == 0 and g.first >= 1:
                        act.wait_ge(s_p, g.t * A)
                    act.activation(hT[:, c, :], psH[:, c % 4, 0:BT], ACT.Gelu,
                                   bias=b1[:, bass.ds(e * FC + c, 1)]).then_inc(s_g, 1)
            pipeline(act, NB, 0, 0, R, 5, step)

        @blk.vector
        def _(dve):
            dve.wait_ge(s_cp, 2)
            dve.tensor_copy(ln[:, :, :], psT[:, 0:DC * 2 * NX].rearrange("p (a e) -> p a e", a=DC)).then_inc(s_cv, 1)
            dve.tensor_copy(b1[:, :], psY[:, 0, 0:NX * FC]).then_inc(s_cv, 1)
            dve.wait_ge(s_cv, 2)
            dve.wait_ge(s_c, 64)

            def step(T):
                g = T(0)
                if g.live:
                    e = dve.value_load(rows[0:1, bass.ds(g.t, 1)], min_val=0, max_val=NX - 1)
                    dve.wait_ge(s_t, g.t + 1)
                    if g.first >= R:
                        dve.wait_ge(s_h, g.t * FC - FC * (R - 1))
                    for a in range(DC):
                        dve.tensor_scalar(xT[g.slot][:, a, :], psT[:, a * BT:(a + 1) * BT],
                                          ln[:, a, bass.ds(e, 1)], ln[:, a, bass.ds(e + NX, 1)],
                                          ALU.mult, ALU.add).then_inc(s_xT, 1)
                c = T(1)
                if c.live:
                    e1 = dve.value_load(rows[0:1, bass.ds(c.t, 1)], min_val=0, max_val=NX - 1)
                    if c.first >= R:
                        dve.wait_ge(s_y[c.slot], c.rnd * 16)
                    for a in range(A):
                        dve.wait_ge(s_p, c.t * A + a + 1)
                        dve.tensor_tensor(y[c.slot][:, a, :], psY[:, a, 0:D], b2[:, bass.ds(e1 * D, D)], ALU.add
                                          ).then_inc(s_e, 1)
            pipeline(dve, NB, 0, 1, R, 5, step)

        @blk.tensor
        def _(pe):
            pe.wait_ge(s_c, 64)
            for a in range(DC):
                mm = pe.transpose(psT[:, a * 2 * NX:(a + 1) * 2 * NX], lnraw[:, a * P:(a + 1) * P],
                                  ident[0:2 * NX, 0:2 * NX])
            mm.then_inc(s_cp, 1)
            pe.transpose(psY[:, 0, 0:NX * FC], b1raw[:, :], ident[0:NX * FC, 0:NX * FC]).then_inc(s_cp, 1)
            pe.wait_ge(s_cv, 2)

            def step(T):
                g = T(0)
                if g.live:
                    pe.wait_ge(s_w[g.slot], (g.rnd + 1) * 48)
                    if g.first >= 1:
                        pe.wait_ge(s_xT, g.t * DC)
                    for a in range(DC):
                        for t in range(A):
                            mm = pe.transpose(psT[:, a * BT + t * P:a * BT + (t + 1) * P],
                                              xs[g.slot][:, t, a * P:(a + 1) * P], ident)
                    mm.then_inc(s_t, 1)
                c = T(1)
                if c.live:
                    for t in range(A):
                        if c.first >= 1:
                            pe.wait_ge(s_e, c.t * A - A + t + 1)
                        for f in range(FC):
                            if t == 0:
                                pe.wait_ge(s_g, c.t * FC + f + 1)
                            mm = pe.matmul(psY[:, t, 0:D], hT[:, f, t * P:(t + 1) * P], w2[c.slot][:, f, :],
                                           start=f == 0, stop=f == FC - 1)
                        mm.then_inc(s_p, 1)
                if g.live:
                    pe.wait_ge(s_xT, g.t * DC + DC)
                    for f in range(FC):
                        if g.first >= 1 or f >= 4:
                            pe.wait_ge(s_g, g.t * FC + f - 3)
                        for a in range(DC):
                            mm = pe.matmul(psH[:, f % 4, 0:BT], w1[g.slot][:, a, f * P:(f + 1) * P],
                                           xT[g.slot][:, a, :], start=a == 0, stop=a == DC - 1)
                        mm.then_inc(s_h, 1)
            pipeline(pe, NB, 0, 1, R, 5, step)


def combine(nc, ctx, cst, dram, out, x1, slots, gap):
    def sb(name, shape, dt=F32):
        return ctx.enter_context(nc.sbuf_tensor(name, shape, dt))

    def sem(name):
        return ctx.enter_context(nc.semaphore(name))

    R = 3
    idx = [sb(f"c_idx{i}", [P, 2], I32) for i in range(R)]
    yy = [sb(f"c_y{i}", [P, 2, D]) for i in range(R)]
    one = [sb(f"c_one{i}", [P, D]) for i in range(R)]
    two = [sb(f"c_two{i}", [P, D]) for i in range(R)]
    ex = sb("c_ex", [P, NT])
    sm = sb("c_sm", [P, NT])
    wa = sb("c_wa", [P, NT])
    wb = sb("c_wb", [P, NT])
    s_e = sem("cs_e")
    s_s = sem("cs_s")
    s_i = sem("cs_i")
    s_y = [sem(f"cs_y{i}") for i in range(R)]
    s_v = sem("cs_v")
    s_o = [sem(f"cs_o{i}") for i in range(R)]

    with nc.Block() as blk:
        @blk.scalar
        def _(act):
            act.activation(ex[:, :], gap[:, :], ACT.Exp).then_inc(s_e, 1)

        @blk.vector
        def _(dve):
            dve.wait_ge(s_e, 1)
            dve.tensor_scalar(sm[:, :], ex[:, :], 1.0, None, ALU.add).then_inc(s_s, 1)
            dve.wait_ge(s_s, 1)
            dve.reciprocal(wa[:, :], sm[:, :]).then_inc(s_s, 1)
            dve.wait_ge(s_s, 2)
            dve.tensor_tensor(wb[:, :], wa[:, :], ex[:, :], ALU.mult).then_inc(s_s, 1)
            dve.wait_ge(s_s, 3)

            def step(T):
                g = T(0)
                if g.live:
                    if g.first >= R:
                        dve.wait_ge(s_y[g.slot], g.rnd * 32)
                    dve.tensor_copy(idx[g.slot][:, :], slots[:, :, bass.ds(g.t, 1)].rearrange("p k a -> p (k a)")
                                    ).then_inc(s_i, 1)
                c = T(2)
                if c.live:
                    i = c.slot
                    dve.wait_ge(s_y[i], (c.rnd + 1) * 32)
                    dve.scalar_tensor_tensor(out=one[i][:, :], in0=yy[i][:, 0, :], scalar=wa[:, bass.ds(c.t, 1)],
                                             in1=x1[:, bass.ds(c.t, 1), :].rearrange("p a d -> p (a d)"), op0=ALU.mult, op1=ALU.add).then_inc(s_v, 1)
                    dve.wait_ge(s_v, c.t * 2 + 1)
                    if c.first >= R:
                        dve.wait_ge(s_o[i], c.rnd * 16)
                    dve.scalar_tensor_tensor(out=two[i][:, :], in0=yy[i][:, 1, :], scalar=wb[:, bass.ds(c.t, 1)],
                                             in1=one[i][:, :], op0=ALU.mult, op1=ALU.add).then_inc(s_v, 1)
            pipeline(dve, NT, 0, 2, R, 6, step)

        @blk.gpsimd
        def _(pool):
            def step(T):
                g = T(0)
                if g.first >= R:
                    hold(pool, s_v, g.t * 2 - 2 * (R - 1))
                hold(pool, s_i, g.t + 1)
                for k in range(2):
                    pool.indirect_dma_start(out=yy[g.slot][:, k, :], out_offset=None, in_=dram["ys"][:, :],
                                            in_offset=bass.IndirectOffsetOnAxis(ap=idx[g.slot][:, k:k + 1], axis=0)
                                            ).then_inc(s_y[g.slot], 16)
            pipeline(pool, NT, 0, 0, R, 6, step)

        @blk.sync
        def _(sp):
            def step(T):
                o = T(2)
                if o.live:
                    hold(sp, s_v, o.t * 2 + 2)
                    lo, r = own_rows(o.t)
                    sp.dma_start(out[r, :], two[o.slot][lo:P, :]
                                 ).then_inc(s_o[o.slot], 16)
            pipeline(sp, NT, 0, 2, R, 6, step)
            for i in range(R):
                sp.wait_ge(s_o[i], 16 * len(range(i, NT, R)))


def build(nc, io, out):
    dram = {name: nc.dram_tensor(f"d_{name}", shape, dt, kind="Internal").ap() for name, shape, dt in (
        ("kv", (N, KVW), F32), ("xn", (N, D), F32), ("src", (NG, G), I32),
        ("featx", (NG, G), BF16), ("featt", (NG, G), BF16), ("agg", (AR, H, CW), F32),
        ("xs", (NX * CAP + 2 * BT, D), F32), ("ys", (NB * BT, D), F32),
        ("q", (N, D), F32), ("best", (N, H), F32))}
    with ExitStack() as whole:
        def sb(name, shape, dt=F32):
            return whole.enter_context(nc.sbuf_tensor(name, shape, dt))
        consts = sb("consts", list(CONSTS.shape))
        slots = sb("slots", [P, 2, NT], I32)
        gap = sb("gap", [P, NT])
        rows = sb("rows", [1, 2 * NB], I32)
        unfit = sb("unfit", [1, 1], I32)
        ints = sb("ints", [1, NX], I32)
        loaded = whole.enter_context(nc.semaphore("loaded"))

        def cst(name):
            return consts[:, CAT[name][0]:CAT[name][1]]

        with nc.Block() as blk:
            @blk.sync
            def _(sp):
                sp.dma_start(consts[:, :], io["consts"]).then_inc(loaded, 16)
                sp.wait_ge(loaded, 16)
        with ExitStack() as ctx:
            def sb1(name, shape, dt=F32):
                return ctx.enter_context(nc.sbuf_tensor(name, shape, dt))
            QT = sb1("QT", [P, DC, QW])
            bases = sb1("bases", [1, NG], I32)
            flag = sb1("flag", [P, NG])
            penc = sb1("penc", [P, NG])
            relT = sb1("relT", [P, NREL])
            with ExitStack() as c1:
                prepare(nc, c1, cst, io, dram, QT, bases, flag, penc, relT[:, :], unfit)
            with ExitStack() as c2:
                edge_pass(nc, c2, cst, QT, dram["kv"], dram["src"], dram["featx"], dram["featt"], dram["agg"],
                          bases, flag, penc, relT[:, :])
            unfit_now = nc.values_load(unfit[0:1, 0:1], min_val=0, max_val=1)
            with nc.If(unfit_now > 0), ExitStack() as c3:
                any_order_pass(nc, c3, cst, io, dram, QT)
        x1 = sb("x1", [P, NT, D])
        with ExitStack() as ctx:
            after_edges(nc, ctx, cst, io, dram, x1, slots, gap, rows, ints)
        with ExitStack() as ctx:
            experts(nc, ctx, cst, io, dram, rows)
        with ExitStack() as ctx:
            combine(nc, ctx, cst, dram, out, x1, slots, gap)


INPUTS = dict(x="x", src="src", dst="dst", etype="edge_type_64", query="L0_gnn_query_emb", Wq="L0_gnn_Wq",
              bq="L0_gnn_bq", Wk="L0_gnn_Wk", bk="L0_gnn_bk", Wv="L0_gnn_Wv", bv="L0_gnn_bv", rel="L0_gnn_rel_w",
              Wo="L0_gnn_Wo", bo="L0_gnn_bo", gamma="L0_gnn_gamma", beta="L0_gnn_beta", Wr="L0_ffn_Wr",
              br="L0_ffn_br", ln_g="L0_ffn_ln_g", ln_b="L0_ffn_ln_b", W1="L0_ffn_W1", b1="L0_ffn_b1",
              W2="L0_ffn_W2", b2="L0_ffn_b2")


def kernel(**inputs):
    import numpy as _np
    import concourse.bacc as _bacc
    from concourse import mybir as _mybir
    from concourse.bass_utils import run_bass_kernel_spmd as _run

    nc = _bacc.Bacc("TRN2", target_bir_lowering=False, num_devices=1)
    arrays = {"in_consts": CONSTS}
    for short, name in INPUTS.items():
        arrays[f"in_{short}"] = _np.ascontiguousarray(inputs[name])
    io = {name[3:]: nc.dram_tensor(name, a.shape, _mybir.dt.from_np(a.dtype), kind="ExternalInput").ap()
          for name, a in arrays.items()}
    out = nc.dram_tensor("out_0", (N, D), F32, kind="ExternalOutput").ap()
    build(nc, io, out)
    r = _run(nc, [arrays], core_ids=[0])
    return r.results[0]["out_0"]
```

```python
from contextlib import ExitStack

import numpy as np

import concourse.bass as bass
from concourse import mybir
from concourse.alu_op_type import AluOpType as ALU

ACT = mybir.ActivationFunctionType
AX = mybir.AxisListType
F32 = mybir.dt.float32
F32R = mybir.dt.float32r
BF16 = mybir.dt.bfloat16
I32 = mybir.dt.int32
U32 = mybir.dt.uint32

P = 128
N, D = 6250, 256
H, HD = 4, 64
DC = D // P
E = 200000
NREL = 64
W = P // H
TG = 6
G = TG * P
NG = -(-E // G)
GH = G // 2
CW = HD + 1
KVW = D + H * CW
GE = 125
GS = E // GE
NT = -(-N // P)
LAST = N - P
QW = N + W + 22
AR = 50 * P
RN = 7
NX, FF = 8, 1024
FC = FF // P
BT = 256
CAP = N + BT + 22
NB = (2 * N - NX) // BT + NX
BPE = -(-N // BT)
EPS = 1e-5
BIG = 2.0 ** 100
FLOOR = -1e28
SCALE = HD ** -0.5


class Tile:

    def __init__(self, t, slot, rnd, live, first):
        self.t, self.slot, self.rnd, self.live, self.first = t, slot, rnd, live, first


def pipeline(eng, n, lo, hi, unroll, warm, step):
    def at(s_static, r, k, base):
        def T(off):
            if r is None:
                t = s_static - off
                return Tile(t, t % unroll, t // unroll, 0 <= t < n, t)
            c = base + k - off
            return Tile(r * unroll + c, c % unroll, r + c // unroll, True, c)
        return T
    loops = (n + lo - warm) // unroll if lo < 0 else (n - warm) // unroll
    for s in range(lo, warm):
        step(at(s, None, 0, 0))
    with eng.Fori(0, loops) as r:
        for k in range(unroll):
            step(at(None, r, k, warm))
    for s in range(warm + loops * unroll, n + hi):
        step(at(s, None, 0, 0))


def hold(eng, sem, value):
    eng.wait_ge(sem, value)
    eng.nop(nofuse=True)


def lay_constants():
    p = np.arange(P)
    q = np.arange(P)
    ident = np.eye(P, dtype=np.float32)
    first = (((q % W) == 0)[None, :] & ((p // W)[:, None] == (q // W)[None, :])).astype(np.float32)
    pen = np.zeros((P, P), np.float32)
    for r in range(W + 2):
        pen[NREL + r] = np.where((q % W) == r, 0.0, -BIG)
    match = np.zeros((P, 1), np.float32)
    match[:NREL, 0] = np.arange(NREL)
    match[NREL:NREL + W + 1, 0] = np.arange(W + 1)
    match[NREL + W + 1, 0] = -1
    inwin = (p % W).astype(np.float32)[:, None]
    isfirst = ((p % W) == 0).astype(np.float32)[:, None]
    before = (p[:, None] < q[None, :]).astype(np.float32)
    parts = dict(ident=ident, first=first, pen=pen, before=before, ones=np.ones((P, P), np.float32),
                 match=match, inwin=inwin, isfirst=isfirst,
                 eps=np.full((P, 1), EPS, np.float32),
                 rank8=np.tile(NX - np.arange(NX, dtype=np.float32), (P, 1)),
                 restart=np.tile((np.arange(NX * RN) % RN > 0).astype(np.float32), (P, 1)),
                 cap8=np.tile(np.arange(NX, dtype=np.float32) * CAP, (P, 1)),
                 lastrows=(p >= P - (N - (NT - 1) * P)).astype(np.float32)[:, None],
                 fills=np.tile(np.arange(BPE, dtype=np.float32) * BT, (P, 1)),
                 nospare=np.zeros((P, 2), np.float32),
                 spare=np.where((p < P - (N - (NT - 1) * P))[:, None], NX * CAP + p[:, None] + [0, P],
                                0).astype(np.float32),
                 steps=np.tile(np.arange(NB, dtype=np.float32), (P, 1)))
    at, cols = {}, 0
    for name, a in parts.items():
        at[name] = (cols, cols + a.shape[1])
        cols += a.shape[1]
    return np.concatenate(list(parts.values()), 1), at


CONSTS, CAT = lay_constants()


def edge_pass(nc, ctx, cst, QT, kv_dram, src_dram, featx_dram, feat_t_dram, agg_dram, bases, flag, penc, relT):
    def sb(name, shape, dt=F32):
        return ctx.enter_context(nc.sbuf_tensor(name, shape, dt))

    def sem(name):
        return ctx.enter_context(nc.semaphore(name))

    R = 4
    NR = NREL + W + 2
    idx = [sb(f"e_idx{i}", [P, TG], I32) for i in range(R)]
    rows = [sb(f"e_rows{i}", [P, G], BF16) for i in range(R)]
    kv = [sb(f"e_kv{i}", [P, TG, KVW]) for i in range(R)]
    onehot = [sb(f"e_onehot{i}", [P, G], F32R) for i in range(R)]
    qblock = [sb(f"e_qblock{i}", [P, DC, P]) for i in range(R)]
    qrel = [[sb(f"e_qrel_{n}{i}", [P, P], F32R) for n in ("high", "low")] for i in range(R)]
    prob = [sb(f"e_prob{i}", [P, G]) for i in range(R)]
    probT = [sb(f"e_probT{i}", [P, TG, P]) for i in range(R)]
    carry = [sb(f"e_carry{i}", [P, P]) for i in range(R)]
    acc = [sb(f"e_acc{i}", [P, CW]) for i in range(R)]
    carried = [sb(f"e_carried{i}", [P, CW]) for i in range(R)]
    small = [sb(f"e_small{i}", [P, 8]) for i in range(R)]
    kT = [sb(f"e_kT{i}", [P, DC, G]) for i in range(2)]
    psK = ctx.enter_context(nc.psum_tensor("psK", [P, 2, 512], F32))
    psD = ctx.enter_context(nc.psum_tensor("psD", [P, 2, 512], F32))
    psP = ctx.enter_context(nc.psum_tensor("psP", [P, 2, 512], F32))
    psA = ctx.enter_context(nc.psum_tensor("psA", [P, 512], F32))
    psX = ctx.enter_context(nc.psum_tensor("psX", [P, 512], F32))
    MX, MC, MM, NM, AL = (slice(i, i + 1) for i in range(5))

    ident = cst("ident")
    s_idx = [sem(f"es_idx{i}") for i in range(R)]
    s_rows = [sem(f"es_rows{i}") for i in range(R)]
    s_kv = [sem(f"es_kv{i}") for i in range(R)]
    s_out = [sem(f"es_out{i}") for i in range(R)]
    s_init = sem("es_init")
    s_qb = sem("es_qb")
    s_exp = sem("es_exp")
    s_pT = sem("es_pT")
    s_cas = sem("es_cas")
    s_m = sem("es_m")
    s_carry = sem("es_carry")
    s_oh = sem("es_oh")
    s_kTv = sem("es_kTv")
    s_kTa = sem("es_kTa")
    s_x = sem("es_x")
    s_acc = sem("es_acc")
    s_d = sem("es_d")
    s_pp = sem("es_pp")
    s_agg = sem("es_agg")
    s_pk = sem("es_pk")
    s_px = sem("es_px")

    LO, HI, WARM = -1, 2, 6

    with nc.Block() as blk:
        @blk.sync
        def _(sp):
            def step(T):
                g = T(0)
                if g.live:
                    if g.first >= R:
                        hold(sp, s_kv[g.slot], g.rnd * (16 * TG))
                    sp.dma_start(idx[g.slot][:, :], src_dram[bass.ds(g.t, 1)].rearrange("a (p t) -> (a p) t", t=TG)
                                 ).then_inc(s_idx[g.slot], 16)
                    if g.first >= R:
                        hold(sp, s_oh, g.t - (R - 1))
                    sp.dma_start(rows[g.slot][0:NREL, :],
                                 feat_t_dram[bass.ds(g.t, 1)].to_broadcast([NREL, G])).then_inc(s_rows[g.slot], 16)
                    sp.dma_start(rows[g.slot][NREL:NR, :],
                                 featx_dram[bass.ds(g.t, 1)].to_broadcast([W + 2, G])).then_inc(s_rows[g.slot], 16)
                o = T(5)
                if o.live:
                    base = sp.value_load(bases[0:1, bass.ds(o.t, 1)], min_val=0, max_val=N - 1)
                    if o.first >= 1:
                        b = T(6)
                        hold(sp, s_out[b.slot], (b.rnd + 1) * (16 * H))
                    hold(sp, s_acc, o.t + 1)
                    for h in range(H):
                        sp.dma_start(agg_dram[bass.ds(base, W), h, :], acc[o.slot][h * W:(h + 1) * W, :]
                                     ).then_inc(s_out[o.slot], 16)
            pipeline(sp, NG, 0, 6, R, WARM, step)
            for i in range(R):
                sp.wait_ge(s_out[i], 16 * H * len(range(i, NG, R)))

        @blk.gpsimd
        def _(pool):
            def step(T):
                g = T(0)
                if g.live:
                    if g.first >= R:
                        pool.wait_ge(s_agg, g.t - (R - 1))
                    hold(pool, s_idx[g.slot], (g.rnd + 1) * 16)
                    for t in range(TG):
                        pool.indirect_dma_start(
                            out=kv[g.slot][:, t, :], out_offset=None, in_=kv_dram[:, :],
                            in_offset=bass.IndirectOffsetOnAxis(ap=idx[g.slot][:, t:t + 1], axis=0),
                        ).then_inc(s_kv[g.slot], 16)
            pipeline(pool, NG, 0, 0, R, WARM, step)

        @blk.scalar
        def _(act):
            act.preload_act_table(ACT.Exp)
            act.wait_ge(s_init, 3)

            def step(T):
                a = T(-1)
                if a.live:
                    base = act.value_load(bases[0:1, bass.ds(a.t, 1)], min_val=0, max_val=N - 1)
                    if a.first >= R:
                        hold(act, s_d, a.t - (R - 1))
                    for b in range(2):
                        act.copy(
                            qblock[a.slot][b * HD:(b + 1) * HD, :, :].rearrange(
                                "p a (h w) -> p a h w", w=W)[:, 0, b, :],
                            QT[b * HD:(b + 1) * HD, 0, bass.ds(base, W)])
                        act.copy(
                            qblock[a.slot][b * HD:(b + 1) * HD, :, :].rearrange(
                                "p a (h w) -> p a h w", w=W)[:, 1, 2 + b, :],
                            QT[b * HD:(b + 1) * HD, 1, bass.ds(base, W)]).then_inc(s_qb, 1)
                def k_half(a, j):
                    act.wait_ge(s_pk, a.t * 4 + 2 * j + 2)
                    act.copy(kT[a.slot % 2][:, 1, j * GH:(j + 1) * GH], psK[:, 1, 0:GH]).then_inc(s_kTa, 1)

                if a.live:
                    if a.first >= 2:
                        act.wait_ge(s_d, a.t - 1)
                    k_half(a, 0)
                g, c = T(0), T(1)
                if c.live:
                    act.wait_ge(s_exp, c.t * 2 + 2)
                    act.wait_ge(s_agg, c.t + 1)
                    act.activation(carried[c.slot][:, :], psA[:, P:P + CW], ACT.Copy,
                                   scale=small[c.slot][:, AL]).then_inc(s_cas, 1)
                if g.live:
                    act.wait_ge(s_m, g.t * 3 + 3)
                    if g.first >= R:
                        act.wait_ge(s_pp, g.t * 2 - 2 * (R - 1))
                    act.activation(prob[g.slot][:, :].rearrange("p (c q) -> p c q", c=2), psD[:, :, 0:GH], ACT.Exp,
                                   bias=small[g.slot][:, NM], scale=SCALE).then_inc(s_exp, 1)
                    act.activation(small[g.slot][:, AL], small[g.slot][:, MC], ACT.Exp,
                                   bias=small[g.slot][:, NM], scale=SCALE).then_inc(s_exp, 1)
                if a.live:
                    k_half(a, 1)
                if g.live:
                    if g.first >= R:
                        act.wait_ge(s_agg, g.t - (R - 1))
                    for j, (lo, hi) in enumerate(((0, 4), (4, TG))):
                        act.wait_ge(s_pp, g.t * 2 + j + 1)
                        act.copy(probT[g.slot][:, lo:hi, :].rearrange("p t q -> p (t q)"),
                                 psP[:, j, 0:(hi - lo) * P]).then_inc(s_pT, 1)
            pipeline(act, NG, LO, HI, R, WARM, step)

        @blk.vector
        def _(dve):
            for i in range(R):
                dve.memset(qblock[i][:, :, :], 0.0)
                dve.tensor_copy(qrel[i][0][:, :], cst("pen"))
                dve.tensor_scalar(qrel[i][1][:, :], cst("pen"), 0.0, None, ALU.mult)
            dve.memset(acc[R - 1][:, :], 0.0).then_inc(s_init, 1)
            dve.memset(small[R - 1][:, :], 0.0).then_inc(s_init, 1)
            dve.memset(prob[0][:, 0:1], 0.0).then_inc(s_init, 1)
            dve.wait_ge(s_init, 3)

            def step(T):
                a, g, c = T(-1), T(0), T(1)

                def k_half(j):
                    dve.wait_ge(s_pk, a.t * 4 + 2 * j + 1)
                    dve.tensor_copy(kT[a.slot % 2][:, 0, j * GH:(j + 1) * GH], psK[:, 0, 0:GH]).then_inc(s_kTv, 1)

                if a.live:
                    if a.first >= 2:
                        dve.wait_ge(s_d, a.t - 1)
                    k_half(0)
                    if a.first >= R:
                        dve.wait_ge(s_agg, a.t - (R - 1))
                    dve.tensor_scalar(carry[a.slot][:, :], cst("first"), flag[:, bass.ds(a.t, 1)], None,
                                      ALU.mult).then_inc(s_carry, 1)
                    dve.wait_ge(s_rows[a.slot], (a.rnd + 1) * 32)
                    if a.first >= R:
                        dve.wait_ge(s_d, a.t - (R - 1))
                    dve.tensor_scalar(onehot[a.slot][0:NR, :], rows[a.slot][0:NR, :], cst("match")[0:NR, :], None,
                                      ALU.is_equal).then_inc(s_oh, 1)
                if g.live:
                    sm = small[g.slot]
                    dve.wait_ge(s_d, g.t + 1)
                    dve.tensor_reduce(sm[:, MX], psD[:, :, 0:GH], AX.XY, ALU.max).then_inc(s_m, 1)
                    dve.wait_ge(s_m, g.t * 3 + 1)
                    dve.wait_ge(s_x, g.t * 3 + 3)
                    dve.scalar_tensor_tensor(out=sm[:, MM], in0=sm[:, MX], scalar=FLOOR, in1=sm[:, MC],
                                             op0=ALU.max, op1=ALU.max).then_inc(s_m, 1)
                    dve.wait_ge(s_m, g.t * 3 + 2)
                    dve.tensor_scalar(sm[:, NM], sm[:, MM], -SCALE, None, ALU.mult).then_inc(s_m, 1)
                if c.live:
                    dve.wait_ge(s_cas, c.t + 1)
                    if c.first >= R:
                        dve.wait_ge(s_out[c.slot], c.rnd * (16 * H))
                    dve.tensor_tensor(acc[c.slot][:, :], psA[:, 0:CW], carried[c.slot][:, :],
                                      ALU.add).then_inc(s_acc, 1)
                if a.live:
                    k_half(1)
                    dve.wait_ge(s_px, a.t + 1)
                    high, low = qrel[a.slot]
                    dve.tensor_copy(high[0:NREL, :], psX[0:NREL, P:2 * P]).then_inc(s_x, 1)
                    dve.wait_ge(s_x, a.t * 3 + 1)
                    dve.tensor_tensor(low[0:NREL, :], psX[0:NREL, P:2 * P], high[0:NREL, :].bitcast(F32), ALU.subtract
                                      ).then_inc(s_x, 1)
                    dve.tensor_tensor(small[a.slot][:, MC], psX[:, 0:1], penc[:, bass.ds(a.t, 1)],
                                      ALU.add).then_inc(s_x, 1)
            pipeline(dve, NG, LO, HI, R, WARM, step)

        @blk.tensor
        def _(pe):
            pe.wait_ge(s_init, 3)
            halves = [slice(a * P // DC, (a + 1) * P // DC) for a in range(DC)]

            def step(T):
                g, a = T(0), T(-1)

                def k_turned(j):
                    half, third = j % 2, j // 2
                    if a.first >= 1 or j >= 2:
                        pe.wait_ge(s_kTa if half else s_kTv, a.t * 2 + third)
                    for t in range(3):
                        mm = pe.transpose(psK[:, half, t * P:(t + 1) * P],
                                          kv[a.slot][:, third * 3 + t, half * P:(half + 1) * P], ident)
                    mm.then_inc(s_pk, 1)

                if a.live:
                    pe.wait_ge(s_kv[a.slot], (a.rnd + 1) * (16 * TG))
                    k_turned(0)
                    k_turned(1)
                if g.live:
                    pe.wait_ge(s_x, g.t * 3 + 2)
                    pe.wait_ge(s_oh, g.t + 1)
                    if g.first >= 1:
                        pe.wait_ge(s_exp, g.t * 2 - 1)
                    for c in range(2):
                        cols = slice(c * GH, (c + 1) * GH)
                        for k, part in enumerate(qrel[g.slot]):
                            pe.matmul(psD[:, c, 0:GH], part[0:NR, :], onehot[g.slot][0:NR, cols],
                                      start=k == 0, stop=False)
                        pe.wait_ge(s_kTv, g.t * 2 + c + 1)
                        pe.wait_ge(s_kTa, g.t * 2 + c + 1)
                        for b, half in enumerate(halves):
                            mm = pe.matmul(psD[half, c, 0:GH], qblock[g.slot][:, b, half], kT[g.slot % 2][:, b, cols],
                                           start=False, stop=True, tile_position=(0, half.start))
                    mm.then_inc(s_d, 1)
                c = T(1)
                if c.live:
                    prev = (c.slot - 1) % R
                    if c.first >= 1:
                        pe.wait_ge(s_acc, c.t)
                    pe.wait_ge(s_carry, c.t + 1)
                    pe.matmul(psA[:, P:P + CW], carry[c.slot][:, :], acc[prev][:, :], start=True, stop=True)
                    for j, (lo, hi) in enumerate(((0, 4), (4, TG))):
                        pe.wait_ge(s_pT, c.t * 2 + j + 1)
                        for t in range(lo, hi):
                            for h in range(H):
                                mm = pe.matmul(psA[h * W:(h + 1) * W, 0:CW], probT[c.slot][:, t, h * W:(h + 1) * W],
                                               kv[c.slot][:, t, D + h * CW:D + (h + 1) * CW],
                                               start=t == 0, stop=t == TG - 1, tile_position=(0, h * W))
                    mm.then_inc(s_agg, 1)
                if a.live:
                    k_turned(2)
                    k_turned(3)
                    if a.first >= 1:
                        pe.wait_ge(s_m, a.t * 3 - 1)
                        pe.wait_ge(s_x, a.t * 3)
                    pe.wait_ge(s_carry, a.t + 1)
                    pe.matmul(psX[:, 0:1], carry[a.slot][:, :], small[(a.slot - 1) % R][:, MM], start=True, stop=True)
                    pe.wait_ge(s_qb, a.t * 2 + 2)
                    for b in range(DC):
                        mm = pe.matmul(psX[0:NREL, P:2 * P], relT, qblock[a.slot][:, b, :],
                                       start=b == 0, stop=b == DC - 1)
                    mm.then_inc(s_px, 1)
                if g.live:
                    pe.wait_ge(s_exp, g.t * 2 + 1)
                    for j, (lo, hi) in enumerate(((0, 4), (4, TG))):
                        if g.first >= 1:
                            pe.wait_ge(s_pT, g.t * 2 + j - 1)
                        for t in range(lo, hi):
                            mm = pe.transpose(psP[:, j, (t - lo) * P:(t - lo + 1) * P],
                                              prob[g.slot][:, t * P:(t + 1) * P], ident)
                        mm.then_inc(s_pp, 1)
            pipeline(pe, NG, LO, HI, R, WARM, step)


def node_rows(t):
    return min(t * P, LAST) if isinstance(t, int) else t * P


def own_rows(t):
    lo = NT * P - N if isinstance(t, int) and t == NT - 1 else 0
    return lo, bass.ds(node_rows(t) + lo, P - lo)


def prepare(nc, ctx, cst, io, dram, QT, bases, flag, penc, relT, unfit):
    def sb(name, shape, dt=F32):
        return ctx.enter_context(nc.sbuf_tensor(name, shape, dt))

    def sem(name):
        return ctx.enter_context(nc.semaphore(name))

    R = 4
    xin = [sb(f"p_x{i}", [P, D]) for i in range(R)]
    xn = [sb(f"p_xn{i}", [P, D]) for i in range(R)]
    xnb = [sb(f"p_xnb{i}", [P, D]) for i in range(R)]
    enh = [sb(f"p_enh{i}", [P, D]) for i in range(R)]
    enhT = [sb(f"p_enhT{i}", [P, DC, P]) for i in range(R)]
    qrow = [sb(f"p_q{i}", [P, D]) for i in range(R)]
    kvrow = [sb(f"p_kv{i}", [P, KVW]) for i in range(R)]
    stat = [sb(f"p_stat{i}", [P, 12]) for i in range(R)]
    wkv = sb("p_wkv", [P, DC, 2 * D])
    wq = sb("p_wq", [P, DC, D])
    bias = sb("p_bias", [P, 4, D])
    qe = sb("p_qe", [P, D])
    qe01 = sb("p_qe01", [P, D])
    relraw = sb("p_relraw", [NREL, 2 * HD])
    chunks = [(c * P, min(NG - c * P, P)) for c in range(-(-NG // P))]
    edge = [[sb(f"p_{n}{c}", [P, G], I32) for n in ("dst", "type")] for c in range(len(chunks))]
    epos = sb("p_epos", [P, G])
    epos2 = sb("p_epos2", [P, G])
    feat = [[sb(f"p_{n}{c}", [P, G], BF16) for n in ("place", "kind")] for c in range(len(chunks))]
    zero = sb("p_zero", [P, 5 * H * CW])
    basef = sb("p_basef", [P, NG])
    baseall = sb("p_baseall", [P, NG])
    delta = sb("p_delta", [P, NG])
    seq = sb("p_seq", [P, E // GE + 1], I32)
    drop = sb("p_drop", [P, E // GE])
    place = sb("p_place", [P, G])
    misfit = sb("p_misfit", [P, 4])
    misfits = sb("p_misfits", [P, 2])
    psT = ctx.enter_context(nc.psum_tensor("p_psT", [P, 512], F32))
    psKV = [ctx.enter_context(nc.psum_tensor(f"p_psKV{i}", [P, 512], F32)) for i in range(2)]
    psQ = [ctx.enter_context(nc.psum_tensor(f"p_psQ{i}", [P, 512], F32)) for i in range(2)]
    psQT = ctx.enter_context(nc.psum_tensor("p_psQT", [P, 512], F32))
    ident = cst("ident")

    s_w = sem("ps_w")
    s_e = [sem(f"ps_e{c}") for c in range(len(chunks))]
    s_f = sem("ps_f")
    s_z = sem("ps_z")
    s_set = sem("ps_set")
    s_zero = sem("ps_zero")
    s_seq = sem("ps_seq")
    s_pb = sem("ps_pb")
    s_x = [sem(f"ps_x{i}") for i in range(R)]
    s_st = [sem(f"ps_st{i}") for i in range(R)]
    s_bn = sem("ps_bn")
    s_ln = sem("ps_ln")
    s_xb = sem("ps_xb")
    s_sd = sem("ps_sd")
    s_eT = sem("ps_eT")
    s_qT = sem("ps_qT")
    s_ev = sem("ps_ev")
    s_t = sem("ps_t")
    s_mm = sem("ps_mm")
    s_tq = sem("ps_tq")

    full, tail = divmod(E, G)
    NSRC = NG * G

    with nc.Block() as blk:
        @blk.sync
        def _(sp):
            for a in range(DC):
                rowsl = slice(a * P, (a + 1) * P)
                sp.dma_start(wkv[:, a, 0:D], io["Wk"][rowsl, :]).then_inc(s_w, 16)
                sp.dma_start(wkv[:, a, D:2 * D], io["Wv"][rowsl, :]).then_inc(s_w, 16)
                sp.dma_start(wq[:, a, :], io["Wq"][rowsl, :]).then_inc(s_w, 16)
            for j, name in enumerate(("bq", "bk", "bv", "bo")):
                sp.dma_start(bias[:, j, :], io[name].rearrange("(a d) -> a d", a=1).to_broadcast([P, D])
                             ).then_inc(s_w, 16)
            sp.dma_start(qe[:, :], io["query"].rearrange("(a d) -> a d", a=1).to_broadcast([P, D])
                         ).then_inc(s_w, 16)
            for b in range(2):
                sp.dma_start(relraw[:, b * HD:(b + 1) * HD], io["rel"]).then_inc(s_w, 16)
            with nc.allow_non_contiguous_dma("the first edge's node of each group"):
                sp.dma_start(bases[0:1, :], io["dst"].rearrange("(a e) -> a e", a=1)[:, 0:E:G]).then_inc(s_w, 16)

            def step(T):
                g = T(0)
                if g.live:
                    r0 = node_rows(g.t)
                    if g.first >= R:
                        hold(sp, s_ln, (g.t - R) * 3 + 2)
                    sp.dma_start(xin[g.slot][:, :], io["x"][bass.ds(r0, P), :]).then_inc(s_x[g.slot], 16)
                o = T(5)
                if o.live:
                    lo, r = own_rows(o.t)
                    hold(sp, s_xb, o.t + 1)
                    sp.dma_start(dram["xn"][r, :], xnb[o.slot][lo:P, :]).then_inc(s_st[o.slot], 16)
                    hold(sp, s_ev, o.t * 3 + 3)
                    sp.dma_start(dram["kv"][r, :], kvrow[o.slot][lo:P, :]).then_inc(s_st[o.slot], 16)
            pipeline(sp, NT, 0, 5, R, 2 * R, step)
            for i in range(R):
                sp.wait_ge(s_st[i], 32 * len(range(i, NT, R)))
            sp.wait_ge(s_f, 32 * len(chunks))
            sp.wait_ge(s_z, 16 * (10 + 2 + 2))

        @blk.gpsimd
        def _(pool):
            for c, (g0, n) in enumerate(chunks):
                whole = min(n, full - g0)
                for j, name in enumerate(("dst", "etype")):
                    if whole < n:
                        pool.memset(edge[c][j][:, :], 0 if j else 1000000).then_inc(s_zero, 1)
                        pool.wait_ge(s_zero, 1 + j)
                    pool.dma_start(edge[c][j][0:whole, :],
                                   io[name][g0 * G:(g0 + whole) * G].rearrange("(g e) -> g e", e=G)
                                   ).then_inc(s_e[c], 16)
                    if whole < n:
                        pool.dma_start(edge[c][j][whole:n, 0:tail],
                                       io[name][full * G:E].rearrange("(a e) -> a e", a=1)).then_inc(s_e[c], 16)
            pool.dma_start(seq[0:GE, 0:E // GE], io["dst"].rearrange("(p e) -> p e", p=GE)).then_inc(s_seq, 16)
            with nc.allow_non_contiguous_dma("the first of the next partition"):
                pool.dma_start(seq[0:GE - 1, E // GE:], io["dst"].rearrange("(p e) -> p e", p=GE)[1:GE, 0:1]
                               ).then_inc(s_seq, 16)
                pool.dma_start(seq[GE - 1:GE, E // GE:], io["dst"].rearrange("(p e) -> p e", p=GE)[
                    GE - 1:GE, E // GE - 1:E // GE]).then_inc(s_seq, 16)
            pool.memset(zero[:, :], 0.0).then_inc(s_zero, 1)
            pool.wait_ge(s_zero, 3)
            pool.dma_start(dram["src"].rearrange("g e -> (g e)")[0:E].rearrange("(a b) -> a b", b=1250),
                           io["src"].rearrange("(a b) -> a b", b=1250)).then_inc(s_z, 16)
            pool.dma_start(dram["src"].rearrange("g e -> (g e)")[E:NSRC].rearrange("(a b) -> a b", a=1),
                           zero[0:1, 0:NSRC - E].bitcast(I32)).then_inc(s_z, 16)
            for j in range(10):
                pool.dma_start(dram["agg"][j * 5 * P:(j + 1) * 5 * P].rearrange("(p a) h c -> p (a h c)", a=5),
                               zero[:, :]).then_inc(s_z, 16)
            for j in range(2):
                pool.dma_start(dram["xs"][NX * CAP + 2 * P * j:NX * CAP + 2 * P * (j + 1)].rearrange(
                    "(p a) c -> p (a c)", a=2), zero[:, 0:2 * D]).then_inc(s_z, 16)
            for c, (g0, n) in enumerate(chunks):
                pool.wait_ge(s_set, 1 + 6 * (c + 1))
                for j, name in enumerate(("featx", "featt")):
                    pool.dma_start(dram[name][g0:g0 + n, :], feat[c][j][0:n, :]).then_inc(s_f, 16)

            def step(T):
                g = T(0)
                pool.wait_ge(s_ln, g.t * 3 + 2)
                if g.first >= R:
                    pool.wait_ge(s_st[g.slot], g.rnd * 32)
                pool.tensor_tensor(xnb[g.slot][:, :], xn[g.slot][:, :], bias[:, 3, :], ALU.add).then_inc(s_xb, 1)
            pool.wait_ge(s_w, 16 * 14)
            pipeline(pool, NT, 0, 0, R, R, step)

        @blk.scalar
        def _(act):
            act.preload_act_table(ACT.Sqrt)

            def step(T):
                g, e, q = T(0), T(2), T(5)
                if g.live:
                    act.wait_ge(s_bn, g.t * 2 + 2)
                    act.activation(stat[g.slot][:, 8:9], stat[g.slot][:, 7:8], ACT.Sqrt, bias=cst("eps")
                                   ).then_inc(s_sd, 1)
                if e.live:
                    act.wait_ge(s_t, e.t + 1)
                    act.copy(enhT[e.slot][:, :, :].rearrange("p a q -> p (a q)"), psT[:, 0:D]).then_inc(s_eT, 1)
                if q.live:
                    act.wait_ge(s_tq, q.t + 1)
                    act.copy(QT[:, :, bass.ds(node_rows(q.t), P)],
                             psQT[:, 0:D].rearrange("p (a q) -> p a q", a=DC)).then_inc(s_qT, 1)
            pipeline(act, NT, 0, 5, R, 3 * R, step)

        @blk.vector
        def _(dve):
            count = [0]

            def link(ins):
                count[0] += 1
                ins.then_inc(s_set, 1)
                dve.wait_ge(s_set, count[0])

            dve.memset(QT[:, :, N:QW], 0.0)
            for i in range(R):
                dve.memset(kvrow[i][:, :], 1.0)
            link(dve.memset(misfit[:, :], 0.0))
            for c, (g0, n) in enumerate(chunks):
                dve.wait_ge(s_e[c], 16 * (4 if g0 + n > full else 2))
                link(dve.tensor_copy(epos[0:n, :], edge[c][0][0:n, :]))
                link(dve.tensor_scalar(epos2[0:n, :], epos[0:n, :], epos[0:n, 0:1], float(W),
                                       ALU.subtract, ALU.min))
                link(dve.scalar_tensor_tensor(out=place[0:n, :], in0=epos[0:n, :], scalar=float(N), in1=epos2[0:n, :],
                                              op0=ALU.is_lt, op1=ALU.mult))
                link(dve.tensor_reduce(misfit[0:n, c:c + 1], place[0:n, :], AX.X, ALU.max))
                link(dve.tensor_scalar(feat[c][0][0:n, :].rearrange("g (t p) -> g t p", t=TG),
                                       epos2[0:n, :].rearrange("g (p t) -> g t p", t=TG), -1.0, None, ALU.max))
                link(dve.tensor_copy(feat[c][1][0:n, :].rearrange("g (t p) -> g t p", t=TG),
                                     edge[c][1][0:n, :].rearrange("g (p t) -> g t p", t=TG)))
            dve.wait_ge(s_w, 16 * 14)
            link(dve.tensor_scalar(qe01[:, :], qe[:, :], 0.1, None, ALU.mult))
            link(dve.tensor_copy(basef[0:1, :], bases[0:1, :]))
            dve.wait_ge(s_pb, 2)
            link(dve.tensor_scalar(misfit[:, 0:3], misfit[:, 0:3], float(W), None, ALU.is_ge))
            dve.wait_ge(s_seq, 48)
            link(dve.tensor_tensor(drop[0:GE, :], seq[0:GE, 1:], seq[0:GE, 0:E // GE], ALU.is_lt))
            link(dve.tensor_reduce(misfit[0:GE, 3:4], drop[0:GE, :], AX.X, ALU.max))
            link(dve.tensor_reduce(misfits[:, 0:1], misfit[:, :], AX.X, ALU.add))
            link(dve.tensor_scalar(relT, psQT[:, 0:NREL], 0.2, None, ALU.mult))
            link(dve.tensor_copy(baseall[:, :], psT[:, 0:NG]))
            dve.wait_ge(s_pb, 3)
            link(dve.tensor_copy(misfits[0:1, 1:2], psKV[0][0:1, 0:1]))
            link(dve.tensor_scalar(unfit[0:1, :], misfits[0:1, 1:2], 1.0, None, ALU.min))
            link(dve.memset(flag[:, 0:1], 0.0))
            link(dve.memset(penc[:, 0:1], -BIG))
            link(dve.tensor_tensor(delta[:, 1:NG], baseall[:, 1:NG], baseall[:, 0:NG - 1], ALU.subtract))
            link(dve.tensor_scalar(flag[:, 1:NG], delta[:, 1:NG], cst("inwin"), None, ALU.is_equal))
            link(dve.tensor_scalar(basef[:, 1:NG], delta[:, 1:NG], float(W), cst("isfirst"), ALU.is_lt, ALU.mult))
            link(dve.tensor_scalar(penc[:, 1:NG], basef[:, 1:NG], -1.0, BIG, ALU.add, ALU.mult))

            def step(T):
                g, f, c = T(0), T(1), T(4)
                if g.live:
                    dve.wait_ge(s_x[g.slot], (g.rnd + 1) * 16)
                    dve.bn_stats(stat[g.slot][:, 0:6], xin[g.slot][:, :]).then_inc(s_bn, 1)
                if f.live:
                    sf = stat[f.slot]
                    dve.wait_ge(s_sd, f.t + 1)
                    dve.reciprocal(sf[:, 9:10], sf[:, 8:9]).then_inc(s_ln, 1)
                if c.live:
                    dve.wait_ge(s_mm, c.t + 1)
                    if c.first >= R:
                        dve.wait_ge(s_st[c.slot], c.rnd * 32)
                    kvr, pkv = kvrow[c.slot], psKV[c.slot % 2]
                    dve.tensor_tensor(kvr[:, 0:D], pkv[:, 0:D], bias[:, 1, :], ALU.add).then_inc(s_ev, 1)
                if g.live:
                    hold(dve, s_bn, g.t * 2 + 1)
                    dve.bn_aggr(stat[g.slot][:, 6:8], stat[g.slot][:, 0:6]).then_inc(s_bn, 1)
                if f.live:
                    dve.wait_ge(s_ln, f.t * 3 + 1)
                    if f.first >= R:
                        dve.wait_ge(s_xb, f.t - (R - 1))
                    dve.tensor_scalar(xn[f.slot][:, :], xin[f.slot][:, :], sf[:, 6:7], sf[:, 9:10],
                                      ALU.subtract, ALU.mult).then_inc(s_ln, 1)
                if c.live:
                    dve.tensor_tensor(kvr[:, D:KVW].rearrange("p (h c) -> p h c", h=H)[:, :, 0:HD],
                                      pkv[:, D:2 * D].rearrange("p (h c) -> p h c", h=H),
                                      bias[:, 2, :].rearrange("p (h c) -> p h c", h=H), ALU.add).then_inc(s_ev, 1)
                if f.live:
                    dve.wait_ge(s_ln, f.t * 3 + 2)
                    if f.first >= R:
                        dve.wait_ge(s_t, f.t - (R - 1))
                    dve.tensor_tensor(enh[f.slot][:, :], xn[f.slot][:, :], qe01[:, :], ALU.add).then_inc(s_ln, 1)
                if c.live:
                    if c.first >= R:
                        dve.wait_ge(s_tq, c.t - (R - 1))
                    dve.tensor_tensor(qrow[c.slot][:, :], psQ[c.slot % 2][:, 0:D], bias[:, 0, :], ALU.add
                                      ).then_inc(s_ev, 1)
            pipeline(dve, NT, 0, 4, R, 2 * R, step)

        @blk.tensor
        def _(pe):
            pe.wait_ge(s_w, 16 * 14)
            pe.transpose(psQT[:, 0:NREL], relraw[:, :], ident[0:NREL, 0:NREL]).then_inc(s_pb, 1)
            pe.wait_ge(s_set, 3 + 6 * len(chunks))
            pe.matmul(psT[:, 0:NG], cst("ones")[0:1, :], basef[0:1, :], start=True, stop=True).then_inc(s_pb, 1)
            pe.wait_ge(s_set, 3 + 6 * len(chunks) + 4)
            pe.matmul(psKV[0][0:1, 0:1], misfits[:, 0:1], cst("ones")[:, 0:1], start=True, stop=True
                      ).then_inc(s_pb, 1)
            pe.wait_ge(s_set, 3 + 6 * len(chunks) + 8)

            def step(T):
                g, m, c = T(2), T(3), T(5)
                if g.live:
                    pe.wait_ge(s_ln, g.t * 3 + 3)
                    if g.first >= 1:
                        pe.wait_ge(s_eT, g.t)
                    for a in range(DC):
                        mm = pe.transpose(psT[:, a * P:(a + 1) * P], enh[g.slot][:, a * P:(a + 1) * P], ident)
                    mm.then_inc(s_t, 1)
                if c.live:
                    pe.wait_ge(s_ev, c.t * 3 + 3)
                    if c.first >= 1:
                        pe.wait_ge(s_qT, c.t)
                    for a in range(DC):
                        mm = pe.transpose(psQT[:, a * P:(a + 1) * P], qrow[c.slot][:, a * P:(a + 1) * P], ident)
                    mm.then_inc(s_tq, 1)
                if m.live:
                    pe.wait_ge(s_eT, m.t + 1)
                    if m.first >= 2:
                        pe.wait_ge(s_ev, (m.t - 1) * 3)
                    for a in range(DC):
                        pe.matmul(psKV[m.slot % 2][:, :], enhT[m.slot][:, a, :], wkv[:, a, :],
                                  start=a == 0, stop=a == DC - 1)
                    for a in range(DC):
                        mm = pe.matmul(psQ[m.slot % 2][:, 0:D], enhT[m.slot][:, a, :], wq[:, a, :],
                                       start=a == 0, stop=a == DC - 1)
                    mm.then_inc(s_mm, 1)
            pipeline(pe, NT, 0, 5, R, 2 * R, step)


def start_over(nc, counters):
    nums = [c.num for c in counters]
    assert nums == list(range(nums[0], nums[0] + len(nums)))
    own = range(nums[0], nums[-1] + 1)
    nc.gpsimd.dma_reset(own)
    nc.all_engine_barrier(sems_to_clear=own)


def any_order_pass(nc, ctx, cst, io, dram, QT):
    def sb(name, shape, dt=F32):
        return ctx.enter_context(nc.sbuf_tensor(name, shape, dt))

    qrows = sb("g_qrows", [P, D])
    floor = sb("g_floor", [P, N * H // GE])
    zero = sb("g_zero", [P, 5 * H * CW])
    ends = sb("g_ends", [P, 3], I32)
    others_i = sb("g_others_i", [P, GE], I32)
    others = sb("g_others", [P, GE])
    own = sb("g_own", [P, 1])
    same = sb("g_same", [P, GE])
    far = sb("g_far", [P, GE])
    q = sb("g_q", [P, D])
    kv = sb("g_kv", [P, KVW])
    rel = sb("g_rel", [P, HD])
    keys = sb("g_keys", [P, D])
    prod = sb("g_prod", [P, D])
    score = sb("g_score", [P, H])
    spread = sb("g_spread", [P, H, GE])
    masked = sb("g_masked", [P, H, GE])
    best = sb("g_best", [P, 3, H])
    diff = sb("g_diff", [P, 2, H])
    factor = sb("g_factor", [P, 2, H])
    weighted = sb("g_weighted", [P, H * CW])
    old = sb("g_old", [P, H * CW])
    kept = sb("g_kept", [P, H * CW])
    new = sb("g_new", [P, H * CW])
    psB = ctx.enter_context(nc.psum_tensor("g_psB", [P, 512], F32))
    psS = ctx.enter_context(nc.psum_tensor("g_psS", [P, 512], F32))
    ident = cst("ident")
    heads = lambda a: a.rearrange("p (h c) -> p h c", h=H)

    nc.all_engine_barrier()
    with ExitStack() as c:
        laid, stored = c.enter_context(nc.semaphore("g_laid")), c.enter_context(nc.semaphore("g_stored"))
        with nc.Block() as blk:
            @blk.vector
            def _(dve):
                dve.memset(zero[:, :], 0.0).then_inc(laid, 1)
                dve.memset(floor[:, :], FLOOR).then_inc(laid, 1)

            @blk.sync
            def _(sp):
                sp.wait_ge(laid, 2)
                for j in range(10):
                    sp.dma_start(dram["agg"][j * 5 * P:(j + 1) * 5 * P].rearrange("(p a) h c -> p (a h c)", a=5),
                                 zero[:, :]).then_inc(stored, 16)
                sp.dma_start(dram["best"].rearrange("(p a) h -> p (a h)", p=GE), floor[0:GE, :]).then_inc(stored, 16)
                sp.wait_ge(stored, 16 * 11)

    with ExitStack() as c:
        turned, copied, stored = counters = [c.enter_context(nc.semaphore(f"g_q{n}")) for n in
                                             ("turned", "copied", "stored")]
        with nc.Fori(0, N // GE) as t:
            with nc.Block() as blk:
                @blk.vector
                def _(dve):
                    for a in range(DC):
                        dve.tensor_copy(prod[:, a * GE:(a + 1) * GE], QT[:, a, bass.ds(t * GE, GE)]).then_inc(copied, 1)
                    dve.wait_ge(turned, 1)
                    dve.tensor_copy(qrows[0:GE, :], psB[0:GE, 0:D]).then_inc(copied, 1)

                @blk.tensor
                def _(pe):
                    pe.wait_ge(copied, DC)
                    for a in range(DC):
                        mm = pe.transpose(psB[0:GE, a * P:(a + 1) * P], prod[:, a * GE:(a + 1) * GE], ident)
                    mm.then_inc(turned, 1)

                @blk.sync
                def _(sp):
                    sp.wait_ge(copied, DC + 1)
                    sp.dma_start(dram["q"][bass.ds(t * GE, GE), :], qrows[0:GE, :]).then_inc(stored, 16)
                    sp.wait_ge(stored, 16)
            start_over(nc, counters)

    with ExitStack() as c:
        loaded, gathered, stepped, weighed, summed, written = counters = [
            c.enter_context(nc.semaphore(f"g_{n}")) for n in
            ("loaded", "gathered", "stepped", "weighed", "summed", "written")]
        with nc.Fori(0, GS) as s:
            with nc.Block() as blk:
                @blk.sync
                def _(sp):
                    with nc.allow_non_contiguous_dma("one word of an edge on each partition"):
                        for j, name in enumerate(("src", "dst", "etype")):
                            sp.dma_start(ends[0:GE, j:j + 1], io[name][bass.ds(s * GE, GE)].rearrange(
                                "(p a) -> p a", a=1)).then_inc(loaded, 16)
                    sp.dma_start(others_i[0:GE, :], io["dst"][bass.ds(s * GE, GE)].rearrange(
                        "(a e) -> a e", a=1).to_broadcast([GE, GE])).then_inc(loaded, 16)
                    sp.wait_ge(loaded, 64)

                @blk.gpsimd
                def _(pool):
                    hold(pool, loaded, 64)
                    for out, table, j in ((q[0:GE, :], dram["q"], 1), (kv[0:GE, :], dram["kv"], 0),
                                          (rel[0:GE, :], io["rel"], 2), (best[0:GE, 1, :], dram["best"], 1),
                                          (old[0:GE, :], dram["agg"].rearrange("n h c -> n (h c)"), 1)):
                        pool.indirect_dma_start(out=out, out_offset=None, in_=table,
                                                in_offset=bass.IndirectOffsetOnAxis(ap=ends[0:GE, j:j + 1], axis=0)
                                                ).then_inc(gathered, 16)
                    hold(pool, stepped, 16)
                    for table, rows_ in ((dram["best"], best[0:GE, 2, :]),
                                         (dram["agg"].rearrange("n h c -> n (h c)"), new[0:GE, :])):
                        pool.indirect_dma_start(out=table, out_offset=bass.IndirectOffsetOnAxis(
                            ap=ends[0:GE, 1:2], axis=0), in_=rows_, in_offset=None).then_inc(written, 16)
                    pool.wait_ge(written, 32)

                @blk.vector
                def _(dve):
                    n = [0]

                    def link(ins):
                        n[0] += 1
                        ins.then_inc(stepped, 1)
                        dve.wait_ge(stepped, n[0])

                    dve.wait_ge(loaded, 64)
                    link(dve.tensor_copy(others[0:GE, :], others_i[0:GE, :]))
                    link(dve.tensor_copy(own[0:GE, :], ends[0:GE, 1:2]))
                    link(dve.tensor_scalar(same[0:GE, :], others[0:GE, :], own[0:GE, :], None, ALU.is_equal))
                    link(dve.tensor_scalar(far[0:GE, :], same[0:GE, :], -1.0, BIG, ALU.add, ALU.mult))
                    dve.wait_ge(gathered, 16 * 5)
                    link(dve.scalar_tensor_tensor(out=heads(keys[0:GE, :]),
                                                  in0=rel[0:GE, :].unsqueeze(1).to_broadcast([GE, H, HD]), scalar=0.2,
                                                  in1=heads(kv[0:GE, 0:D]), op0=ALU.mult, op1=ALU.add))
                    link(dve.tensor_tensor(prod[0:GE, :], keys[0:GE, :], q[0:GE, :], ALU.mult))
                    link(dve.tensor_reduce(score[0:GE, :], heads(prod[0:GE, :]), AX.X, ALU.add))
                    link(dve.tensor_tensor(spread[0:GE], ident[0:GE, 0:GE].unsqueeze(1).to_broadcast([GE, H, GE]),
                                           score[0:GE, :].unsqueeze(2).to_broadcast([GE, H, GE]), ALU.mult))
                    assert n[0] == 8
                    dve.wait_ge(summed, 1)
                    link(dve.tensor_tensor(masked[0:GE], psB[0:GE, 0:H * GE].rearrange("p (h e) -> p h e", h=H),
                                           far[0:GE, :].unsqueeze(1).to_broadcast([GE, H, GE]), ALU.add))
                    link(dve.tensor_reduce(best[0:GE, 0, :], masked[0:GE], AX.X, ALU.max))
                    link(dve.tensor_tensor(best[0:GE, 2, :], best[0:GE, 0, :], best[0:GE, 1, :], ALU.max))
                    link(dve.tensor_tensor(diff[0:GE, 0, :], score[0:GE, :], best[0:GE, 2, :], ALU.subtract))
                    link(dve.tensor_tensor(diff[0:GE, 1, :], best[0:GE, 1, :], best[0:GE, 2, :], ALU.subtract))
                    assert n[0] == 13
                    dve.wait_ge(weighed, 1)
                    wide = lambda a: a.unsqueeze(2).to_broadcast([GE, H, CW])
                    link(dve.tensor_tensor(heads(weighted[0:GE, :]), heads(kv[0:GE, D:KVW]),
                                           wide(factor[0:GE, 0, :]), ALU.mult))
                    link(dve.tensor_tensor(heads(kept[0:GE, :]), heads(old[0:GE, :]),
                                           wide(factor[0:GE, 1, :]), ALU.mult))
                    assert n[0] == 15
                    dve.wait_ge(summed, 2)
                    link(dve.tensor_tensor(new[0:GE, :], psS[0:GE, 0:H * CW], kept[0:GE, :], ALU.add))

                @blk.scalar
                def _(act):
                    act.wait_ge(stepped, 13)
                    act.activation(factor[0:GE], diff[0:GE], ACT.Exp, scale=SCALE).then_inc(weighed, 1)

                @blk.tensor
                def _(pe):
                    pe.wait_ge(stepped, 8)
                    pe.matmul(psB[0:GE, 0:H * GE], cst("ones")[0:GE, 0:GE],
                              spread[0:GE].rearrange("p h e -> p (h e)"), start=True, stop=True).then_inc(summed, 1)
                    pe.wait_ge(stepped, 14)
                    pe.matmul(psS[0:GE, 0:H * CW], same[0:GE, :], weighted[0:GE, :], start=True, stop=True
                              ).then_inc(summed, 1)
            start_over(nc, counters)


assert NT % RN == 0
CHAINS = dict(A=4, B=3, C=5, D=4, E=3, R=14, S=12)


def after_edges(nc, ctx, cst, io, dram, x1, slots, gap, rows, ints):
    def sb(name, shape, dt=F32):
        return ctx.enter_context(nc.sbuf_tensor(name, shape, dt))

    def sem(name):
        return ctx.enter_context(nc.semaphore(name))

    R = B = RN
    x = [sb(f"n_x{i}", [P, D]) for i in range(R)]
    xn = [sb(f"n_xn{i}", [P, D]) for i in range(R)]
    agg = [sb(f"n_agg{i}", [P, H * CW]) for i in range(R)]
    v = [sb(f"n_v{i}", [P, H * CW]) for i in range(R)]
    own = [sb(f"n_own{i}", [P, D]) for i in range(R)]
    msg = [sb(f"n_msg{i}", [P, D]) for i in range(R)]
    msgT = [sb(f"n_msgT{i}", [P, DC, P]) for i in range(R)]
    y = [sb(f"n_y{i}", [P, D]) for i in range(R)]
    h2 = [sb(f"n_h2{i}", [P, D]) for i in range(R)]
    h2T = [sb(f"n_h2T{i}", [P, DC, P]) for i in range(R)]
    x2 = [sb(f"n_x2{i}", [P, D]) for i in range(R)]
    x2all = sb("n_x2all", [P, NT, D])
    st = [sb(f"n_st{i}", [P, 3, 10]) for i in range(R)]
    den = [sb(f"n_den{i}", [P, 2, H]) for i in range(R)]
    lone = [sb(f"n_lone{i}", [P, H]) for i in range(R)]
    logit = sb("n_logit", [P, NT, NX])
    key = sb("n_key", [P, 4, B, NX])
    eq = sb("n_eq", [P, 2, B, NX])
    hot = sb("n_hot", [P, 2, B, NX])
    top = sb("n_top", [P, 4, B])
    both = sb("n_both", [P, NX, B])
    tot = sb("n_tot", [P, 3, NX * B])
    base = sb("n_base", [P, NX, B])
    pos = sb("n_pos", [P, NX, B])
    cand = sb("n_cand", [P, 2, B, NX])
    at = sb("n_at", [P, 2, B])
    slot = sb("n_slot", [P, 2, B], I32)
    run = sb("n_run", [P, NX])
    places = sb("n_places", [P, 2, NT])
    wo = sb("n_wo", [P, DC, D])
    wr = sb("n_wr", [P, DC, NX])
    vec = sb("n_vec", [P, 2, D])
    br = sb("n_br", [P, NX])
    zero = sb("n_zero", [P, 2 * D])
    beyond = sb("n_beyond", [P, 2 * NT, NX])
    shift = sb("n_shift", [P, 2 * NT])
    bl = sb("n_bl", [P, 8, NX])
    blk_gt = sb("n_gt", [P, NX, BPE])
    blk_ge = sb("n_ge", [1, NB, NX])
    blk_gn = sb("n_gn", [1, NB, NX])
    blk_r = sb("n_r", [1, 6, NB])
    psM = ctx.enter_context(nc.psum_tensor("n_psM", [P, 512], F32))
    psO = ctx.enter_context(nc.psum_tensor("n_psO", [P, 512], F32))
    psH = ctx.enter_context(nc.psum_tensor("n_psH", [P, 512], F32))
    psL = ctx.enter_context(nc.psum_tensor("n_psL", [P, 512], F32))
    psR = ctx.enter_context(nc.psum_tensor("n_psR", [P, 512], F32))
    ident = cst("ident")
    heads = lambda a: a.rearrange("p (h c) -> p h c", h=H)
    wide = lambda a: a.unsqueeze(2).to_broadcast([P, H, HD])

    s_w = sem("ns_w")
    s_in = [sem(f"ns_in{i}") for i in range(R)]
    s_sc = [sem(f"ns_sc{i}") for i in range(R)]
    s_tail = sem("ns_tail")
    s_z = sem("ns_z")
    s_pool = sem("ns_pool")
    s_c = {k: sem(f"ns_{k}") for k in CHAINS}
    s_sd = [sem(f"ns_sd{j}") for j in range(3)]
    s_mT = sem("ns_mT")
    s_hT = sem("ns_hT")
    s_x2 = sem("ns_x2")
    s_pm = sem("ns_pm")
    s_po = sem("ns_po")
    s_ph = sem("ns_ph")
    s_pl = sem("ns_pl")
    s_pr = sem("ns_pr")
    s_end = sem("ns_end")
    LAG = dict(A=0, M=1, B=2, C=3, D=4, L=5, E=6, R=7, S=8)
    SCAT = 6 + LAG["S"] + 1

    def chain(dve, name, count, ops):
        assert len(ops) == CHAINS[name], (name, len(ops))
        for k, op in enumerate(ops):
            alone = isinstance(op, tuple)
            if k and alone:
                hold(dve, s_c[name], count + k)
            elif k:
                dve.wait_ge(s_c[name], count + k)
            (op[0] if alone else op)().then_inc(s_c[name], 1)
            yield

    with nc.Block() as blk:
        @blk.sync
        def _(sp):
            for a in range(DC):
                sp.dma_start(wo[:, a, :], io["Wo"][a * P:(a + 1) * P, :]).then_inc(s_w, 16)
                sp.dma_start(wr[:, a, :], io["Wr"][a * P:(a + 1) * P, :]).then_inc(s_w, 16)
            for j, name in enumerate(("gamma", "beta")):
                sp.dma_start(vec[:, j, :], io[name].rearrange("(a d) -> a d", a=1).to_broadcast([P, D])
                             ).then_inc(s_w, 16)
            sp.dma_start(br[:, :], io["br"].rearrange("(a d) -> a d", a=1).to_broadcast([P, NX])).then_inc(s_w, 16)

            def step(T):
                g = T(0)
                r0 = bass.ds(node_rows(g.t), P)
                if g.first >= R:
                    hold(sp, s_c["C"], (g.t - (R - 1)) * CHAINS["C"])
                sp.dma_start(agg[g.slot][:, :], dram["agg"][r0].rearrange("n h c -> n (h c)")
                             ).then_inc(s_in[g.slot], 16)
                sp.dma_start(v[g.slot][:, :], dram["kv"][r0, D:KVW]).then_inc(s_in[g.slot], 16)
                sp.dma_start(xn[g.slot][:, :], dram["xn"][r0, :]).then_inc(s_in[g.slot], 16)
                sp.dma_start(x[g.slot][:, :], io["x"][r0, :]).then_inc(s_in[g.slot], 16)
            pipeline(sp, NT - 1, 0, 0, R, R, step)
            step(lambda off: Tile(NT - 1, (NT - 1) % R, (NT - 1) // R, True, NT - 1))
            sp.wait_ge(s_end, 2)
            for e in range(NX):
                n = sp.value_load(ints[0:1, e:e + 1], min_val=0, max_val=N)
                sp.dma_start(dram["xs"][bass.ds(n + e * CAP, BT), :].rearrange("(p a) c -> p (a c)", a=2),
                             zero[:, :]).then_inc(s_tail, 16)
            sp.wait_ge(s_tail, 16 * NX)
            for i in range(R):
                sp.wait_ge(s_sc[i], 32 * len(range(i, NT, R)))

        @blk.gpsimd
        def _(pool):
            pool.wait_ge(s_w, 16 * 7)

            def step(T):
                g = T(0)
                if g.live:
                    i = g.slot
                    hold(pool, s_in[i], (g.rnd + 1) * 64)
                    pool.tensor_scalar(lone[i][:, :], heads(agg[i][:, :])[:, :, HD], 0.0, None, ALU.is_equal
                                       ).then_inc(s_pool, 1)
                    pool.wait_ge(s_pool, g.t * 3 + 1)
                    pool.tensor_tensor(heads(own[i][:, :]), heads(v[i][:, :])[:, :, 0:HD], wide(lone[i][:, :]),
                                       ALU.mult).then_inc(s_pool, 1)
                    pool.tensor_tensor(x[i][:, :], x[i][:, :], vec[:, 1, :], ALU.add).then_inc(s_pool, 1)
                o = T(SCAT)
                if o.live:
                    pool.wait_ge(s_c["S"], (o.rnd + 1) * CHAINS["S"])
                    hold(pool, s_x2, o.t + 1)
                    for k in range(2):
                        pool.indirect_dma_start(
                            out=dram["xs"][:, :], out_offset=bass.IndirectOffsetOnAxis(
                                ap=slot[:, k, o.slot:o.slot + 1], axis=0),
                            in_=x2[o.slot][:, :], in_offset=None).then_inc(s_sc[o.slot], 16)
            pipeline(pool, NT, 0, SCAT, R, 3 * R, step)

        @blk.scalar
        def _(act):
            act.preload_act_table(ACT.Sqrt)

            def step(T):
                def sqrt(j, g, name, steps):
                    act.wait_ge(s_c[name], g.t * CHAINS[name] + steps)
                    act.activation(st[g.slot][:, j, 8:9], st[g.slot][:, j, 7:8], ACT.Sqrt, bias=cst("eps")
                                   ).then_inc(s_sd[j], 1)
                a, l, o = T(LAG["M"]), T(LAG["L"]), T(SCAT - 1)
                if a.live:
                    act.wait_ge(s_pm, a.t + 1)
                    act.copy(msgT[a.slot][:, :, :].rearrange("p a q -> p (a q)"), psM[:, 0:D]).then_inc(s_mT, 1)
                if l.live:
                    act.wait_ge(s_ph, l.t + 1)
                    act.copy(h2T[l.slot][:, :, :].rearrange("p a q -> p (a q)"), psH[:, 0:D]).then_inc(s_hT, 1)
                if o.live:
                    act.wait_ge(s_c["E"], (o.t + 1) * CHAINS["E"])
                    if o.first >= R:
                        act.wait_ge(s_sc[o.slot], o.rnd * 32)
                    act.copy(x2[o.slot][:, :], x2all[:, bass.ds(o.t, 1), :].rearrange("p a d -> p (a d)")
                             ).then_inc(s_x2, 1)
                for j, name in ((0, "B"), (2, "D"), (1, "C")):
                    if T(LAG[name]).live:
                        sqrt(j, T(LAG[name]), name, CHAINS[name])
            pipeline(act, NT, 0, SCAT - 1, R, 3 * R, step)

        @blk.vector
        def _(dve):
            dve.memset(zero[:, :], 0.0).then_inc(s_z, 1)
            dve.tensor_copy(run[:, :], cst("cap8")).then_inc(s_z, 1)
            dve.wait_ge(s_z, 2)
            dve.wait_ge(s_w, 16 * 7)
            whole = lambda a, t: a[:, bass.ds(t, 1), :].rearrange("p a d -> p (a d)")


            def after(sem_, value, op):
                def lay():
                    dve.wait_ge(sem_, value)
                    return op()
                return lay

            def stats(j, i, inp):
                return [(lambda: dve.bn_stats(st[i][:, j, 0:6], inp),) if j == 1 else
                        lambda: dve.bn_stats(st[i][:, j, 0:6], inp),
                        (lambda: dve.bn_aggr(st[i][:, j, 6:8], st[i][:, j, 0:6]),)]

            def normed(j, g, out, inp):
                i = g.slot
                return [after(s_sd[j], g.t + 1, lambda: dve.reciprocal(st[i][:, j, 9:10], st[i][:, j, 8:9])),
                        lambda: dve.tensor_scalar(out, inp, st[i][:, j, 6:7], st[i][:, j, 9:10],
                                                  ALU.subtract, ALU.mult)]

            def messages(g):
                i = g.slot
                sums = heads(agg[i][:, :])
                return [
                    after(s_in[i], (g.rnd + 1) * 64, lambda: dve.scalar_tensor_tensor(
                        out=den[i][:, 0, :], in0=sums[:, :, HD], scalar=0.0, in1=sums[:, :, HD],
                        op0=ALU.is_equal, op1=ALU.add)),
                    lambda: dve.reciprocal(den[i][:, 1, :], den[i][:, 0, :]),
                    lambda: dve.tensor_tensor(heads(msg[i][:, :]), sums[:, :, 0:HD], wide(den[i][:, 1, :]), ALU.mult),
                    after(s_pool, g.t * 3 + 2,
                          lambda: dve.tensor_tensor(msg[i][:, :], msg[i][:, :], own[i][:, :], ALU.add))]

            def projected(g):
                i = g.slot
                return [after(s_po, g.t + 1,
                              lambda: dve.tensor_tensor(y[i][:, :], psO[:, 0:D], xn[i][:, :], ALU.add))
                        ] + stats(0, i, y[i][:, :])

            def attended(g):
                i, x1t = g.slot, whole(x1, g.t)
                inv, _ = normed(0, g, None, None)
                return [inv,
                        lambda: dve.scalar_tensor_tensor(out=y[i][:, :], in0=y[i][:, :], scalar=st[i][:, 0, 6:7],
                                                         in1=vec[:, 0, :], op0=ALU.subtract, op1=ALU.mult),
                        after(s_pool, g.t * 3 + 3, lambda: dve.scalar_tensor_tensor(
                            out=x1t, in0=y[i][:, :], scalar=st[i][:, 0, 9:10], in1=x[i][:, :],
                            op0=ALU.mult, op1=ALU.add))] + stats(1, i, x1t)

            def second(g):
                i = g.slot
                return normed(1, g, h2[i][:, :], whole(x1, g.t)) + stats(2, i, h2[i][:, :])

            def third(g):
                return normed(2, g, whole(x2all, g.t), h2[g.slot][:, :]) + [
                    after(s_pl, g.t + 1,
                          lambda: dve.tensor_tensor(whole(logit, g.t), psL[:, 0:NX], br[:, :], ALU.add))]

            flat = lambda a: a.rearrange("p e t -> p (e t)")
            by_tile = lambda a: a.rearrange("p e t -> p t e")

            def chosen(g):
                end = isinstance(g.t, int) and g.t == NT - 1
                lg = logit[:, bass.ds(g.t - (B - 1), B), :]
                now = bass.ds(g.t - (B - 1), B)
                bc = lambda a: a.unsqueeze(2).to_broadcast([P, B, NX])
                rank = cst("rank8").unsqueeze(1).to_broadcast([P, B, NX])

                def best(k, src):
                    return [after(s_c["E"], (g.t + 1) * CHAINS["E"],
                                  lambda: dve.tensor_reduce(top[:, 2 * k, :], src, AX.X, ALU.max)),
                            lambda: dve.tensor_tensor(eq[:, k, :, :], src, bc(top[:, 2 * k, :]), ALU.is_equal),
                            lambda: dve.tensor_tensor(key[:, k, :, :], eq[:, k, :, :], rank, ALU.mult),
                            lambda: dve.tensor_reduce(top[:, 2 * k + 1, :], key[:, k, :, :], AX.X, ALU.max),
                            lambda: dve.tensor_tensor(hot[:, k, :, :], key[:, k, :, :], bc(top[:, 2 * k + 1, :]),
                                                      ALU.is_equal)]
                kept = cst("lastrows") if end else cst("ones")[:, 0:1]
                tiles = hot[:, :, B - 1:B, :]

                return best(0, lg) + [
                    lambda: dve.scalar_tensor_tensor(out=key[:, 2, :, :], in0=hot[:, 0, :, :], scalar=-BIG, in1=lg,
                                                     op0=ALU.mult, op1=ALU.add)
                ] + best(1, key[:, 2, :, :]) + [
                    lambda: dve.tensor_tensor(gap[:, now], top[:, 2, :], top[:, 0, :], ALU.subtract),
                    lambda: dve.tensor_scalar(tiles, tiles, kept, None, ALU.mult),
                    lambda: dve.tensor_tensor(by_tile(both[:, :, :]), hot[:, 0, :, :], hot[:, 1, :, :], ALU.add)]

            def placed(g):
                end = isinstance(g.t, int) and g.t == NT - 1
                now = bass.ds(g.t - (B - 1), B)

                def free_slots():
                    for sc in s_sc:
                        if g.first >= B:
                            dve.wait_ge(sc, g.rnd * 32)
                    return dve.tensor_copy(slot[:, :, :], at[:, :, :])

                return [
                    after(s_pr, g.rnd + 1, lambda: dve.tensor_copy(tot[:, 0, :], psR[:, NX * B:2 * NX * B])),
                    lambda: dve.tensor_tensor_scan(tot[:, 1, :], cst("restart"), tot[:, 0, :], 0.0, ALU.mult, ALU.add),
                    lambda: dve.tensor_tensor(tot[:, 2, :], tot[:, 1, :], tot[:, 0, :], ALU.subtract),
                    lambda: dve.tensor_tensor(base[:, :, :], tot[:, 2, :].rearrange("p (e t) -> p e t", t=B),
                                              run[:, :].unsqueeze(2).to_broadcast([P, NX, B]), ALU.add),
                    lambda: dve.tensor_tensor(flat(pos[:, :, :]), psR[:, 0:NX * B], flat(base[:, :, :]), ALU.add),
                    lambda: dve.tensor_tensor(run[:, :], run[:, :],
                                              tot[:, 1, :].rearrange("p (e t) -> p e t", t=B)[:, :, B - 1], ALU.add),
                    lambda: dve.tensor_tensor(cand[:, 0, :, :], by_tile(pos[:, :, :]), hot[:, 0, :, :], ALU.mult),
                    lambda: dve.tensor_tensor(cand[:, 1, :, :], by_tile(pos[:, :, :]), hot[:, 1, :, :], ALU.mult),
                    lambda: dve.tensor_reduce(at[:, :, :], cand[:, :, :, :], AX.X, ALU.add),
                    lambda: dve.tensor_tensor(at[:, :, B - 1], at[:, :, B - 1], cst("spare" if end else "nospare"),
                                              ALU.add),
                    lambda: dve.tensor_copy(places[:, :, now], at[:, :, :]),
                    free_slots]

            def step(T):
                parts = [chain(dve, name, g.t * CHAINS[name], ops(g)) for name, ops in (
                    ("B", projected), ("A", messages), ("E", third), ("C", attended), ("D", second))
                    for g in (T(LAG[name]),) if g.live]
                g = T(LAG["R"])
                if g.live and g.slot == B - 1:
                    picks = chain(dve, "R", g.rnd * CHAINS["R"], chosen(g))
                    parts = [picks] + parts[0:2] + [picks] + parts[2:4] + [picks] + parts[4:]
                g = T(LAG["S"])
                if g.live and g.slot == B - 1:
                    puts = chain(dve, "S", g.rnd * CHAINS["S"], placed(g))
                    parts = parts[0:2] + [puts] + parts[2:4] + [puts] + parts[4:] + [puts]
                while parts:
                    parts = [p for p in parts if next(p, "end") != "end"]
            pipeline(dve, NT, 0, LAG["S"], R, 3 * R, step)

            c = [0]

            def link(ins):
                c[0] += 1
                ins.then_inc(s_end, 1)
                dve.wait_ge(s_end, c[0])
            dve.wait_ge(s_c["S"], NT // B * CHAINS["S"])
            link(dve.tensor_tensor(bl[:, 3, :], run[:, :], cst("cap8"), ALU.subtract))
            link(dve.tensor_copy(ints[0:1, 0:NX], bl[0:1, 3, :]))
            steps = cst("steps")[0:1, :]
            link(dve.tensor_tensor(blk_gt[:, :, :], bl[:, 3, :].unsqueeze(2).to_broadcast([P, NX, BPE]),
                                   cst("fills").unsqueeze(1).to_broadcast([P, NX, BPE]), ALU.is_gt))
            link(dve.tensor_reduce(bl[:, 0, :], blk_gt[:, :, :], AX.X, ALU.add))
            link(dve.tensor_scalar(bl[:, 2, :], bl[:, 0, :], float(BT), float(-CAP), ALU.mult, ALU.add))
            flat = places[:, :, :].rearrange("p k t -> p (k t)")
            link(dve.tensor_tensor(beyond[:, :, 0:NX - 1], flat.unsqueeze(2).to_broadcast([P, 2 * NT, NX - 1]),
                                   cst("cap8")[:, 1:NX].unsqueeze(1).to_broadcast([P, 2 * NT, NX - 1]), ALU.is_ge))
            link(dve.tensor_tensor(beyond[:, :, 0:NX - 1], beyond[:, :, 0:NX - 1],
                                   bl[:, 2:3, 0:NX - 1].to_broadcast([P, 2 * NT, NX - 1]), ALU.mult))
            link(dve.tensor_reduce(shift[:, :], beyond[:, :, 0:NX - 1], AX.X, ALU.add))
            link(dve.tensor_tensor(flat, flat, shift[:, :], ALU.add))
            link(dve.tensor_scalar(slots[:, :, :].rearrange("p k t -> p (k t)"), flat, float(NB * BT - 1), None,
                                   ALU.min))
            link(dve.tensor_tensor_scan(bl[0:1, 1, :], cst("ones")[0:1, 0:NX], bl[0:1, 0, :], 0.0, ALU.mult, ALU.add))
            link(dve.tensor_tensor(blk_ge[0:1], steps.unsqueeze(2).to_broadcast([1, NB, NX]),
                                   bl[0:1, 1:2, :].to_broadcast([1, NB, NX]), ALU.is_ge))
            link(dve.tensor_tensor(blk_gn[0:1], blk_ge[0:1], bl[0:1, 0:1, :].to_broadcast([1, NB, NX]), ALU.mult))
            link(dve.tensor_reduce(blk_r[0:1, 1, :], blk_ge[0:1], AX.X, ALU.add))
            link(dve.tensor_reduce(blk_r[0:1, 2, :], blk_gn[0:1], AX.X, ALU.add))
            link(dve.tensor_tensor(blk_r[0:1, 3, :], steps, blk_r[0:1, 2, :], ALU.subtract))
            link(dve.tensor_scalar(blk_r[0:1, 4, :], blk_r[0:1, 3, :], float(BT), None, ALU.mult))
            link(dve.tensor_scalar(blk_r[0:1, 5, :], blk_r[0:1, 1, :], float(CAP), None, ALU.mult))
            link(dve.tensor_tensor(blk_r[0:1, 2, :], blk_r[0:1, 4, :], blk_r[0:1, 5, :], ALU.add))
            link(dve.tensor_scalar(rows[0:1, NB:2 * NB], blk_r[0:1, 2, :], float(NX * CAP + BT), None, ALU.min))
            link(dve.tensor_scalar(rows[0:1, 0:NB], blk_r[0:1, 1, :], float(NX - 1), None, ALU.min))

        @blk.tensor
        def _(pe):
            pe.wait_ge(s_w, 16 * 7)

            def step(T):
                a, d, g = T(LAG["M"]), T(LAG["L"]), T(LAG["R"])
                if a.live:
                    pe.wait_ge(s_c["A"], (a.t + 1) * CHAINS["A"])
                    if a.first >= 1:
                        pe.wait_ge(s_mT, a.t)
                    for b in range(DC):
                        mm = pe.transpose(psM[:, b * P:(b + 1) * P], msg[a.slot][:, b * P:(b + 1) * P], ident)
                    mm.then_inc(s_pm, 1)
                if d.live:
                    pe.wait_ge(s_c["D"], d.t * CHAINS["D"] + 2)
                    if d.first >= 1:
                        pe.wait_ge(s_hT, d.t)
                    for b in range(DC):
                        mm = pe.transpose(psH[:, b * P:(b + 1) * P], h2[d.slot][:, b * P:(b + 1) * P], ident)
                    mm.then_inc(s_ph, 1)
                if a.live:
                    pe.wait_ge(s_mT, a.t + 1)
                    if a.first >= 1:
                        pe.wait_ge(s_c["B"], (a.t - 1) * CHAINS["B"] + 1)
                    for b in range(DC):
                        mm = pe.matmul(psO[:, 0:D], msgT[a.slot][:, b, :], wo[:, b, :], start=b == 0, stop=b == DC - 1)
                    mm.then_inc(s_po, 1)
                if d.live:
                    pe.wait_ge(s_hT, d.t + 1)
                    if d.first >= 1:
                        pe.wait_ge(s_c["E"], d.t * CHAINS["E"])
                    for b in range(DC):
                        mm = pe.matmul(psL[:, 0:NX], h2T[d.slot][:, b, :], wr[:, b, :], start=b == 0, stop=b == DC - 1)
                    mm.then_inc(s_pl, 1)
                if g.live and g.slot == B - 1:
                    pe.wait_ge(s_c["R"], (g.rnd + 1) * CHAINS["R"])
                    chosen = both[:, :, :].rearrange("p e t -> p (e t)")
                    pe.matmul(psR[:, 0:NX * B], cst("before"), chosen, start=True, stop=True)
                    pe.matmul(psR[:, NX * B:2 * NX * B], cst("ones"), chosen, start=True, stop=True).then_inc(s_pr, 1)
            pipeline(pe, NT, 0, LAG["R"], R, 2 * R, step)


def experts(nc, ctx, cst, io, dram, rows):
    def sb(name, shape, dt=F32):
        return ctx.enter_context(nc.sbuf_tensor(name, shape, dt))

    def sem(name):
        return ctx.enter_context(nc.semaphore(name))

    R = 3
    A = BT // P
    xs = [sb(f"f_xs{i}", [P, A, D]) for i in range(R)]
    xT = [sb(f"f_xT{i}", [P, DC, BT]) for i in range(R)]
    w1 = [sb(f"f_w1{i}", [P, DC, FF]) for i in range(R)]
    w2 = [sb(f"f_w2{i}", [P, FC, D]) for i in range(R)]
    y = [sb(f"f_y{i}", [P, A, D]) for i in range(R)]
    hT = sb("f_hT", [P, FC, BT])
    lnraw = sb("f_lnraw", [2 * NX, D])
    ln = sb("f_ln", [P, DC, 2 * NX])
    b1raw = sb("f_b1raw", [NX * FC, P])
    b1 = sb("f_b1", [P, NX * FC])
    b2 = sb("f_b2", [P, NX * D])
    psT = ctx.enter_context(nc.psum_tensor("f_psT", [P, 512], F32))
    psH = ctx.enter_context(nc.psum_tensor("f_psH", [P, 4, 512], F32))
    psY = ctx.enter_context(nc.psum_tensor("f_psY", [P, A, 512], F32))
    ident = cst("ident")

    s_c = sem("fs_c")
    s_cp = sem("fs_cp")
    s_cv = sem("fs_cv")
    s_r = [sem(f"fs_r{i}") for i in range(R)]
    s_w1 = [sem(f"fs_w1{i}") for i in range(R)]
    s_w2 = [sem(f"fs_w2{i}") for i in range(R)]
    s_y = [sem(f"fs_y{i}") for i in range(R)]
    s_t = sem("fs_t")
    s_xT = sem("fs_xT")
    s_h = sem("fs_h")
    s_g = sem("fs_g")
    s_p = sem("fs_p")
    s_e = sem("fs_e")

    with nc.Block() as blk:
        @blk.sync
        def _(sp):
            sp.dma_start(lnraw[0:NX, :], io["ln_g"]).then_inc(s_c, 16)
            sp.dma_start(lnraw[NX:2 * NX, :], io["ln_b"]).then_inc(s_c, 16)
            sp.dma_start(b1raw[:, :], io["b1"].rearrange("e (c p) -> (e c) p", p=P)).then_inc(s_c, 16)
            sp.dma_start(b2[:, :], io["b2"].rearrange("(a e) d -> a (e d)", a=1).to_broadcast([P, NX * D])
                         ).then_inc(s_c, 16)

            def step(T):
                g = T(0)
                if g.live:
                    e = sp.value_load(rows[0:1, bass.ds(g.t, 1)], min_val=0, max_val=NX - 1)
                    r0 = sp.value_load(rows[0:1, bass.ds(g.t + NB, 1)], min_val=0, max_val=NX * CAP + BT)
                    if g.first >= R:
                        hold(sp, s_p, g.t * A - A * (R - 1))
                    sp.dma_start(xs[g.slot][:, :, :], dram["xs"][bass.ds(r0, BT), :].rearrange(
                        "(a p) c -> p a c", p=P)).then_inc(s_r[g.slot], 16)
                    sp.dma_start(w1[g.slot][:, :, :], io["W1"][bass.ds(e, 1)].rearrange(
                        "e (a p) f -> p (e a) f", p=P)).then_inc(s_w1[g.slot], 16)
                    sp.dma_start(w2[g.slot][:, :, :], io["W2"][bass.ds(e, 1)].rearrange(
                        "e (c p) d -> p (e c) d", p=P)).then_inc(s_w2[g.slot], 16)
                o = T(2)
                if o.live:
                    hold(sp, s_e, o.t * A + A)
                    sp.dma_start(dram["ys"][bass.ds(o.t * BT, BT), :].rearrange("(a p) c -> p a c", p=P),
                                 y[o.slot][:, :, :]).then_inc(s_y[o.slot], 16)
            pipeline(sp, NB, 0, 2, R, 5, step)
            for i in range(R):
                sp.wait_ge(s_y[i], 16 * len(range(i, NB, R)))

        @blk.scalar
        def _(act):
            act.preload_act_table(ACT.Gelu)
            act.wait_ge(s_cv, 2)

            def step(T):
                g = T(0)
                e = act.value_load(rows[0:1, bass.ds(g.t, 1)], min_val=0, max_val=NX - 1)
                for c in range(FC):
                    act.wait_ge(s_h, g.t * FC + c + 1)
                    if c == 0 and g.first >= 1:
                        act.wait_ge(s_p, g.t * A)
                    act.activation(hT[:, c, :], psH[:, c % 4, 0:BT], ACT.Gelu,
                                   bias=b1[:, bass.ds(e * FC + c, 1)]).then_inc(s_g, 1)
            pipeline(act, NB, 0, 0, R, 5, step)

        @blk.vector
        def _(dve):
            dve.wait_ge(s_cp, 2)
            dve.tensor_copy(ln[:, :, :], psT[:, 0:DC * 2 * NX].rearrange("p (a e) -> p a e", a=DC)).then_inc(s_cv, 1)
            dve.tensor_copy(b1[:, :], psY[:, 0, 0:NX * FC]).then_inc(s_cv, 1)
            dve.wait_ge(s_cv, 2)
            dve.wait_ge(s_c, 64)

            def step(T):
                g = T(0)
                if g.live:
                    e = dve.value_load(rows[0:1, bass.ds(g.t, 1)], min_val=0, max_val=NX - 1)
                    dve.wait_ge(s_t, g.t + 1)
                    if g.first >= R:
                        dve.wait_ge(s_h, g.t * FC - FC * (R - 1))
                    for a in range(DC):
                        dve.tensor_scalar(xT[g.slot][:, a, :], psT[:, a * BT:(a + 1) * BT],
                                          ln[:, a, bass.ds(e, 1)], ln[:, a, bass.ds(e + NX, 1)],
                                          ALU.mult, ALU.add).then_inc(s_xT, 1)
                c = T(1)
                if c.live:
                    e1 = dve.value_load(rows[0:1, bass.ds(c.t, 1)], min_val=0, max_val=NX - 1)
                    if c.first >= R:
                        dve.wait_ge(s_y[c.slot], c.rnd * 16)
                    for a in range(A):
                        dve.wait_ge(s_p, c.t * A + a + 1)
                        dve.tensor_tensor(y[c.slot][:, a, :], psY[:, a, 0:D], b2[:, bass.ds(e1 * D, D)], ALU.add
                                          ).then_inc(s_e, 1)
            pipeline(dve, NB, 0, 1, R, 5, step)

        @blk.tensor
        def _(pe):
            pe.wait_ge(s_c, 64)
            for a in range(DC):
                mm = pe.transpose(psT[:, a * 2 * NX:(a + 1) * 2 * NX], lnraw[:, a * P:(a + 1) * P],
                                  ident[0:2 * NX, 0:2 * NX])
            mm.then_inc(s_cp, 1)
            pe.transpose(psY[:, 0, 0:NX * FC], b1raw[:, :], ident[0:NX * FC, 0:NX * FC]).then_inc(s_cp, 1)
            pe.wait_ge(s_cv, 2)

            def step(T):
                g = T(0)
                if g.live:
                    pe.wait_ge(s_r[g.slot], (g.rnd + 1) * 16)
                    if g.first >= 1:
                        pe.wait_ge(s_xT, g.t * DC)
                    for a in range(DC):
                        for t in range(A):
                            mm = pe.transpose(psT[:, a * BT + t * P:a * BT + (t + 1) * P],
                                              xs[g.slot][:, t, a * P:(a + 1) * P], ident)
                    mm.then_inc(s_t, 1)
                c = T(1)
                if c.live:
                    pe.wait_ge(s_w2[c.slot], (c.rnd + 1) * 16)
                    for t in range(A):
                        if c.first >= 1:
                            pe.wait_ge(s_e, c.t * A - A + t + 1)
                        for f in range(FC):
                            if t == 0:
                                pe.wait_ge(s_g, c.t * FC + f + 1)
                            mm = pe.matmul(psY[:, t, 0:D], hT[:, f, t * P:(t + 1) * P], w2[c.slot][:, f, :],
                                           start=f == 0, stop=f == FC - 1)
                        mm.then_inc(s_p, 1)
                if g.live:
                    pe.wait_ge(s_w1[g.slot], (g.rnd + 1) * 16)
                    pe.wait_ge(s_xT, g.t * DC + DC)
                    for f in range(FC):
                        if g.first >= 1 or f >= 4:
                            pe.wait_ge(s_g, g.t * FC + f - 3)
                        for a in range(DC):
                            mm = pe.matmul(psH[:, f % 4, 0:BT], w1[g.slot][:, a, f * P:(f + 1) * P],
                                           xT[g.slot][:, a, :], start=a == 0, stop=a == DC - 1)
                        mm.then_inc(s_h, 1)
            pipeline(pe, NB, 0, 1, R, 5, step)


def combine(nc, ctx, cst, dram, out, x1, slots, gap):
    def sb(name, shape, dt=F32):
        return ctx.enter_context(nc.sbuf_tensor(name, shape, dt))

    def sem(name):
        return ctx.enter_context(nc.semaphore(name))

    R = 3
    idx = [sb(f"c_idx{i}", [P, 2], I32) for i in range(R)]
    yy = [sb(f"c_y{i}", [P, 2, D]) for i in range(R)]
    one = [sb(f"c_one{i}", [P, D]) for i in range(R)]
    two = [sb(f"c_two{i}", [P, D]) for i in range(R)]
    ex = sb("c_ex", [P, NT])
    sm = sb("c_sm", [P, NT])
    wa = sb("c_wa", [P, NT])
    wb = sb("c_wb", [P, NT])
    s_e = sem("cs_e")
    s_s = sem("cs_s")
    s_i = sem("cs_i")
    s_y = [sem(f"cs_y{i}") for i in range(R)]
    s_v = sem("cs_v")
    s_o = [sem(f"cs_o{i}") for i in range(R)]

    with nc.Block() as blk:
        @blk.scalar
        def _(act):
            act.activation(ex[:, :], gap[:, :], ACT.Exp).then_inc(s_e, 1)

        @blk.vector
        def _(dve):
            dve.wait_ge(s_e, 1)
            dve.tensor_scalar(sm[:, :], ex[:, :], 1.0, None, ALU.add).then_inc(s_s, 1)
            dve.wait_ge(s_s, 1)
            dve.reciprocal(wa[:, :], sm[:, :]).then_inc(s_s, 1)
            dve.wait_ge(s_s, 2)
            dve.tensor_tensor(wb[:, :], wa[:, :], ex[:, :], ALU.mult).then_inc(s_s, 1)
            dve.wait_ge(s_s, 3)

            def step(T):
                g = T(0)
                if g.live:
                    if g.first >= R:
                        dve.wait_ge(s_y[g.slot], g.rnd * 32)
                    dve.tensor_copy(idx[g.slot][:, :], slots[:, :, bass.ds(g.t, 1)].rearrange("p k a -> p (k a)")
                                    ).then_inc(s_i, 1)
                c = T(2)
                if c.live:
                    i = c.slot
                    dve.wait_ge(s_y[i], (c.rnd + 1) * 32)
                    dve.scalar_tensor_tensor(out=one[i][:, :], in0=yy[i][:, 0, :], scalar=wa[:, bass.ds(c.t, 1)],
                                             in1=x1[:, bass.ds(c.t, 1), :].rearrange("p a d -> p (a d)"),
                                             op0=ALU.mult, op1=ALU.add).then_inc(s_v, 1)
                    dve.wait_ge(s_v, c.t * 2 + 1)
                    if c.first >= R:
                        dve.wait_ge(s_o[i], c.rnd * 16)
                    dve.scalar_tensor_tensor(out=two[i][:, :], in0=yy[i][:, 1, :], scalar=wb[:, bass.ds(c.t, 1)],
                                             in1=one[i][:, :], op0=ALU.mult, op1=ALU.add).then_inc(s_v, 1)
            pipeline(dve, NT, 0, 2, R, 6, step)

        @blk.gpsimd
        def _(pool):
            def step(T):
                g = T(0)
                if g.first >= R:
                    hold(pool, s_v, g.t * 2 - 2 * (R - 1))
                hold(pool, s_i, g.t + 1)
                for k in range(2):
                    pool.indirect_dma_start(out=yy[g.slot][:, k, :], out_offset=None, in_=dram["ys"][:, :],
                                            in_offset=bass.IndirectOffsetOnAxis(ap=idx[g.slot][:, k:k + 1], axis=0)
                                            ).then_inc(s_y[g.slot], 16)
            pipeline(pool, NT, 0, 0, R, 6, step)

        @blk.sync
        def _(sp):
            def step(T):
                o = T(2)
                if o.live:
                    hold(sp, s_v, o.t * 2 + 2)
                    lo, r = own_rows(o.t)
                    sp.dma_start(out[r, :], two[o.slot][lo:P, :]
                                 ).then_inc(s_o[o.slot], 16)
            pipeline(sp, NT, 0, 2, R, 6, step)
            for i in range(R):
                sp.wait_ge(s_o[i], 16 * len(range(i, NT, R)))


def build(nc, io, out):
    dram = {name: nc.dram_tensor(f"d_{name}", shape, dt, kind="Internal").ap() for name, shape, dt in (
        ("kv", (N, KVW), F32), ("xn", (N, D), F32), ("src", (NG, G), I32),
        ("featx", (NG, G), BF16), ("featt", (NG, G), BF16), ("agg", (AR, H, CW), F32),
        ("xs", (NX * CAP + 2 * BT, D), F32), ("ys", (NB * BT, D), F32),
        ("q", (N, D), F32), ("best", (N, H), F32))}
    with ExitStack() as whole:
        def sb(name, shape, dt=F32):
            return whole.enter_context(nc.sbuf_tensor(name, shape, dt))
        consts = sb("consts", list(CONSTS.shape))
        slots = sb("slots", [P, 2, NT], I32)
        gap = sb("gap", [P, NT])
        rows = sb("rows", [1, 2 * NB], I32)
        unfit = sb("unfit", [1, 1], I32)
        ints = sb("ints", [1, NX], I32)
        loaded = whole.enter_context(nc.semaphore("loaded"))

        def cst(name):
            return consts[:, CAT[name][0]:CAT[name][1]]

        with nc.Block() as blk:
            @blk.sync
            def _(sp):
                sp.dma_start(consts[:, :], io["consts"]).then_inc(loaded, 16)
                sp.wait_ge(loaded, 16)
        with ExitStack() as ctx:
            def sb1(name, shape, dt=F32):
                return ctx.enter_context(nc.sbuf_tensor(name, shape, dt))
            QT = sb1("QT", [P, DC, QW])
            bases = sb1("bases", [1, NG], I32)
            flag = sb1("flag", [P, NG])
            penc = sb1("penc", [P, NG])
            relT = sb1("relT", [P, NREL])
            with ExitStack() as c1:
                prepare(nc, c1, cst, io, dram, QT, bases, flag, penc, relT[:, :], unfit)
            with ExitStack() as c2:
                edge_pass(nc, c2, cst, QT, dram["kv"], dram["src"], dram["featx"], dram["featt"], dram["agg"],
                          bases, flag, penc, relT[:, :])
            unfit_now = nc.values_load(unfit[0:1, 0:1], min_val=0, max_val=1)
            with nc.If(unfit_now > 0), ExitStack() as c3:
                any_order_pass(nc, c3, cst, io, dram, QT)
        x1 = sb("x1", [P, NT, D])
        with ExitStack() as ctx:
            after_edges(nc, ctx, cst, io, dram, x1, slots, gap, rows, ints)
        with ExitStack() as ctx:
            experts(nc, ctx, cst, io, dram, rows)
        with ExitStack() as ctx:
            combine(nc, ctx, cst, dram, out, x1, slots, gap)


INPUTS = dict(x="x", src="src", dst="dst", etype="edge_type_64", query="L0_gnn_query_emb", Wq="L0_gnn_Wq",
              bq="L0_gnn_bq", Wk="L0_gnn_Wk", bk="L0_gnn_bk", Wv="L0_gnn_Wv", bv="L0_gnn_bv", rel="L0_gnn_rel_w",
              Wo="L0_gnn_Wo", bo="L0_gnn_bo", gamma="L0_gnn_gamma", beta="L0_gnn_beta", Wr="L0_ffn_Wr",
              br="L0_ffn_br", ln_g="L0_ffn_ln_g", ln_b="L0_ffn_ln_b", W1="L0_ffn_W1", b1="L0_ffn_b1",
              W2="L0_ffn_W2", b2="L0_ffn_b2")


def kernel(**inputs):
    import numpy as _np
    import concourse.bacc as _bacc
    from concourse import mybir as _mybir
    from concourse.bass_utils import run_bass_kernel_spmd as _run

    nc = _bacc.Bacc("TRN2", target_bir_lowering=False, num_devices=1)
    arrays = {"in_consts": CONSTS}
    for short, name in INPUTS.items():
        arrays[f"in_{short}"] = _np.ascontiguousarray(inputs[name])
    io = {name[3:]: nc.dram_tensor(name, a.shape, _mybir.dt.from_np(a.dtype), kind="ExternalInput").ap()
          for name, a in arrays.items()}
    out = nc.dram_tensor("out_0", (N, D), F32, kind="ExternalOutput").ap()
    build(nc, io, out)
    r = _run(nc, [arrays], core_ids=[0])
    return r.results[0]["out_0"]
```
